# Optimizing a Trainium2 kernel written in Bass

```python
import numpy as np
import jax
import jax.numpy as jnp

def _softmax(x, axis=-1):
    return jax.nn.softmax(x, axis=axis)

def _gelu(x):
    return jax.nn.gelu(x, approximate=True)

def _silu(x):
    return jax.nn.silu(x)

def _sigmoid(x):
    return jax.nn.sigmoid(x)

def _layernorm(x, axis=-1, eps=1e-05):
    m = jnp.mean(x, axis=axis, keepdims=True)
    v = jnp.var(x, axis=axis, keepdims=True)
    return (x - m) / jnp.sqrt(v + eps)

def _scatter_add(tgt, idx, src, axis=0):
    return tgt.at[idx].add(src)

def _segment_sum(src, seg, n):
    return jax.ops.segment_sum(src, seg, n)
kernel_name = 'mk_decoder_preln_d4_seqx_r8_7397d7'

def setup_inputs(seed: int=0):
    np.random.seed(seed)
    _w = jnp.asarray

    def _rec_inputs():
        import jax
        import jax.numpy as jnp
        _rk = jax.random.key(seed)
        x = -0.0002928 + 1 * jax.random.normal(jax.random.fold_in(_rk, 1), (8, 100, 256), jnp.float32)
        _lenS = 100 - jax.random.randint(jax.random.fold_in(_rk, 7), (8,), 0, max(1, 100 // 4) + 1, jnp.int32)
        _lenS2 = 1444 - jax.random.randint(jax.random.fold_in(_rk, 8), (8,), 0, max(1, 1444 // 4) + 1, jnp.int32)
        _ctx_512P = jax.random.normal(jax.random.fold_in(_rk, 11), (8, 16, 64), jnp.float32)
        _ctx_512c = jax.random.dirichlet(jax.random.fold_in(_rk, 511), 0.3 * jnp.ones((16,), jnp.float32), (8, 1444))
        _ctx_512t = jnp.einsum('bsk,bkd->bsd', _ctx_512c, _ctx_512P)
        _ctx_512t = _ctx_512t * jax.lax.rsqrt(jnp.mean(jnp.square(_ctx_512t)) + 1e-12) * 0.953939
        ctx_512 = 0.000227908 + 0.99994 * (_ctx_512t + 0.3 * jax.random.normal(jax.random.fold_in(_rk, 611), (8, 1444, 64), jnp.float32))
        return (x, ctx_512)
    x, ctx_512 = _rec_inputs()

    def _L0_attn_setup():
        import jax, jax.numpy as jnp
        import numpy as np
        D = 256
        H = 16
        HD = D // H
        key = jax.random.key(seed)
        k1, k2, k3 = jax.random.split(key, 3)
        x = jax.random.normal(k1, (2, 256, D), dtype=jnp.float32)
        Wqkv = jax.random.normal(k2, (D, 3 * D), dtype=jnp.float32) * D ** (-0.5)
        Wo = jax.random.normal(k3, (D, D), dtype=jnp.float32) * D ** (-0.5)
        return {'x': x, 'Wqkv': Wqkv, 'Wo': Wo}
    _L0_attn_all = _L0_attn_setup()
    _L0_attn_in = {k: v for k, v in _L0_attn_all.items() if k in ('Wqkv', 'Wo')}
    del _L0_attn_all

    def _L0_xattn_setup():
        import jax, jax.numpy as jnp
        import numpy as np
        B, S, L = (2, 128, 128)
        DIM_Q, H, K, D_C, D_CQ, R = (256, 16, 128, 64, 192, 64)

        def _rope_tables(seq_len, dim, dtype):
            inv_freq = 1.0 / 10000.0 ** (jnp.arange(0, dim, 2, dtype=dtype) / dim)
            t = jnp.arange(seq_len, dtype=dtype)
            freqs = t[:, None] * inv_freq[None, :]
            sin = jnp.repeat(jnp.sin(freqs), 2, axis=-1)
            cos = jnp.repeat(jnp.cos(freqs), 2, axis=-1)
            return (sin, cos)

        def _rotate_half(x):
            h = x.shape[-1] // 2
            return jnp.concatenate([-x[..., h:], x[..., :h]], axis=-1)
        key = jax.random.key(seed)
        ks = jax.random.split(key, 8)
        s_in = 1.0 / np.sqrt(DIM_Q)
        s_k = 1.0 / np.sqrt(K)
        s_cq = 1.0 / np.sqrt(D_CQ)
        s_c = 1.0 / np.sqrt(D_C)
        return {'hidden_q': jax.random.normal(ks[0], (B, S, DIM_Q), jnp.float32), 'kv_c': jax.random.normal(ks[1], (B, L, D_C), jnp.float32), 'Wq': jax.random.normal(ks[2], (H * K, DIM_Q), jnp.float32) * s_in, 'w_kc_q': jax.random.normal(ks[3], (H, K, D_CQ), jnp.float32) * s_k, 'w_kc_kv': jax.random.normal(ks[4], (H, K, D_C), jnp.float32) * s_k, 'W_qr': jax.random.normal(ks[5], (H, D_CQ, R), jnp.float32) * s_cq / np.sqrt(R), 'W_kr': jax.random.normal(ks[6], (H, D_C, R), jnp.float32) * s_c, 'Wo': jax.random.normal(ks[7], (DIM_Q, H * K), jnp.float32) * s_k}
    _L0_xattn_all = _L0_xattn_setup()
    _L0_xattn_in = {k: v for k, v in _L0_xattn_all.items() if k in ('Wq', 'w_kc_q', 'w_kc_kv', 'W_qr', 'W_kr', 'Wo')}
    del _L0_xattn_all

    def _L0_ffn_setup():
        import jax, jax.numpy as jnp
        import numpy as np
        SEQ, BS, H, I, E = (256, 4, 256, 512, 8)
        key = jax.random.key(seed)
        ks = jax.random.split(key, 5)
        s = 0.02
        return {'hidden_states': jax.random.normal(ks[0], (SEQ, BS, H), dtype=jnp.float32), 'router_w': jax.random.normal(ks[1], (H, E), dtype=jnp.float32) * s, 'gate_w': jax.random.normal(ks[2], (E, H, I), dtype=jnp.float32) * s, 'up_w': jax.random.normal(ks[3], (E, H, I), dtype=jnp.float32) * s, 'down_w': jax.random.normal(ks[4], (E, I, H), dtype=jnp.float32) * s}
    _L0_ffn_all = _L0_ffn_setup()
    _L0_ffn_in = {k: v for k, v in _L0_ffn_all.items() if k in ('router_w', 'gate_w', 'up_w', 'down_w')}
    del _L0_ffn_all

    def _L1_attn_setup():
        import jax, jax.numpy as jnp
        import numpy as np
        D_MODEL = 256
        N_HEADS = 16
        N_KV_HEADS = 2
        D_HEAD = D_MODEL // N_HEADS
        N_GROUPS = N_HEADS // N_KV_HEADS
        B, T = (2, 256)
        key = jax.random.key(seed)
        ks = jax.random.split(key, 9)
        s = 0.02
        return {'x': jax.random.normal(ks[0], (B, T, D_MODEL), jnp.float32), 'Wq': jax.random.normal(ks[1], (D_MODEL, N_HEADS * D_HEAD), jnp.float32) * s, 'bq': jnp.zeros((N_HEADS * D_HEAD,), jnp.float32), 'Wk': jax.random.normal(ks[2], (D_MODEL, N_KV_HEADS * D_HEAD), jnp.float32) * s, 'bk': jnp.zeros((N_KV_HEADS * D_HEAD,), jnp.float32), 'Wv': jax.random.normal(ks[3], (D_MODEL, N_KV_HEADS * D_HEAD), jnp.float32) * s, 'bv': jnp.zeros((N_KV_HEADS * D_HEAD,), jnp.float32), 'Wo': jax.random.normal(ks[4], (D_MODEL, D_MODEL), jnp.float32) * s, 'bo': jnp.zeros((D_MODEL,), jnp.float32)}
    _L1_attn_all = _L1_attn_setup()
    _L1_attn_in = {k: v for k, v in _L1_attn_all.items() if k in ('Wq', 'bq', 'Wk', 'bk', 'Wv', 'bv', 'Wo', 'bo')}
    del _L1_attn_all

    def _L1_xattn_setup():
        import jax, jax.numpy as jnp
        import numpy as np
        B, S, L = (2, 128, 128)
        DIM_Q, H, K, D_C, D_CQ, R = (256, 16, 128, 64, 192, 64)

        def _rope_tables(length, dim):
            inv = 1.0 / 10000.0 ** (jnp.arange(0, dim, 2, dtype=jnp.float32) / dim)
            f = jnp.arange(length, dtype=jnp.float32)[:, None] * inv[None, :]
            sin = jnp.repeat(jnp.sin(f), 2, axis=-1)
            cos = jnp.repeat(jnp.cos(f), 2, axis=-1)
            return (sin, cos)

        def _rotate_half(x):
            half = x.shape[-1] // 2
            return jnp.concatenate([-x[..., half:], x[..., :half]], axis=-1)

        def _apply_rope(x, sin, cos):
            return x * cos + _rotate_half(x) * sin
        key = jax.random.key(seed)
        ks = jax.random.split(key, 8)
        return {'hidden_q': jax.random.normal(ks[0], (B, S, DIM_Q), jnp.float32), 'kv_c': jax.random.normal(ks[1], (B, L, D_C), jnp.float32), 'Wq': jax.random.normal(ks[2], (H * K, DIM_Q), jnp.float32) / np.sqrt(DIM_Q).astype(np.float32), 'w_kc_q': jax.random.normal(ks[3], (H, K, D_CQ), jnp.float32) / np.sqrt(K).astype(np.float32), 'w_kc_kv': jax.random.normal(ks[4], (H, K, D_C), jnp.float32) / np.sqrt(K).astype(np.float32), 'W_qr': jax.random.normal(ks[5], (H, D_CQ, R), jnp.float32) / np.float32(np.sqrt(D_CQ) * np.sqrt(R)), 'W_kr': jax.random.normal(ks[6], (H, D_C, R), jnp.float32) / np.sqrt(D_C).astype(np.float32), 'Wo': jax.random.normal(ks[7], (DIM_Q, H * K), jnp.float32) / np.sqrt(H * K).astype(np.float32)}
    _L1_xattn_all = _L1_xattn_setup()
    _L1_xattn_in = {k: v for k, v in _L1_xattn_all.items() if k in ('Wq', 'w_kc_q', 'w_kc_kv', 'W_qr', 'W_kr', 'Wo')}
    del _L1_xattn_all

    def _L1_ffn_setup():
        import jax, jax.numpy as jnp
        import numpy as np
        B, S, D = (2, 256, 256)
        MOE_D = 176
        E = 16
        K = 6
        ALPHA = 0.001

        def _moe_forward(x, gate_w, w_gate, w_up, w_down):
            b, s, d = x.shape
            T = b * s
            h = x.reshape(T, d)
            logits = h @ gate_w.T
            scores = jax.nn.softmax(logits.astype(jnp.float32), axis=-1)
            topk_w, topk_idx = jax.lax.top_k(scores, K)
            cw = jnp.zeros((T, E), jnp.float32)
            cw = cw.at[jnp.arange(T)[:, None], topk_idx].add(topk_w)
            y = jnp.zeros((T, d), x.dtype)
            for e in range(E):
                g = h @ w_gate[e].T
                u = h @ w_up[e].T
                out = jax.nn.silu(g) * u @ w_down[e].T
                y = y + cw[:, e:e + 1].astype(x.dtype) * out
            counts = jnp.sum(jax.nn.one_hot(topk_idx.reshape(b, s * K), E, dtype=jnp.float32), axis=1)
            ce = counts * (E / (s * K))
            scores_bse = scores.reshape(b, s, E)
            aux = jnp.mean(jnp.sum(ce * scores_bse.mean(axis=1), axis=1)) * ALPHA
            return (y.reshape(b, s, d), aux)
        key = jax.random.key(seed)
        ks = jax.random.split(key, 5)
        sd = 1.0 / np.sqrt(D)
        sm = 1.0 / np.sqrt(MOE_D)
        return {'x': jax.random.normal(ks[0], (B, S, D), jnp.float32), 'gate_w': jax.random.normal(ks[1], (E, D), jnp.float32) * sd, 'w_gate': jax.random.normal(ks[2], (E, MOE_D, D), jnp.float32) * sd, 'w_up': jax.random.normal(ks[3], (E, MOE_D, D), jnp.float32) * sd, 'w_down': jax.random.normal(ks[4], (E, D, MOE_D), jnp.float32) * sm}
    _L1_ffn_all = _L1_ffn_setup()
    _L1_ffn_in = {k: v for k, v in _L1_ffn_all.items() if k in ('gate_w', 'w_gate', 'w_up', 'w_down')}
    del _L1_ffn_all

    def _L2_attn_setup():
        import jax, jax.numpy as jnp
        import numpy as np
        HIDDEN = 256
        NUM_HEADS = 16
        HEAD_DIM = HIDDEN // NUM_HEADS
        INIT_RANGE = 0.02

        def _split_heads(x):
            B, S, _ = x.shape
            return x.reshape(B, S, NUM_HEADS, HEAD_DIM).transpose(0, 2, 1, 3)
        key = jax.random.key(seed)
        ks = jax.random.split(key, 5)
        B, S = (2, 256)
        hidden_states = jax.random.normal(ks[0], (B, S, HIDDEN), dtype=jnp.float32)

        def w(k):
            return INIT_RANGE * jax.random.normal(k, (HIDDEN, HIDDEN), dtype=jnp.float32)
        return {'hidden_states': hidden_states, 'wq': w(ks[1]), 'bq': jnp.zeros((HIDDEN,), jnp.float32), 'wk': w(ks[2]), 'bk': jnp.zeros((HIDDEN,), jnp.float32), 'wv': w(ks[3]), 'bv': jnp.zeros((HIDDEN,), jnp.float32), 'wo': w(ks[4]), 'bo': jnp.zeros((HIDDEN,), jnp.float32)}
    _L2_attn_all = _L2_attn_setup()
    _L2_attn_in = {k: v for k, v in _L2_attn_all.items() if k in ('wq', 'bq', 'wk', 'bk', 'wv', 'bv', 'wo', 'bo')}
    del _L2_attn_all

    def _L2_xattn_setup():
        import jax, jax.numpy as jnp
        import numpy as np
        B, S, L = (2, 128, 128)
        DIM_Q, H, K, D_C, D_CQ, R = (256, 16, 128, 64, 192, 64)

        def _rope_tables(length, dim):
            inv = 1.0 / 10000.0 ** (jnp.arange(0, dim, 2, dtype=jnp.float32) / dim)
            f = jnp.arange(length, dtype=jnp.float32)[:, None] * inv[None, :]
            sin = jnp.repeat(jnp.sin(f), 2, axis=-1)
            cos = jnp.repeat(jnp.cos(f), 2, axis=-1)
            return (sin, cos)

        def _rotate_half(x):
            half = x.shape[-1] // 2
            return jnp.concatenate([-x[..., half:], x[..., :half]], axis=-1)

        def _apply_rope(x, sin, cos):
            return x * cos + _rotate_half(x) * sin
        key = jax.random.key(seed)
        ks = jax.random.split(key, 8)
        return {'hidden_q': jax.random.normal(ks[0], (B, S, DIM_Q), jnp.float32), 'kv_c': jax.random.normal(ks[1], (B, L, D_C), jnp.float32), 'Wq': jax.random.normal(ks[2], (H * K, DIM_Q), jnp.float32) / np.sqrt(DIM_Q).astype(np.float32), 'w_kc_q': jax.random.normal(ks[3], (H, K, D_CQ), jnp.float32) / np.sqrt(K).astype(np.float32), 'w_kc_kv': jax.random.normal(ks[4], (H, K, D_C), jnp.float32) / np.sqrt(K).astype(np.float32), 'W_qr': jax.random.normal(ks[5], (H, D_CQ, R), jnp.float32) / np.float32(np.sqrt(D_CQ) * np.sqrt(R)), 'W_kr': jax.random.normal(ks[6], (H, D_C, R), jnp.float32) / np.sqrt(D_C).astype(np.float32), 'Wo': jax.random.normal(ks[7], (DIM_Q, H * K), jnp.float32) / np.sqrt(H * K).astype(np.float32)}
    _L2_xattn_all = _L2_xattn_setup()
    _L2_xattn_in = {k: v for k, v in _L2_xattn_all.items() if k in ('Wq', 'w_kc_q', 'w_kc_kv', 'W_qr', 'W_kr', 'Wo')}
    del _L2_xattn_all

    def _L2_ffn_setup():
        import jax, jax.numpy as jnp
        import numpy as np
        HIDDEN = 256
        INTER = 1024
        SCALE = 64.0

        def fwht(x):
            orig_shape = x.shape
            n = orig_shape[-1]
            x = x.reshape(-1, n)
            h = 1
            while h < n:
                x = x.reshape(-1, n // (2 * h), 2, h)
                a, b = (x[:, :, 0, :], x[:, :, 1, :])
                x = jnp.stack([a + b, a - b], axis=2).reshape(-1, n)
                h *= 2
            return (x / jnp.sqrt(jnp.asarray(n, x.dtype))).reshape(orig_shape)
        key = jax.random.key(seed)
        ks = jax.random.split(key, 8)
        inp = jax.random.normal(ks[0], (4, 256, HIDDEN), dtype=jnp.float32)
        SU_ug = jnp.where(jax.random.bernoulli(ks[1], 0.5, (HIDDEN,)), 1.0, -1.0).astype(jnp.float32)
        SU_dp = jnp.where(jax.random.bernoulli(ks[2], 0.5, (INTER,)), 1.0, -1.0).astype(jnp.float32)
        Wscale_ug = jax.random.uniform(ks[3], (2 * INTER,), jnp.float32, 0.5, 1.5)
        Wscale_dp = jax.random.uniform(ks[4], (HIDDEN,), jnp.float32, 0.5, 1.5)
        W_up = jax.random.normal(ks[5], (INTER, HIDDEN), dtype=jnp.float32) * 0.02
        W_gate = jax.random.normal(ks[6], (INTER, HIDDEN), dtype=jnp.float32) * 0.02
        W_down = jax.random.normal(ks[7], (HIDDEN, INTER), dtype=jnp.float32) * 0.02
        return {'input': inp, 'SU_ug': SU_ug, 'SU_dp': SU_dp, 'Wscale_ug': Wscale_ug, 'Wscale_dp': Wscale_dp, 'W_up': W_up, 'W_gate': W_gate, 'W_down': W_down}
    _L2_ffn_all = _L2_ffn_setup()
    _L2_ffn_in = {k: v for k, v in _L2_ffn_all.items() if k in ('SU_ug', 'SU_dp', 'Wscale_ug', 'Wscale_dp', 'W_up', 'W_gate', 'W_down')}
    del _L2_ffn_all

    def _L3_attn_setup():
        import math
        import jax, jax.numpy as jnp
        import numpy as np
        HID = 256
        H = 16
        HKV = 8
        D = HID // H
        F = D
        SEQ = 256
        BATCH = 2
        THETA = 10000.0

        def _rotate_half(x):
            x1, x2 = (x[..., :x.shape[-1] // 2], x[..., x.shape[-1] // 2:])
            return jnp.concatenate((-x2, x1), axis=-1)

        def _softmax_kernel(x, R):
            n = jnp.sqrt(jnp.sum(x * x, axis=-1, keepdims=True))
            x = x / jnp.maximum(n, 1e-06)
            p = jnp.einsum('...d,ed->...e', x, R)
            feats = jnp.concatenate([jnp.sin(p), jnp.cos(p)], axis=-1)
            return feats / math.sqrt(F)
        key = jax.random.key(seed)
        ks = jax.random.split(key, 10)
        s = lambda k, shape, scale=0.02: jax.random.normal(k, shape, dtype=jnp.float32) * scale
        return {'hidden_states': jax.random.normal(ks[0], (BATCH, SEQ, HID), dtype=jnp.float32), 'Wq': s(ks[1], (HID, HID)), 'bq': s(ks[2], (HID,)), 'Wk': s(ks[3], (HKV * D, HID)), 'bk': s(ks[4], (HKV * D,)), 'Wv': s(ks[5], (HKV * D, HID)), 'bv': s(ks[6], (HKV * D,)), 'Wo': s(ks[7], (HID, HID)), 'bo': s(ks[8], (HID,)), 'rand_matrix': jax.random.normal(ks[9], (F // 2, D), dtype=jnp.float32)}
    _L3_attn_all = _L3_attn_setup()
    _L3_attn_in = {k: v for k, v in _L3_attn_all.items() if k in ('Wq', 'bq', 'Wk', 'bk', 'Wv', 'bv', 'Wo', 'bo', 'rand_matrix')}
    del _L3_attn_all

    def _L3_xattn_setup():
        import jax, jax.numpy as jnp
        import numpy as np
        B, S, H, NH, L = (2, 256, 256, 16, 64)
        HD = H // NH
        key = jax.random.key(seed)
        k1, k2, k3, k4, k5 = jax.random.split(key, 5)
        scale = 0.02
        return {'q': jax.random.normal(k1, (B, S, H), dtype=jnp.float32), 'latent_kv': jax.random.normal(k2, (B, S, L), dtype=jnp.float32), 'Wq': jax.random.normal(k3, (H, H), dtype=jnp.float32) * scale, 'Wkv_expand': jax.random.normal(k4, (2 * H, L), dtype=jnp.float32) * scale, 'Wout': jax.random.normal(k5, (H, H), dtype=jnp.float32) * scale}
    _L3_xattn_all = _L3_xattn_setup()
    _L3_xattn_in = {k: v for k, v in _L3_xattn_all.items() if k in ('Wq', 'Wkv_expand', 'Wout')}
    del _L3_xattn_all

    def _L3_ffn_setup():
        import jax, jax.numpy as jnp
        import numpy as np
        TOP_K = 2
        key = jax.random.key(seed)
        ks = jax.random.split(key, 5)
        B, T, D, E, H = (4, 256, 256, 8, 176)
        s = 1.0 / np.sqrt(D)
        sh = 1.0 / np.sqrt(H)
        return {'x': jax.random.normal(ks[0], (B, T, D), dtype=jnp.float32), 'Wg': jax.random.normal(ks[1], (E, D), dtype=jnp.float32) * s, 'W1': jax.random.normal(ks[2], (E, H, D), dtype=jnp.float32) * s, 'W2': jax.random.normal(ks[3], (E, H, D), dtype=jnp.float32) * s, 'W3': jax.random.normal(ks[4], (E, D, H), dtype=jnp.float32) * sh}
    _L3_ffn_all = _L3_ffn_setup()
    _L3_ffn_in = {k: v for k, v in _L3_ffn_all.items() if k in ('Wg', 'W1', 'W2', 'W3')}
    del _L3_ffn_all
    return {'x': x, 'ctx_512': ctx_512, 'L0_attn_Wqkv': _L0_attn_in['Wqkv'], 'L0_attn_Wo': _L0_attn_in['Wo'], 'L0_xattn_Wq': _L0_xattn_in['Wq'], 'L0_xattn_w_kc_q': _L0_xattn_in['w_kc_q'], 'L0_xattn_w_kc_kv': _L0_xattn_in['w_kc_kv'], 'L0_xattn_W_qr': _L0_xattn_in['W_qr'], 'L0_xattn_W_kr': _L0_xattn_in['W_kr'], 'L0_xattn_Wo': _L0_xattn_in['Wo'], 'L0_ffn_router_w': _L0_ffn_in['router_w'], 'L0_ffn_gate_w': _L0_ffn_in['gate_w'], 'L0_ffn_up_w': _L0_ffn_in['up_w'], 'L0_ffn_down_w': _L0_ffn_in['down_w'], 'L1_attn_Wq': _L1_attn_in['Wq'], 'L1_attn_bq': _L1_attn_in['bq'], 'L1_attn_Wk': _L1_attn_in['Wk'], 'L1_attn_bk': _L1_attn_in['bk'], 'L1_attn_Wv': _L1_attn_in['Wv'], 'L1_attn_bv': _L1_attn_in['bv'], 'L1_attn_Wo': _L1_attn_in['Wo'], 'L1_attn_bo': _L1_attn_in['bo'], 'L1_xattn_Wq': _L1_xattn_in['Wq'], 'L1_xattn_w_kc_q': _L1_xattn_in['w_kc_q'], 'L1_xattn_w_kc_kv': _L1_xattn_in['w_kc_kv'], 'L1_xattn_W_qr': _L1_xattn_in['W_qr'], 'L1_xattn_W_kr': _L1_xattn_in['W_kr'], 'L1_xattn_Wo': _L1_xattn_in['Wo'], 'L1_ffn_gate_w': _L1_ffn_in['gate_w'], 'L1_ffn_w_gate': _L1_ffn_in['w_gate'], 'L1_ffn_w_up': _L1_ffn_in['w_up'], 'L1_ffn_w_down': _L1_ffn_in['w_down'], 'L2_attn_wq': _L2_attn_in['wq'], 'L2_attn_bq': _L2_attn_in['bq'], 'L2_attn_wk': _L2_attn_in['wk'], 'L2_attn_bk': _L2_attn_in['bk'], 'L2_attn_wv': _L2_attn_in['wv'], 'L2_attn_bv': _L2_attn_in['bv'], 'L2_attn_wo': _L2_attn_in['wo'], 'L2_attn_bo': _L2_attn_in['bo'], 'L2_xattn_Wq': _L2_xattn_in['Wq'], 'L2_xattn_w_kc_q': _L2_xattn_in['w_kc_q'], 'L2_xattn_w_kc_kv': _L2_xattn_in['w_kc_kv'], 'L2_xattn_W_qr': _L2_xattn_in['W_qr'], 'L2_xattn_W_kr': _L2_xattn_in['W_kr'], 'L2_xattn_Wo': _L2_xattn_in['Wo'], 'L2_ffn_SU_ug': _L2_ffn_in['SU_ug'], 'L2_ffn_SU_dp': _L2_ffn_in['SU_dp'], 'L2_ffn_Wscale_ug': _L2_ffn_in['Wscale_ug'], 'L2_ffn_Wscale_dp': _L2_ffn_in['Wscale_dp'], 'L2_ffn_W_up': _L2_ffn_in['W_up'], 'L2_ffn_W_gate': _L2_ffn_in['W_gate'], 'L2_ffn_W_down': _L2_ffn_in['W_down'], 'L3_attn_Wq': _L3_attn_in['Wq'], 'L3_attn_bq': _L3_attn_in['bq'], 'L3_attn_Wk': _L3_attn_in['Wk'], 'L3_attn_bk': _L3_attn_in['bk'], 'L3_attn_Wv': _L3_attn_in['Wv'], 'L3_attn_bv': _L3_attn_in['bv'], 'L3_attn_Wo': _L3_attn_in['Wo'], 'L3_attn_bo': _L3_attn_in['bo'], 'L3_attn_rand_matrix': _L3_attn_in['rand_matrix'], 'L3_xattn_Wq': _L3_xattn_in['Wq'], 'L3_xattn_Wkv_expand': _L3_xattn_in['Wkv_expand'], 'L3_xattn_Wout': _L3_xattn_in['Wout'], 'L3_ffn_Wg': _L3_ffn_in['Wg'], 'L3_ffn_W1': _L3_ffn_in['W1'], 'L3_ffn_W2': _L3_ffn_in['W2'], 'L3_ffn_W3': _L3_ffn_in['W3']}

def reference(x, ctx_512, L0_attn_Wqkv, L0_attn_Wo, L0_xattn_Wq, L0_xattn_w_kc_q, L0_xattn_w_kc_kv, L0_xattn_W_qr, L0_xattn_W_kr, L0_xattn_Wo, L0_ffn_router_w, L0_ffn_gate_w, L0_ffn_up_w, L0_ffn_down_w, L1_attn_Wq, L1_attn_bq, L1_attn_Wk, L1_attn_bk, L1_attn_Wv, L1_attn_bv, L1_attn_Wo, L1_attn_bo, L1_xattn_Wq, L1_xattn_w_kc_q, L1_xattn_w_kc_kv, L1_xattn_W_qr, L1_xattn_W_kr, L1_xattn_Wo, L1_ffn_gate_w, L1_ffn_w_gate, L1_ffn_w_up, L1_ffn_w_down, L2_attn_wq, L2_attn_bq, L2_attn_wk, L2_attn_bk, L2_attn_wv, L2_attn_bv, L2_attn_wo, L2_attn_bo, L2_xattn_Wq, L2_xattn_w_kc_q, L2_xattn_w_kc_kv, L2_xattn_W_qr, L2_xattn_W_kr, L2_xattn_Wo, L2_ffn_SU_ug, L2_ffn_SU_dp, L2_ffn_Wscale_ug, L2_ffn_Wscale_dp, L2_ffn_W_up, L2_ffn_W_gate, L2_ffn_W_down, L3_attn_Wq, L3_attn_bq, L3_attn_Wk, L3_attn_bk, L3_attn_Wv, L3_attn_bv, L3_attn_Wo, L3_attn_bo, L3_attn_rand_matrix, L3_xattn_Wq, L3_xattn_Wkv_expand, L3_xattn_Wout, L3_ffn_Wg, L3_ffn_W1, L3_ffn_W2, L3_ffn_W3):
    import jax
    import jax.numpy as jnp

    def _L0_attn_ref(x, Wqkv, Wo):
        import jax, jax.numpy as jnp
        import numpy as np
        D = 256
        H = 16
        HD = D // H
        B, S, _ = x.shape
        qkv = (x @ Wqkv).reshape(B, S, 3, H, HD)
        q = qkv[:, :, 0].transpose(0, 2, 1, 3)
        k = qkv[:, :, 1].transpose(0, 2, 1, 3)
        v = qkv[:, :, 2].transpose(0, 2, 1, 3)
        scores = jnp.einsum('bhqd,bhkd->bhqk', q, k) * HD ** (-0.5)
        causal = jnp.tril(jnp.ones((S, S), dtype=bool))
        scores = jnp.where(causal, scores, jnp.float32(-1000000000.0))
        a = jax.nn.softmax(scores, axis=-1)
        o = jnp.einsum('bhqk,bhkd->bhqd', a, v)
        o = o.transpose(0, 2, 1, 3).reshape(B, S, H * HD)
        return o @ Wo

    def _L0_xattn_ref(hidden_q, kv_c, Wq, w_kc_q, w_kc_kv, W_qr, W_kr, Wo):
        import jax, jax.numpy as jnp
        import numpy as np
        B, S, L = (2, 128, 128)
        DIM_Q, H, K, D_C, D_CQ, R = (256, 16, 128, 64, 192, 64)

        def _rope_tables(seq_len, dim, dtype):
            inv_freq = 1.0 / 10000.0 ** (jnp.arange(0, dim, 2, dtype=dtype) / dim)
            t = jnp.arange(seq_len, dtype=dtype)
            freqs = t[:, None] * inv_freq[None, :]
            sin = jnp.repeat(jnp.sin(freqs), 2, axis=-1)
            cos = jnp.repeat(jnp.cos(freqs), 2, axis=-1)
            return (sin, cos)

        def _rotate_half(x):
            h = x.shape[-1] // 2
            return jnp.concatenate([-x[..., h:], x[..., :h]], axis=-1)
        b, s, _ = hidden_q.shape
        l = kv_c.shape[1]
        q_hk = (hidden_q @ Wq.T).reshape(b, s, H, K)
        q_big = jnp.einsum('bshk,hkq->bshq', q_hk, w_kc_q)
        sin, cos = _rope_tables(l, D_C, kv_c.dtype)
        kv_rope = kv_c * cos[None] + _rotate_half(kv_c) * sin[None]
        q_r = jnp.einsum('bshq,hqr->bhsr', q_big, W_qr)
        k_r = jnp.einsum('bld,hdr->bhlr', kv_rope, W_kr)
        scores = jnp.einsum('bhsr,bhlr->bhsl', q_r, k_r)
        attn = jax.nn.softmax(scores, axis=-1)
        ctx_c = jnp.einsum('bhsl,bld->bhsd', attn, kv_rope)
        ctx_lat = jnp.einsum('bhsd,hkd->bshk', ctx_c, w_kc_kv)
        out = ctx_lat.reshape(b, s, H * K) @ Wo.T
        return out

    def _L0_ffn_ref(hidden_states, router_w, gate_w, up_w, down_w):
        import jax, jax.numpy as jnp
        import numpy as np
        SEQ, BS, H, I, E = (256, 4, 256, 512, 8)
        router_logits = jnp.einsum('sbh,he->sbe', hidden_states, router_w)
        routing_indices = jnp.argmax(router_logits, axis=-1)
        routing_weights = jax.nn.sigmoid(jnp.max(router_logits, axis=-1))
        out = jnp.zeros_like(hidden_states)
        for e in range(E):
            mask = (routing_indices == e)[..., None]
            g = jnp.einsum('sbh,hi->sbi', hidden_states, gate_w[e])
            u = jnp.einsum('sbh,hi->sbi', hidden_states, up_w[e])
            y = jnp.einsum('sbi,ih->sbh', jax.nn.silu(g) * u, down_w[e])
            out = out + jnp.where(mask, y, jnp.zeros((), out.dtype))
        return out

    def _L1_attn_ref(x, Wq, bq, Wk, bk, Wv, bv, Wo, bo):
        import jax, jax.numpy as jnp
        import numpy as np
        D_MODEL = 256
        N_HEADS = 16
        N_KV_HEADS = 2
        D_HEAD = D_MODEL // N_HEADS
        N_GROUPS = N_HEADS // N_KV_HEADS
        B, T = (2, 256)
        Bx, Tx, C = x.shape
        Q = (x @ Wq + bq).reshape(Bx, Tx, N_HEADS, D_HEAD)
        K = (x @ Wk + bk).reshape(Bx, Tx, N_KV_HEADS, D_HEAD)
        V = (x @ Wv + bv).reshape(Bx, Tx, N_KV_HEADS, D_HEAD)
        Qg = Q.reshape(Bx, Tx, N_KV_HEADS, N_GROUPS, D_HEAD)
        scale = jnp.sqrt(jnp.float32(D_HEAD))
        scores = jnp.einsum('bqkgd,bskd->bkgqs', Qg, K) / scale
        causal = jnp.triu(jnp.ones((Tx, Tx), bool), k=1)
        scores = jnp.where(causal, -jnp.inf, scores)
        attn = jax.nn.softmax(scores, axis=-1)
        out = jnp.einsum('bkgqs,bskd->bqkgd', attn, V).reshape(Bx, Tx, C)
        return out @ Wo + bo

    def _L1_xattn_ref(hidden_q, kv_c, Wq, w_kc_q, w_kc_kv, W_qr, W_kr, Wo):
        import jax, jax.numpy as jnp
        import numpy as np
        B, S, L = (2, 128, 128)
        DIM_Q, H, K, D_C, D_CQ, R = (256, 16, 128, 64, 192, 64)

        def _rope_tables(length, dim):
            inv = 1.0 / 10000.0 ** (jnp.arange(0, dim, 2, dtype=jnp.float32) / dim)
            f = jnp.arange(length, dtype=jnp.float32)[:, None] * inv[None, :]
            sin = jnp.repeat(jnp.sin(f), 2, axis=-1)
            cos = jnp.repeat(jnp.cos(f), 2, axis=-1)
            return (sin, cos)

        def _rotate_half(x):
            half = x.shape[-1] // 2
            return jnp.concatenate([-x[..., half:], x[..., :half]], axis=-1)

        def _apply_rope(x, sin, cos):
            return x * cos + _rotate_half(x) * sin
        Bv, Sv, _ = hidden_q.shape
        _, Lv, _ = kv_c.shape
        q_hk = (hidden_q @ Wq.T).reshape(Bv, Sv, H, K)
        q_big = jnp.einsum('bshk,hkq->bshq', q_hk, w_kc_q)
        sin_q, cos_q = _rope_tables(Sv, D_CQ)
        q_big = _apply_rope(q_big, sin_q[None, :, None, :], cos_q[None, :, None, :])
        sin_k, cos_k = _rope_tables(Lv, D_C)
        kv_r = _apply_rope(kv_c, sin_k[None], cos_k[None])
        q_r = jnp.einsum('bshq,hqr->bhsr', q_big, W_qr)
        k_r = jnp.einsum('bld,hdr->bhlr', kv_r, W_kr)
        scores = jnp.einsum('bhsr,bhlr->bhsl', q_r, k_r)
        attn = jax.nn.softmax(scores, axis=-1)
        ctx_c = jnp.einsum('bhsl,bld->bhsd', attn, kv_r)
        ctx_lat = jnp.einsum('bhsd,hkd->bhsk', ctx_c, w_kc_kv)
        ctx = ctx_lat.transpose(0, 2, 1, 3).reshape(Bv, Sv, H * K)
        return ctx @ Wo.T

    def _L1_ffn_ref(x, gate_w, w_gate, w_up, w_down):
        import jax, jax.numpy as jnp
        import numpy as np
        B, S, D = (2, 256, 256)
        MOE_D = 176
        E = 16
        K = 6
        ALPHA = 0.001

        def _moe_forward(x, gate_w, w_gate, w_up, w_down):
            b, s, d = x.shape
            T = b * s
            h = x.reshape(T, d)
            logits = h @ gate_w.T
            scores = jax.nn.softmax(logits.astype(jnp.float32), axis=-1)
            topk_w, topk_idx = jax.lax.top_k(scores, K)
            cw = jnp.zeros((T, E), jnp.float32)
            cw = cw.at[jnp.arange(T)[:, None], topk_idx].add(topk_w)
            y = jnp.zeros((T, d), x.dtype)
            for e in range(E):
                g = h @ w_gate[e].T
                u = h @ w_up[e].T
                out = jax.nn.silu(g) * u @ w_down[e].T
                y = y + cw[:, e:e + 1].astype(x.dtype) * out
            counts = jnp.sum(jax.nn.one_hot(topk_idx.reshape(b, s * K), E, dtype=jnp.float32), axis=1)
            ce = counts * (E / (s * K))
            scores_bse = scores.reshape(b, s, E)
            aux = jnp.mean(jnp.sum(ce * scores_bse.mean(axis=1), axis=1)) * ALPHA
            return (y.reshape(b, s, d), aux)
        y, _aux = _moe_forward(x, gate_w, w_gate, w_up, w_down)
        return y

    def _L2_attn_ref(hidden_states, wq, bq, wk, bk, wv, bv, wo, bo):
        import jax, jax.numpy as jnp
        import numpy as np
        HIDDEN = 256
        NUM_HEADS = 16
        HEAD_DIM = HIDDEN // NUM_HEADS
        INIT_RANGE = 0.02

        def _split_heads(x):
            B, S, _ = x.shape
            return x.reshape(B, S, NUM_HEADS, HEAD_DIM).transpose(0, 2, 1, 3)
        B, S, H = hidden_states.shape
        scale = 1.0 / np.sqrt(HEAD_DIM).astype(np.float32)
        q = _split_heads(hidden_states @ wq.T + bq)
        k = _split_heads(hidden_states @ wk.T + bk)
        v = _split_heads(hidden_states @ wv.T + bv)
        attn = jnp.einsum('bhqd,bhkd->bhqk', q, k) * scale
        causal = jnp.where(jnp.tril(jnp.ones((S, S), dtype=bool)), jnp.float32(0.0), jnp.float32(-jnp.inf))
        attn = attn + causal
        probs = jax.nn.softmax(attn, axis=-1)
        out = jnp.einsum('bhqk,bhkd->bhqd', probs, v)
        out = out.transpose(0, 2, 1, 3).reshape(B, S, H)
        return out @ wo.T + bo

    def _L2_xattn_ref(hidden_q, kv_c, Wq, w_kc_q, w_kc_kv, W_qr, W_kr, Wo):
        import jax, jax.numpy as jnp
        import numpy as np
        B, S, L = (2, 128, 128)
        DIM_Q, H, K, D_C, D_CQ, R = (256, 16, 128, 64, 192, 64)

        def _rope_tables(length, dim):
            inv = 1.0 / 10000.0 ** (jnp.arange(0, dim, 2, dtype=jnp.float32) / dim)
            f = jnp.arange(length, dtype=jnp.float32)[:, None] * inv[None, :]
            sin = jnp.repeat(jnp.sin(f), 2, axis=-1)
            cos = jnp.repeat(jnp.cos(f), 2, axis=-1)
            return (sin, cos)

        def _rotate_half(x):
            half = x.shape[-1] // 2
            return jnp.concatenate([-x[..., half:], x[..., :half]], axis=-1)

        def _apply_rope(x, sin, cos):
            return x * cos + _rotate_half(x) * sin
        Bv, Sv, _ = hidden_q.shape
        _, Lv, _ = kv_c.shape
        q_hk = (hidden_q @ Wq.T).reshape(Bv, Sv, H, K)
        q_big = jnp.einsum('bshk,hkq->bshq', q_hk, w_kc_q)
        sin_q, cos_q = _rope_tables(Sv, D_CQ)
        q_big = _apply_rope(q_big, sin_q[None, :, None, :], cos_q[None, :, None, :])
        sin_k, cos_k = _rope_tables(Lv, D_C)
        kv_r = _apply_rope(kv_c, sin_k[None], cos_k[None])
        q_r = jnp.einsum('bshq,hqr->bhsr', q_big, W_qr)
        k_r = jnp.einsum('bld,hdr->bhlr', kv_r, W_kr)
        scores = jnp.einsum('bhsr,bhlr->bhsl', q_r, k_r)
        attn = jax.nn.softmax(scores, axis=-1)
        ctx_c = jnp.einsum('bhsl,bld->bhsd', attn, kv_r)
        ctx_lat = jnp.einsum('bhsd,hkd->bhsk', ctx_c, w_kc_kv)
        ctx = ctx_lat.transpose(0, 2, 1, 3).reshape(Bv, Sv, H * K)
        return ctx @ Wo.T

    def _L2_ffn_ref(input, SU_ug, SU_dp, Wscale_ug, Wscale_dp, W_up, W_gate, W_down):
        import jax, jax.numpy as jnp
        import numpy as np
        HIDDEN = 256
        INTER = 1024
        SCALE = 64.0

        def fwht(x):
            orig_shape = x.shape
            n = orig_shape[-1]
            x = x.reshape(-1, n)
            h = 1
            while h < n:
                x = x.reshape(-1, n // (2 * h), 2, h)
                a, b = (x[:, :, 0, :], x[:, :, 1, :])
                x = jnp.stack([a + b, a - b], axis=2).reshape(-1, n)
                h *= 2
            return (x / jnp.sqrt(jnp.asarray(n, x.dtype))).reshape(orig_shape)
        n = SU_ug.shape[0]
        x = input.reshape(-1, n)
        x = fwht(x * SU_ug) / SCALE
        x_up = x @ W_up.T * (Wscale_ug[:INTER] * SCALE)
        x_gate = x @ W_gate.T * (Wscale_ug[INTER:] * SCALE)
        x = jax.nn.silu(x_gate) * x_up
        x = fwht(x * SU_dp) / SCALE
        x = x @ W_down.T * (Wscale_dp * SCALE)
        return x.reshape(input.shape)

    def _L3_attn_ref(hidden_states, Wq, bq, Wk, bk, Wv, bv, Wo, bo, rand_matrix):
        import math
        import jax, jax.numpy as jnp
        import numpy as np
        HID = 256
        H = 16
        HKV = 8
        D = HID // H
        F = D
        SEQ = 256
        BATCH = 2
        THETA = 10000.0

        def _rotate_half(x):
            x1, x2 = (x[..., :x.shape[-1] // 2], x[..., x.shape[-1] // 2:])
            return jnp.concatenate((-x2, x1), axis=-1)

        def _softmax_kernel(x, R):
            n = jnp.sqrt(jnp.sum(x * x, axis=-1, keepdims=True))
            x = x / jnp.maximum(n, 1e-06)
            p = jnp.einsum('...d,ed->...e', x, R)
            feats = jnp.concatenate([jnp.sin(p), jnp.cos(p)], axis=-1)
            return feats / math.sqrt(F)
        b, s, _ = hidden_states.shape
        q = (hidden_states @ Wq.T + bq).reshape(b, s, H, D).transpose(0, 2, 1, 3)
        k = (hidden_states @ Wk.T + bk).reshape(b, s, HKV, D).transpose(0, 2, 1, 3)
        v = (hidden_states @ Wv.T + bv).reshape(b, s, HKV, D).transpose(0, 2, 1, 3)
        inv_freq = 1.0 / THETA ** (jnp.arange(0, D, 2, dtype=jnp.float32) / D)
        freqs = jnp.arange(s, dtype=jnp.float32)[:, None] * inv_freq[None, :]
        emb = jnp.concatenate((freqs, freqs), axis=-1)
        cos = jnp.cos(emb)[None, None, :, :]
        sin = jnp.sin(emb)[None, None, :, :]
        q = q * cos + _rotate_half(q) * sin
        k = k * cos + _rotate_half(k) * sin
        rep = H // HKV
        k = jnp.repeat(k, rep, axis=1)
        v = jnp.repeat(v, rep, axis=1)
        qp = _softmax_kernel(q, rand_matrix)
        kp = _softmax_kernel(k, rand_matrix)
        kv = jnp.einsum('bhsf,bhsd->bsfd', kp, v)
        out = jnp.einsum('bhsf,bsfd->bhsd', qp, kv)
        out = out.reshape(b, s, HID)
        return out @ Wo.T + bo

    def _L3_xattn_ref(q, latent_kv, Wq, Wkv_expand, Wout):
        import jax, jax.numpy as jnp
        import numpy as np
        B, S, H, NH, L = (2, 256, 256, 16, 64)
        HD = H // NH
        b, sq, _ = q.shape
        sk = latent_kv.shape[1]
        qp = q @ Wq.T
        kv = latent_kv @ Wkv_expand.T
        k, v = jnp.split(kv, 2, axis=-1)
        qh = qp.reshape(b, sq, NH, HD).transpose(0, 2, 1, 3)
        kh = k.reshape(b, sk, NH, HD).transpose(0, 2, 1, 3)
        vh = v.reshape(b, sk, NH, HD).transpose(0, 2, 1, 3)
        inv_sqrt_d = 1.0 / jnp.sqrt(jnp.float32(HD))
        scores = jnp.einsum('bhqd,bhkd->bhqk', qh, kh) * inv_sqrt_d
        causal = jnp.tril(jnp.ones((sq, sk), dtype=bool))
        scores = jnp.where(causal, scores, jnp.finfo(scores.dtype).min)
        attn = jax.nn.softmax(scores, axis=-1)
        out = jnp.einsum('bhqk,bhkd->bhqd', attn, vh)
        out = out.transpose(0, 2, 1, 3).reshape(b, sq, H)
        return out @ Wout.T

    def _L3_ffn_ref(x, Wg, W1, W2, W3):
        import jax, jax.numpy as jnp
        import numpy as np
        TOP_K = 2
        E = Wg.shape[0]
        scores = jnp.einsum('btd,ed->bte', x, Wg)
        topk_s, topk_i = jax.lax.top_k(scores, TOP_K)
        probs = jax.nn.softmax(topk_s, axis=-1)
        onehot = (topk_i[..., None] == jnp.arange(E)).astype(x.dtype)
        w = jnp.einsum('btk,btke->bte', probs, onehot)
        y = jnp.zeros_like(x)
        for e in range(E):
            h = jax.nn.silu(jnp.einsum('btd,hd->bth', x, W1[e])) * jnp.einsum('btd,hd->bth', x, W2[e])
            y = y + w[..., e:e + 1] * jnp.einsum('bth,dh->btd', h, W3[e])
        return y
    x = x + _L0_attn_ref(_layernorm(x, axis=-1), L0_attn_Wqkv, L0_attn_Wo)
    x = x + _L0_xattn_ref(_layernorm(x, axis=-1), ctx_512, L0_xattn_Wq, L0_xattn_w_kc_q, L0_xattn_w_kc_kv, L0_xattn_W_qr, L0_xattn_W_kr, L0_xattn_Wo)
    x = x + _L0_ffn_ref(_layernorm(x, axis=-1), L0_ffn_router_w, L0_ffn_gate_w, L0_ffn_up_w, L0_ffn_down_w)
    x = x + _L1_attn_ref(_layernorm(x, axis=-1), L1_attn_Wq, L1_attn_bq, L1_attn_Wk, L1_attn_bk, L1_attn_Wv, L1_attn_bv, L1_attn_Wo, L1_attn_bo)
    x = x + _L1_xattn_ref(_layernorm(x, axis=-1), ctx_512, L1_xattn_Wq, L1_xattn_w_kc_q, L1_xattn_w_kc_kv, L1_xattn_W_qr, L1_xattn_W_kr, L1_xattn_Wo)
    x = x + _L1_ffn_ref(_layernorm(x, axis=-1), L1_ffn_gate_w, L1_ffn_w_gate, L1_ffn_w_up, L1_ffn_w_down)
    x = x + _L2_attn_ref(_layernorm(x, axis=-1), L2_attn_wq, L2_attn_bq, L2_attn_wk, L2_attn_bk, L2_attn_wv, L2_attn_bv, L2_attn_wo, L2_attn_bo)
    x = x + _L2_xattn_ref(_layernorm(x, axis=-1), ctx_512, L2_xattn_Wq, L2_xattn_w_kc_q, L2_xattn_w_kc_kv, L2_xattn_W_qr, L2_xattn_W_kr, L2_xattn_Wo)
    x = x + _L2_ffn_ref(_layernorm(x, axis=-1), L2_ffn_SU_ug, L2_ffn_SU_dp, L2_ffn_Wscale_ug, L2_ffn_Wscale_dp, L2_ffn_W_up, L2_ffn_W_gate, L2_ffn_W_down)
    x = x + _L3_attn_ref(_layernorm(x, axis=-1), L3_attn_Wq, L3_attn_bq, L3_attn_Wk, L3_attn_bk, L3_attn_Wv, L3_attn_bv, L3_attn_Wo, L3_attn_bo, L3_attn_rand_matrix)
    x = x + _L3_xattn_ref(_layernorm(x, axis=-1), ctx_512, L3_xattn_Wq, L3_xattn_Wkv_expand, L3_xattn_Wout)
    x = x + _L3_ffn_ref(_layernorm(x, axis=-1), L3_ffn_Wg, L3_ffn_W1, L3_ffn_W2, L3_ffn_W3)
    return x

_drawn_inputs = setup_inputs


def setup_inputs(seed=0):
    import zlib

    import numpy as np

    out = dict(_drawn_inputs(seed))
    spreads = {'L1_attn_bq': (0.0, 0.775),
     'L1_attn_bk': (0.0, 2.0),
     'L1_attn_bv': (0.0, 0.1),
     'L1_attn_bo': (0.0, 0.1),
     'L2_attn_bq': (0.0, 0.8),
     'L2_attn_bk': (0.0, 2.0),
     'L2_attn_bv': (0.0, 0.1),
     'L2_attn_bo': (0.0, 0.1)}
    factors = {'L1_attn_Wq': 8.0,
     'L1_attn_Wk': 8.0,
     'L2_attn_wq': 8.0,
     'L2_attn_wk': 7.927,
     'L2_ffn_Wscale_ug': 3.13,
     'L2_ffn_Wscale_dp': 3.68,
     'L3_attn_bq': 17.03,
     'L3_attn_bk': 16.449,
     'L3_attn_bv': 15.846,
     'L3_xattn_Wq': 64.0,
     'L3_attn_bo': 4.282,
     'L3_xattn_Wkv_expand': 3.222,
     'L3_xattn_Wout': 3.278}
    for name, (base, spread) in spreads.items():
        noise = np.random.default_rng([zlib.crc32(name.encode()), seed]).standard_normal(out[name].shape)
        drawn = base * np.exp(spread * noise) if base else spread * noise
        out[name] = jnp.asarray(drawn.astype(out[name].dtype))
    for name, factor in factors.items():
        out[name] = (out[name] * factor).astype(out[name].dtype)
    return out
```

```python
from contextlib import ExitStack

import concourse.bass as bass
from concourse import mybir

F32 = mybir.dt.float32
F16 = mybir.dt.float16
BF16 = mybir.dt.bfloat16
ALU = mybir.AluOpType
ACT = mybir.ActivationFunctionType
X = mybir.AxisListType.X

B, S, D = 8, 100, 256
T = B * S
P = 128
DC = D // P
NT = 400
H = 16
HD = D // H
HH = H // 2
L, DL = 1444, 64
LT = (L + P - 1) // P
EPS = 1e-5


class Core:

    def sems(self, kind, names):
        if kind not in self.kinds:
            self.kinds[kind] = {nm: self.sem(f"{kind}_{nm}") for nm in names}
        return self.kinds[kind]

    def clear(self, kind):
        with self.nc.Block() as block:
            @block.gpsimd
            def _(pool):
                for s in self.kinds[kind].values():
                    pool.sem_clear(s)


class Steps:

    def __init__(self, eng, sem):
        self.eng, self.sem, self.base, self.n = eng, sem, 0, 0

    def link(self, ins):
        self.n += 1
        ins.then_inc(self.sem, 1)
        self.eng.wait_ge(self.sem, self.base + self.n)

    def inside(self, i, per):
        self.start, self.per = self.base + self.n, per
        self.base, self.n = self.start + i * per, 0

    def after(self, iterations):
        assert self.n == self.per, (self.n, self.per)
        self.base, self.n = self.start + iterations * self.per, 0


def banks_view(k, first, n, rows, cols):
    return k.banks[0:rows, first:first + n, 0:cols]


def setup(k):
    nc = k.nc
    s_load, s_credit = k.sem("setup_loaded"), k.sem("setup_made")
    with nc.Block() as block:
        @block.sync
        def _(sp):
            sp.dma_start(k.x[:, :, :], k.a["x"]).then_inc(s_load, 16)
            sp.dma_start(k.ident[:, :], k.a["ident"]).then_inc(s_load, 16)
            sp.dma_start(k.ident16[:, :], k.a["ident16"]).then_inc(s_load, 16)
            sp.dma_start(k.mask16[:, :], k.a["mask16"]).then_inc(s_load, 16)
            sp.dma_start(k.head_rows[:, :], k.a["head_rows"]).then_inc(s_load, 16)
            sp.wait_ge(s_load, 80)

        @block.vector
        def _(dve):
            dve.memset(k.ones64[:, :], 1.0).then_inc(s_credit, 1)
            dve.memset(k.eps[:, :], EPS).then_inc(s_credit, 1)
            dve.memset(k.gates[:, :], 0.0).then_inc(s_credit, 1)
            dve.wait_ge(s_credit, 3)

        @block.tensor
        def _(pe):
            pe.sem_inc(k.ln_transposed, 2)
            pe.wait_ge(k.ln_transposed, 2)

        @block.scalar
        def _(act):
            act.sem_inc(k.ln_copied, 2)
            act.wait_ge(k.ln_copied, 2)


def layer_norm(k):
    nc = k.nc
    n = k.ln_calls
    k.ln_calls += 1
    sums, norm, tr, cp = B * n, B * n, 2 + B * n, 2 + B * n
    with nc.Block() as block:
        @block.vector
        def _(dve):
            with dve.Fori(0, B) as b:
                dve.bn_stats(k.ln_stats[:, b, :], k.x[:, b, :]).then_inc(k.ln_summed, 1)
            dve.wait_ge(k.ln_summed, sums + B)
            for b in range(B):
                dve.bn_aggr(k.ln_mv[:, b, :], k.ln_stats[:, b, :]).then_inc(k.ln_var, 1)
            dve.wait_ge(k.ln_std, n + 1)
            dve.reciprocal(k.ln_rstd[:, :], k.ln_root[:, :]).then_inc(k.ln_recip, 1)
            dve.wait_ge(k.ln_recip, n + 1)
            with dve.Fori(0, B // 2) as i:
                for j in range(2):
                    b = 2 * i + j
                    dve.wait_ge(k.ln_transposed, tr + b - 1)
                    dve.tensor_scalar(k.ln_xn[:, j, :], k.x[:, b, :], k.ln_mv[:, b, 0:1], k.ln_rstd[:, bass.ds(b, 1)],
                                      ALU.subtract, ALU.mult).then_inc(k.ln_normed, 1)

        @block.scalar
        def _(act):
            act.wait_ge(k.ln_var, B * (n + 1))
            act.activation(k.ln_root[:, :], k.ln_mv[:, :, 1], ACT.Sqrt, bias=k.eps[0:S, :]).then_inc(k.ln_std, 1)
            with act.Fori(0, B // 2) as i:
                for j in range(2):
                    b = 2 * i + j
                    act.wait_ge(k.ln_transposed, tr + b + 1)
                    act.copy(k.xnT[:, :, bass.ds(b * S, S)],
                             k.banks[:, j, 0:DC * S].rearrange("p (c s) -> p c s", c=DC)).then_inc(k.ln_copied, 1)

        @block.tensor
        def _(pe):
            with pe.Fori(0, B // 2) as i:
                for j in range(2):
                    b = 2 * i + j
                    pe.wait_ge(k.ln_normed, norm + b + 1)
                    pe.wait_ge(k.ln_copied, cp + b - 1)
                    for c in range(DC):
                        ins = pe.transpose(k.banks[:, j, c * S:(c + 1) * S], k.ln_xn[:, j, c * P:(c + 1) * P],
                                           k.ident[0:S, 0:S])
                    ins.then_inc(k.ln_transposed, 1)


def self_attention(k, name, src, chunks, rows, scale, bias):
    nc, a = k.nc, k.a
    with ExitStack() as ctx:
        def sb(nm, shape, dt=F32):
            return ctx.enter_context(nc.sbuf_tensor(f"{name}_{nm}", shape, dt))

        wq = sb("wq", [P, DC, D])
        wk = sb("wk", [rows, chunks, D])
        wv = sb("wv", [rows, chunks, D])
        wo = sb("wo", [P, DC, D])
        qT = sb("qT", [P, DC, T])
        kT = sb("kT", [P, DC, T])
        v = sb("v", [S, B, H, HD + 1])
        q_st = sb("q_st", [P, 2, S])
        k_st = sb("k_st", [P, 2, HH, S])
        sc = sb("sc", [S, 2, HH, S])
        pr = sb("pr", [S, 2, HH, S])
        prT = sb("prT", [S, HH, S])
        top = sb("top", [S, 2, HH])
        den = sb("den", [S, HH])
        o = sb("o", [S, HH, HD])
        oT = sb("oT", [P, S])
        if bias:
            bq, bk = sb("bq", [P, DC]), sb("bk", [P, DC])
            bv, bo = sb("bv", [S, D]), sb("bo", [S, D])
        sem = k.sems("attn", (
            "wq", "wk", "wv", "wo", "bias", "ones", "proj", "proj_qk", "proj_v", "staged", "scored", "maxed", "less",
            "exped", "transposed", "copied", "pv", "denom", "normed", "yready", "added"))
        qk_jobs = [(dst, w, s_, c, t, n) for dst, w, s_, c in (("q", wq, k.xnT, DC), ("k", wk, src, chunks))
                   for t in range(DC) for n in range(2)]
        nqk = len(qk_jobs)

        with nc.Block() as block:
            @block.sync
            def _(sp):
                sp.dma_start(wq[:, :, :], a[f"{name}_wq"]).then_inc(sem["wq"], 16)
                sp.dma_start(wk[:, :, :], a[f"{name}_wk"]).then_inc(sem["wk"], 16)
                sp.dma_start(wv[:, :, :], a[f"{name}_wv"]).then_inc(sem["wv"], 16)
                sp.dma_start(wo[:, :, :], a[f"{name}_wo"]).then_inc(sem["wo"], 16)
                if bias:
                    sp.dma_start(bq[:, :], a[f"{name}_bq"]).then_inc(sem["bias"], 16)
                    sp.dma_start(bk[:, :], a[f"{name}_bk"]).then_inc(sem["bias"], 16)
                    for dst, nm in ((bv, "bv"), (bo, "bo")):
                        sp.dma_start(dst[:, :], a[f"{name}_{nm}"].partition_broadcast(S)).then_inc(sem["bias"], 16)

            @block.tensor
            def _(pe):
                pe.wait_ge(sem["wq"], 16)
                for n_job, (_, w, s_, cc, t, n) in enumerate(qk_jobs):
                    if n_job == nqk // 2:
                        pe.wait_ge(sem["wk"], 16)
                    if n_job >= 4:
                        pe.wait_ge(sem["proj_qk"], n_job - 3)
                    for c in range(cc):
                        ins = pe.matmul(k.banks[:, n_job % 4, 0:NT], w[:, c, t * P:(t + 1) * P],
                                        s_[:, c, n * NT:(n + 1) * NT], start=c == 0, stop=c == cc - 1)
                    ins.then_inc(sem["proj"], 1)
                pe.wait_ge(sem["wv"], 16)
                for b in range(B):
                    if b >= 4:
                        pe.wait_ge(sem["proj_v"], b - 3)
                    for c in range(chunks):
                        ins = pe.matmul(k.banks[0:S, 4 + b % 4, 0:D], src[:, c, b * S:(b + 1) * S],
                                        wv[:, c, :], start=c == 0, stop=c == chunks - 1)
                    ins.then_inc(sem["proj"], 1)
                pe.wait_ge(sem["proj_qk"], nqk)
                pe.wait_ge(sem["proj_v"], B)
                pe.wait_ge(sem["wo"], 16)

                def scores(u, half):
                    pe.wait_ge(sem["staged"], u + 1)
                    for g in range(2):
                        bank = k.banks[0:S, 2 * half + g, 0:4 * S]
                        pe.matmul(bank, k.ident16[0:S, 0:S], k.mask16[:, :], start=True, stop=False)
                        ins = pe.matmul(bank, q_st[:, half, :], k_st[:, half, 4 * g:4 * g + 4, :],
                                        start=False, stop=True)
                    ins.then_inc(sem["scored"], 1)

                def project(half):
                    ins = pe.matmul(k.banks[0:S, 7, 0:D], oT[:, :], wo[:, half, :], start=half == 0, stop=half == 1)
                    ins.then_inc(sem["yready"], 1)

                def unit(b, half, following, previous):
                    u = 2 * b + half
                    if following:
                        scores(u + 1, 1 - half)
                    pe.wait_ge(sem["exped"], u + 1)
                    if previous:
                        pe.wait_ge(sem["copied"], 2 * u)
                    for h in range(HH):
                        ins = pe.transpose(k.banks[0:S, 4 + h // 4, (h % 4) * S:(h % 4 + 1) * S], pr[:, half, h, :],
                                           k.ident[0:S, 0:S])
                    if previous:
                        pe.wait_ge(sem["normed"], u)
                        ins = pe.transpose(k.banks[:, 5, 4 * S:5 * S], o[:, :, :].rearrange("s h d -> s (h d)"),
                                           k.ident[0:S, 0:S])
                    ins.then_inc(sem["transposed"], 1)
                    pe.wait_ge(sem["copied"], 2 * u + 2)
                    for h in range(HH):
                        ins = pe.matmul(k.banks[0:S, 6, h * (HD + 1):(h + 1) * (HD + 1)], prT[:, h, :],
                                        v[:, b, HH * half + h, :], start=True, stop=True)
                    ins.then_inc(sem["pv"], 1)
                    if previous:
                        if half == 1:
                            if not isinstance(b, int) or b >= 1:
                                pe.wait_ge(sem["added"], b)
                        project(1 - half)

                scores(0, 0)
                unit(0, 0, True, False)
                unit(0, 1, True, True)
                with pe.Fori(1, B - 1) as b:
                    unit(b, 0, True, True)
                    unit(b, 1, True, True)
                unit(B - 1, 0, True, True)
                unit(B - 1, 1, False, True)
                pe.wait_ge(sem["copied"], 4 * B)
                pe.wait_ge(sem["normed"], 2 * B)
                pe.transpose(k.banks[:, 5, 4 * S:5 * S], o[:, :, :].rearrange("s h d -> s (h d)"),
                             k.ident[0:S, 0:S]).then_inc(sem["transposed"], 1)
                pe.wait_ge(sem["copied"], 4 * B + 1)
                project(1)

            @block.scalar
            def _(act):
                if bias:
                    act.wait_ge(sem["bias"], 64)
                for n_job, (which, _, _, _, t, n) in enumerate(qk_jobs):
                    act.wait_ge(sem["proj"], n_job + 1)
                    dst = (qT if which == "q" else kT)[:, t, n * NT:(n + 1) * NT]
                    if bias:
                        bb = (bq if which == "q" else bk)[:, t:t + 1]
                        act.activation(dst, k.banks[:, n_job % 4, 0:NT], ACT.Identity, bias=bb).then_inc(sem["proj_qk"], 1)
                    else:
                        act.copy(dst, k.banks[:, n_job % 4, 0:NT]).then_inc(sem["proj_qk"], 1)

                def exponentials(u, half):
                    act.wait_ge(sem["less"], u + 1)
                    act.activation(pr[:, half], sc[:, half], ACT.Exp, scale=scale).then_inc(sem["exped"], 1)

                def unit(u, half, following, previous):
                    act.wait_ge(sem["transposed"], u + 1)
                    if previous:
                        act.wait_ge(sem["pv"], u)
                    act.copy(prT[:, :, :].rearrange("s (g h) t -> s g (h t)", g=2),
                             banks_view(k, 4, 2, S, 4 * S)).then_inc(sem["copied"], 1 if previous else 2)
                    if previous:
                        if isinstance(u, int) and u == 1:
                            pass
                        else:
                            act.wait_ge(sem["yready"], u - 1)
                        act.copy(oT[:, :], k.banks[:, 5, 4 * S:5 * S]).then_inc(sem["copied"], 1)
                    if following:
                        exponentials(u + 1, 1 - half)

                exponentials(0, 0)
                unit(0, 0, True, False)
                unit(1, 1, True, True)
                with act.Fori(1, B - 1) as b:
                    unit(2 * b, 0, True, True)
                    unit(2 * b + 1, 1, True, True)
                unit(2 * B - 2, 0, True, True)
                unit(2 * B - 1, 1, False, True)
                act.wait_ge(sem["transposed"], 2 * B + 1)
                act.wait_ge(sem["yready"], 2 * B - 1)
                act.copy(oT[:, :], k.banks[:, 5, 4 * S:5 * S]).then_inc(sem["copied"], 1)

            @block.gpsimd
            def _(pool):
                pool.wait_ge(sem["proj_qk"], nqk)
                def stage(b, half):
                    at = bass.ds(b * S, S)
                    pool.tensor_copy(q_st[:, half, :], qT[:, half, at])
                    pool.tensor_tensor(k_st[:, half], kT[:, half, at].unsqueeze(1).broadcast_to((P, HH, S)),
                                       k.head_rows[:, :].unsqueeze(2).broadcast_to((P, HH, S)), ALU.mult)\
                        .then_inc(sem["staged"], 1)
                stage(0, 0)
                stage(0, 1)
                with pool.Fori(1, B) as b:
                    for half in range(2):
                        pool.wait_ge(sem["scored"], 2 * b + half - 1)
                        stage(b, half)

            @block.vector
            def _(dve):
                dve.memset(v[:, :, :, HD:HD + 1], 1.0).then_inc(sem["ones"], 1)
                if bias:
                    dve.wait_ge(sem["bias"], 64)
                    dve.tensor_tensor(k.x[:, :, :], k.x[:, :, :],
                                      bo[:, :].unsqueeze(1).broadcast_to((S, B, D)), ALU.add).then_inc(sem["ones"], 1)
                for b in range(B):
                    dve.wait_ge(sem["proj"], nqk + b + 1)
                    dst, got = v[:, b, :, 0:HD], k.banks[0:S, 4 + b % 4, 0:D].rearrange("s (h d) -> s h d", h=H)
                    if bias:
                        dve.tensor_tensor(dst, got, bv[:, :].rearrange("s (h d) -> s h d", h=H), ALU.add)\
                           .then_inc(sem["proj_v"], 1)
                    else:
                        dve.tensor_copy(dst, got).then_inc(sem["proj_v"], 1)

                def subtract_max(u, half, first):
                    dve.wait_ge(sem["scored"], u + 1)
                    got = banks_view(k, 2 * half, 2, S, 4 * S).rearrange("s g (h t) -> s g h t", t=S)
                    tp = top[:, half, :].rearrange("s (g h) -> s g h", g=2)
                    dve.tensor_reduce(tp, got, X, ALU.max).then_inc(sem["maxed"], 1)
                    dve.wait_ge(sem["maxed"], u + 1)
                    if not first:
                        dve.wait_ge(sem["exped"], u - 1)
                    for g in range(2):
                        ins = dve.tensor_tensor(sc[:, half, 4 * g:4 * g + 4, :], got[:, g],
                                                tp[:, g].unsqueeze(2).broadcast_to((S, 4, S)), ALU.subtract)
                    ins.then_inc(sem["less"], 1)

                def normalize(u):
                    dve.wait_ge(sem["pv"], u + 1)
                    got = k.banks[0:S, 6, 0:HH * (HD + 1)].rearrange("s (h d) -> s h d", h=HH)
                    dve.reciprocal(den[:, :].unsqueeze(2), got[:, :, HD:HD + 1]).then_inc(sem["denom"], 1)
                    dve.wait_ge(sem["denom"], u + 1)
                    dve.tensor_tensor(o[:, :, :], got[:, :, 0:HD], den[:, :].unsqueeze(2).broadcast_to((S, HH, HD)),
                                      ALU.mult).then_inc(sem["normed"], 1)

                def add(b):
                    dve.wait_ge(sem["yready"], 2 * b + 2)
                    dve.tensor_tensor(k.x[:, b, :], k.x[:, b, :], k.banks[0:S, 7, 0:D], ALU.add)\
                       .then_inc(sem["added"], 1)

                dve.wait_ge(sem["ones"], 2 if bias else 1)
                subtract_max(0, 0, True)
                subtract_max(1, 1, True)
                normalize(0)
                with dve.Fori(1, B) as b:
                    subtract_max(2 * b, 0, False)
                    normalize(2 * b - 1)
                    subtract_max(2 * b + 1, 1, False)
                    add(b - 1)
                    normalize(2 * b)
                normalize(2 * B - 1)
                add(B - 1)
    k.clear("attn")


KV_BANKS = 3
L_LAST = L - (LT - 1) * P


def context(k):
    nc, a = k.nc, k.a
    HL = DL // 2
    with ExitStack() as ctx:
        def sb(nm, shape, dt=F32):
            return ctx.enter_context(nc.sbuf_tensor(f"ctx_{nm}", shape, dt))

        raw = sb("raw", [P, 2, LT, DL])
        cos, sin = sb("cos", [P, LT, DL]), sb("sin", [P, LT, DL])
        c_part, s_part = sb("c_part", [P, LT, DL]), sb("s_part", [P, LT, DL])
        twice = sb("twice", [P, 2, LT, 2, DL])
        loaded = [k.sem("ctx_loaded0"), k.sem("ctx_loaded1")]
        tables, cleared, parts, roped = k.sem("ctx_tables"), k.sem("ctx_cleared"), k.sem("ctx_parts"), k.sem("ctx_roped")
        doubled, kept, turned = k.sem("ctx_doubled"), k.sem("ctx_kept"), k.sem("ctx_turned")
        high, ones, low = k.sem("ctx_high"), k.sem("ctx_ones"), k.sem("ctx_low")

        with nc.Block() as block:
            @block.sync
            def _(sp):
                sp.dma_start(cos[:, :, :], a["ctx_cos"]).then_inc(tables, 16)
                sp.dma_start(sin[:, :, :], a["ctx_sin"]).then_inc(tables, 16)

                def load(b, j):
                    sp.dma_start(raw[:, j, 0:LT - 1, :],
                                 a["ctx"][b, 0:(LT - 1) * P, :].rearrange("(t p) d -> p t d", p=P)).then_inc(loaded[j], 16)
                    sp.dma_start(raw[0:L_LAST, j, LT - 1, :], a["ctx"][b, (LT - 1) * P:L, :]).then_inc(loaded[j], 16)
                sp.wait_ge(cleared, 1)
                load(0, 0)
                load(1, 1)
                with sp.Fori(1, B // 2) as i:
                    for j in range(2):
                        sp.wait_ge(roped, 2 * i + j - 1)
                        load(2 * i + j, j)

            @block.vector
            def _(dve):
                dve.memset(raw[:, :, LT - 1, :], 0.0).then_inc(cleared, 1)
                dve.memset(k.kv_h1[DL:DL + 2, :], 1.0).then_inc(cleared, 1)
                dve.memset(k.kv_h1[0:DL, B * L:], 0.0).then_inc(cleared, 1)
                dve.memset(k.kv_hl[:, B * L:], 0.0).then_inc(cleared, 1)
                dve.wait_ge(tables, 32)

                def batch(i, j, first):
                    b = 2 * i + j
                    dve.wait_ge(loaded[j], 32 * i + 32)
                    dve.tensor_tensor(c_part[:, :, :], raw[:, j], cos[:, :, :], ALU.mult).then_inc(parts, 1)
                    dve.tensor_tensor(s_part[:, :, 0:HL], raw[:, j, :, HL:DL], sin[:, :, 0:HL], ALU.mult).then_inc(parts, 1)
                    dve.tensor_tensor(s_part[:, :, HL:DL], raw[:, j, :, 0:HL], sin[:, :, HL:DL], ALU.mult).then_inc(parts, 1)
                    dve.wait_ge(parts, 3 * b + 3)
                    if not first:
                        dve.wait_ge(turned, b - 1)
                        dve.wait_ge(kept, b - 1)
                    dve.tensor_tensor(twice[:, j, :, 0, :], c_part[:, :, :], s_part[:, :, :], ALU.add).then_inc(roped, 1)
                    dve.wait_ge(high, b + 1)
                    dve.wait_ge(ones, b + 1)
                    at = k.kv_hl[DL:2 * DL, bass.ds(b * L, L)]
                    got = k.banks[DL:2 * DL, KV_BANKS * j:KV_BANKS * (j + 1), :].rearrange("p a c -> p (a c)")[:, 0:L]
                    dve.tensor_tensor(at, got, at, ALU.subtract).then_inc(low, 1)
                batch(0, 0, True)
                batch(0, 1, True)
                with dve.Fori(1, B // 2) as i:
                    batch(i, 0, False)
                    batch(i, 1, False)

            @block.scalar
            def _(act):
                with act.Fori(0, B // 2) as i:
                    for j in range(2):
                        b = 2 * i + j
                        act.wait_ge(roped, b + 1)
                        act.copy(twice[:, j, :, 1, :], twice[:, j, :, 0, :]).then_inc(doubled, 1)
                        act.wait_ge(turned, b + 1)
                        got = k.banks[:, KV_BANKS * j:KV_BANKS * (j + 1), :].rearrange("p a c -> p (a c)")[:, 0:L]
                        act.copy(k.kv_hl[:, bass.ds(b * L, L)], got).then_inc(high, 1)

            @block.gpsimd
            def _(pool):
                with pool.Fori(0, B // 2) as i:
                    for j in range(2):
                        b = 2 * i + j
                        pool.wait_ge(roped, b + 1)
                        pool.tensor_copy(k.kv_tok[:, b], twice[:, j, :, 0, :]).then_inc(kept, 1)
                        pool.wait_ge(high, b + 1)
                        at = bass.ds(b * L, L)
                        pool.tensor_copy(k.kv_h1[0:DL, at], k.kv_hl[0:DL, at]).then_inc(ones, 1)

            @block.tensor
            def _(pe):
                def batch(b, j, first):
                    pe.wait_ge(doubled, b + 1)
                    if not first:
                        pe.wait_ge(low, b - 1)
                    for t in range(LT):
                        m = P if t < LT - 1 else L_LAST
                        bank = k.banks[:, KV_BANKS * j + t // 4, (t % 4) * P:(t % 4) * P + m]
                        ins = pe.transpose(bank, twice[0:m, j, t, :, :].rearrange("p a d -> p (a d)"), k.ident[0:m, 0:m])
                    ins.then_inc(turned, 1)
                batch(0, 0, True)
                batch(1, 1, True)
                with pe.Fori(1, B // 2) as i:
                    batch(2 * i, 0, False)
                    batch(2 * i + 1, 1, False)


HK, CQ, R = 128, 192, 64
CH = CQ // 2
PAIRS = H // 2


def cross_queries(k, name, rope):
    nc, a = k.nc, k.a
    with ExitStack() as ctx:
        def sb(nm, shape, dt=F32):
            return ctx.enter_context(nc.sbuf_tensor(f"{name}_{nm}", shape, dt))

        raw = sb("raw", [P, 2, D + CQ + DL + D])
        rkr = sb("rkr", [R, 2, CQ + 2 * DL])
        w1 = sb("w1", [P, 2, DC, CQ])
        w2 = sb("w2", [CH, 2, 2, P])
        q_rot = sb("q_rot", [CH, 2, 2, NT])
        if rope:
            prod = sb("prod", [CH, 2, 2, 2, NT])
            cos, sin = sb("cos", [CH, 2, S]), sb("sin", [CH, 2, S])
        sem = k.sems("queries", (
            "loaded0", "loaded1", "tables", "merged", "merged_copied", "w1_copied", "big", "taken", "rotated", "absorbed", "high", "low",
            "padded"))
        loaded = [sem["loaded0"], sem["loaded1"]]

        with nc.Block() as block:
            @block.sync
            def _(sp):
                if rope:
                    sp.dma_start(cos[:, :, :], a["q_cos"]).then_inc(sem["tables"], 16)
                    sp.dma_start(sin[:, :, :], a["q_sin"]).then_inc(sem["tables"], 16)

                def load(h, j):
                    sp.dma_start(raw[:, j, :], a[f"{name}_raw"][h]).then_inc(loaded[j], 16)
                    sp.dma_start(rkr[:, j, :], a[f"{name}_rkr"][h]).then_inc(loaded[j], 16)
                load(0, 0)
                load(1, 1)
                with sp.Fori(1, PAIRS) as i:
                    for j in range(2):
                        sp.wait_ge(sem["merged"], 2 * i + j - 1)
                        load(2 * i + j, j)

            @block.tensor
            def _(pe):
                def merge(i, j, first):
                    h = 2 * i + j
                    pe.wait_ge(loaded[j], 32 * i + 32)
                    if not first:
                        pe.wait_ge(sem["merged_copied"], h)
                    for c in range(DC):
                        pe.matmul(k.banks[:, 0, c * CQ:(c + 1) * CQ], raw[:, j, c * P:(c + 1) * P],
                                  raw[:, j, D:D + CQ], start=True, stop=True)
                    for c in range(2):
                        pe.matmul(k.banks[0:CH, 1, c * P:(c + 1) * P], rkr[:, j, c * CH:(c + 1) * CH],
                                  rkr[:, j, CQ:CQ + 2 * DL], start=True, stop=True)
                    pe.matmul(k.banks[DL * j:DL * (j + 1), 2, 0:D], raw[:, j, D + CQ:D + CQ + DL],
                              raw[:, j, D + CQ + DL:], start=True, stop=True).then_inc(sem["merged"], 1)

                def compressed(i, j, n, first):
                    h = 2 * i + j
                    if n == 0:
                        pe.wait_ge(sem["w1_copied"], h + 1)
                    if not first:
                        pe.wait_ge(sem["taken"], 2 * h + n - 1)
                    for half in range(2):
                        for c in range(DC):
                            ins = pe.matmul(k.banks[0:CH, 3 + 2 * n + half, 0:NT], w1[:, j, c, half * CH:(half + 1) * CH],
                                            k.xnT[:, c, n * NT:(n + 1) * NT], start=c == 0, stop=c == DC - 1)
                    ins.then_inc(sem["big"], 1)

                def absorbed(i, j, n, first):
                    t = 2 * (2 * i + j) + n
                    pe.wait_ge(sem["rotated" if rope else "taken"], t + 1)
                    if n == 0:
                        pe.wait_ge(sem["merged_copied"], 2 * i + j + 1)
                    if not first:
                        pe.wait_ge(sem["low"], t)
                    for half in range(2):
                        ins = pe.matmul(k.banks[:, 7, 0:NT], w2[:, j, half, :], q_rot[:, n, half, :],
                                        start=half == 0, stop=half == 1)
                    ins.then_inc(sem["absorbed"], 1)

                def head(i, j, first, last):
                    ni, nj = (i, 1) if j == 0 else (i + 1, 0)
                    if not last:
                        merge(ni, nj, False)
                    for n in range(2):
                        if not last:
                            compressed(ni, nj, n, False)
                        absorbed(i, j, n, first and n == 0)
                merge(0, 0, True)
                compressed(0, 0, 0, True)
                compressed(0, 0, 1, True)
                head(0, 0, True, False)
                head(0, 1, False, False)
                with pe.Fori(1, PAIRS - 1) as i:
                    head(i, 0, False, False)
                    head(i, 1, False, False)
                head(PAIRS - 1, 0, False, False)
                head(PAIRS - 1, 1, False, True)

            @block.scalar
            def _(act):
                def copy_merged(i, j):
                    act.wait_ge(sem["merged"], 2 * i + j + 1)
                    act.copy(w1[:, j, :, :], k.banks[:, 0, 0:DC * CQ].rearrange("p (c q) -> p c q", c=DC))\
                       .then_inc(sem["w1_copied"], 1)
                    act.copy(w2[:, j, :, :], k.banks[0:CH, 1, 0:2 * P].rearrange("p (c q) -> p c q", c=2))
                    act.copy(k.wvo[DL * j:DL * (j + 1), i, :], k.banks[DL * j:DL * (j + 1), 2, 0:D])\
                       .then_inc(sem["merged_copied"], 1)

                def high(i, j, n):
                    t = 2 * (2 * i + j) + n
                    act.wait_ge(sem["absorbed"], t + 1)
                    act.copy(k.q_hh[:, 4 * n:4 * n + 4, bass.ds((2 * i + j) * S, S)],
                             k.banks[:, 7, 0:NT].rearrange("p (b s) -> p b s", b=4)).then_inc(sem["high"], 1)
                copy_merged(0, 0)
                with act.Fori(0, PAIRS - 1) as i:
                    for j in range(2):
                        copy_merged(*((i, 1) if j == 0 else (i + 1, 0)))
                        high(i, j, 0)
                        high(i, j, 1)
                copy_merged(PAIRS - 1, 1)
                for j in range(2):
                    high(PAIRS - 1, j, 0)
                    high(PAIRS - 1, j, 1)

            @block.vector
            def _(dve):
                def take(i, j, n, first):
                    t = 2 * (2 * i + j) + n
                    dve.wait_ge(sem["big"], t + 1)
                    got = k.banks[0:CH, 3 + 2 * n:5 + 2 * n, 0:NT]
                    if not rope:
                        if not first:
                            dve.wait_ge(sem["absorbed"], t - 1)
                        dve.tensor_copy(q_rot[:, n, :, :], got).then_inc(sem["taken"], 1)
                        return
                    if not first:
                        dve.wait_ge(sem["rotated"], t - 1)
                    g4 = got.rearrange("p a (b s) -> p a b s", s=S)
                    for half in range(2):
                        dve.tensor_tensor(prod[:, n, 0, half, :].rearrange("p (b s) -> p b s", s=S), g4[:, half],
                                          cos[:, half, :].unsqueeze(1).broadcast_to((CH, 4, S)), ALU.mult)
                        ins = dve.tensor_tensor(prod[:, n, 1, 1 - half, :].rearrange("p (b s) -> p b s", s=S), g4[:, half],
                                                sin[:, half, :].unsqueeze(1).broadcast_to((CH, 4, S)), ALU.mult)
                    ins.then_inc(sem["taken"], 1)

                def low(i, j, n):
                    t = 2 * (2 * i + j) + n
                    dve.wait_ge(sem["high"], t + 1)
                    at = (slice(0, DL), slice(4 * n, 4 * n + 4), bass.ds((2 * i + j) * S, S))
                    dve.tensor_tensor(k.q_l[at], k.banks[0:DL, 7, 0:NT].rearrange("p (b s) -> p b s", b=4),
                                      k.q_hh[at], ALU.subtract).then_inc(sem["low"], 1)
                dve.memset(k.q_hh[:, :, Q:], 0.0).then_inc(sem["padded"], 1)
                if rope:
                    dve.wait_ge(sem["tables"], 32)
                take(0, 0, 0, True)
                take(0, 0, 1, True)
                for n in range(2):
                    take(0, 1, n, False)
                    low(0, 0, n)
                for n in range(2):
                    take(1, 0, n, False)
                    low(0, 1, n)
                with dve.Fori(1, PAIRS - 1) as i:
                    for j in range(2):
                        for n in range(2):
                            take(*((i, 1) if j == 0 else (i + 1, 0)), n, False)
                            low(i, j, n)
                for n in range(2):
                    take(PAIRS - 1, 1, n, False)
                    low(PAIRS - 1, 0, n)
                low(PAIRS - 1, 1, 0)
                low(PAIRS - 1, 1, 1)

            @block.gpsimd
            def _(pool):
                def rotate(i, j, n, first):
                    t = 2 * (2 * i + j) + n
                    pool.wait_ge(sem["taken"], t + 1)
                    if not first:
                        pool.wait_ge(sem["absorbed"], t - 1)
                    pool.tensor_tensor(q_rot[:, n, :, :], prod[:, n, 0], prod[:, n, 1], ALU.add)\
                        .then_inc(sem["rotated"], 1)
                if rope:
                    for n in range(2):
                        rotate(0, 0, n, True)
                    for n in range(2):
                        rotate(0, 1, n, False)
                    with pool.Fori(1, PAIRS) as i:
                        for j in range(2):
                            for n in range(2):
                                rotate(i, j, n, False)
    k.clear("queries")


MAX_CHUNKS = [(0, 482), (482, 482), (964, 480)]
Q = H * S
QT = (Q + P - 1) // P
TASKS = QT * len(MAX_CHUNKS)
STEPS = 2 * LT
TURN = TASKS // 2 + 3


def cross_attention(k, name):
    nc = k.nc
    with ExitStack() as ctx:
        def sb(nm, shape, dt=F32):
            return ctx.enter_context(nc.sbuf_tensor(f"{name}_{nm}", shape, dt))

        kv = sb("kv", [P, LT, DL])
        pr = sb("pr", [P, 2, 2 * NT])
        pr_last = sb("pr_last", [P, 2 * NT])
        rden = sb("rden", [P, NT])
        att = sb("att", [P, 2, NT])
        top3 = sb("top3", [P, QT, len(MAX_CHUNKS)])
        top = sb("top", [P, QT])
        shift = sb("shift", [QT, 2, P], F16)
        sem = k.sems("cross", (
            "staged", "scored", "exped", "weighted", "recip", "normed", "aux", "aux_used", "topped", "shift_high",
            "shifted", "shift_in", "cleared"))

        def rows(t):
            return P if t < LT - 1 else L_LAST

        def weights_of(s):
            return pr[:, s % 2, :] if s % LT < LT - 1 else pr_last

        def queries(q, b, half, c):
            return q[:, b, half * 2 * NT:(half + 1) * 2 * NT].rearrange("p (i j s) -> p j i s", j=2, s=S)[:, c]

        with nc.Block() as block:
            @block.sync
            def _(sp):
                def place_shift(b, after):
                    sp.wait_ge(sem["shifted"], after)
                    for part in range(2):
                        sp.dma_start(k.q_l[DL + part:DL + part + 1, b, :].rearrange("o (t c) -> o t c", c=P),
                                     shift[:, part, :]).then_inc(sem["shift_in"], 16)
                place_shift(0, 1)
                with sp.Fori(1, B) as b:
                    place_shift(b, b + 1)

            @block.gpsimd
            def _(pool):
                pool.tensor_copy(kv[:, :, :], k.kv_tok[:, 0]).then_inc(sem["staged"], LT)
                with pool.Fori(1, B) as b:
                    for t in range(LT):
                        pool.wait_ge(sem["weighted"], 2 + STEPS * b - LT + t + 1)
                        pool.tensor_copy(kv[:, t, :], k.kv_tok[:, b, t, :]).then_inc(sem["staged"], 1)

            @block.tensor
            def _(pe):
                pe.sem_inc(sem["weighted"], 2)

                def top_task(b, base, n):
                    t, (at, cols) = n // len(MAX_CHUNKS), MAX_CHUNKS[n % len(MAX_CHUNKS)]
                    pe.wait_ge(sem["aux_used"], base + max(n - 1, 0))
                    pe.matmul(k.banks[:, 6 + n % 2, 0:cols], k.q_hh[:, b, t * P:(t + 1) * P],
                              k.kv_hl[:, bass.ds(b * L + at, cols)], start=True, stop=True).then_inc(sem["aux"], 1)

                def turn_tops(after, base):
                    pe.wait_ge(sem["topped"], after)
                    pe.wait_ge(sem["aux_used"], base + TASKS)
                    pe.transpose(k.banks[0:QT, 7, 0:P], top[:, :], k.ident[:, :]).then_inc(sem["aux"], 1)

                def scores(b, s):
                    half, t, slot, m = s // LT, s % LT, s % 2, P
                    pe.wait_ge(sem["exped"], STEPS * b + s + 1)
                    if s == 0:
                        pe.wait_ge(sem["shift_in"], 32 * b + 32)
                    at = bass.ds(b * L + t * P, m)
                    for c in range(2):
                        pe.matmul(k.banks[0:m, 2 * slot + c, 0:NT], k.kv_hl[:, at], queries(k.q_hh, b, half, c),
                                  start=True, stop=False)
                    for c in range(2):
                        ins = pe.matmul(k.banks[0:m, 2 * slot + c, 0:NT], k.kv_h1[:, at], queries(k.q_l, b, half, c),
                                        start=False, stop=True)
                    ins.then_inc(sem["scored"], 1)

                def weigh(b, s):
                    half, t = s // LT, s % LT
                    weights = weights_of(s)
                    pe.wait_ge(sem["exped"], STEPS * b + s + 3)
                    if half == 0:
                        pe.wait_ge(sem["staged"], LT * b + t + 1)
                    if t == 0:
                        pe.wait_ge(sem["normed"], 2 * b + half + 1)
                    for bank, lhs in ((4, kv[:, t, :]), (5, k.ones64[:, :])):
                        for c in range(2):
                            ins = pe.matmul(k.banks[DL * c:DL * (c + 1), bank, 0:NT], lhs,
                                            weights[:, c * NT:(c + 1) * NT], start=t == 0, stop=t == LT - 1)
                    ins.then_inc(sem["weighted"], 1)

                def output(b, base):
                    pe.wait_ge(sem["normed"], 2 * b + 3)
                    pe.wait_ge(sem["aux_used"], base)
                    for n in range(PAIRS):
                        ins = pe.matmul(k.banks[0:S, 6, 0:D], att[:, n // 4, (n % 4) * S:(n % 4 + 1) * S],
                                        k.wvo[:, n, :], start=n == 0, stop=n == PAIRS - 1)
                    ins.then_inc(sem["aux"], 1)

                def batch(b, base, last):
                    for s in range(STEPS):
                        if s + 1 < STEPS:
                            scores(b, s + 1)
                        if not last:
                            for n in range(2 * s, min(2 * s + 2, TASKS)):
                                top_task(b + 1, base, n)
                            if s == TURN:
                                turn_tops(b + 2, base)
                        weigh(b, s)
                    if not last:
                        scores(b + 1, 0)
                    output(b, base + (0 if last else TASKS + 1))

                for n in range(TASKS):
                    top_task(0, 1, n)
                turn_tops(1, 1)
                scores(0, 0)
                with pe.Fori(0, B - 1) as b:
                    batch(b, (TASKS + 2) * (b + 1), False)
                batch(B - 1, (TASKS + 2) * B, True)

            @block.scalar
            def _(act):
                act.sem_inc(sem["exped"], 2)
                act.wait_ge(sem["cleared"], 1)
                with act.Fori(0, B) as b:
                    for s in range(STEPS):
                        slot, m = s % 2, rows(s % LT)
                        act.wait_ge(sem["scored"], STEPS * b + s + 1)
                        act.wait_ge(sem["weighted"], STEPS * b + s + 1)
                        act.activation(weights_of(s)[0:m, :].rearrange("p (c n) -> p c n", c=2),
                                       k.banks[0:m, 2 * slot:2 * slot + 2, 0:NT], ACT.Exp).then_inc(sem["exped"], 1)

            @block.vector
            def _(dve):
                dve.memset(pr_last[:, :], 0.0).then_inc(sem["cleared"], 1)
                dve.sem_inc(sem["aux_used"], 1)
                dve.sem_inc(sem["normed"], 1)

                def top_task(base, n):
                    t, (_, cols) = n // len(MAX_CHUNKS), MAX_CHUNKS[n % len(MAX_CHUNKS)]
                    dve.wait_ge(sem["aux"], base + n)
                    dve.tensor_reduce(top3[:, t, n % len(MAX_CHUNKS):n % len(MAX_CHUNKS) + 1],
                                      k.banks[:, 6 + n % 2, 0:cols], X, ALU.max).then_inc(sem["aux_used"], 1)

                def combine(base):
                    dve.wait_ge(sem["aux_used"], base + TASKS)
                    dve.tensor_reduce(top[:, :], top3[:, :, :], X, ALU.max).then_inc(sem["topped"], 1)

                def make_shift(base, b, first):
                    dve.wait_ge(sem["aux"], base + TASKS)
                    if not first:
                        dve.wait_ge(sem["shift_in"], 32 * b)
                    got = k.banks[0:QT, 7, 0:P]
                    dve.tensor_scalar(shift[:, 0, :], got, -1.0, None, ALU.mult).then_inc(sem["shift_high"], 1)
                    dve.wait_ge(sem["shift_high"], b + 1)
                    dve.scalar_tensor_tensor(shift[:, 1, :], got, -1.0, shift[:, 0, :], ALU.mult, ALU.subtract)\
                       .then_inc(sem["shifted"], 1)
                    dve.wait_ge(sem["shifted"], b + 1)
                    dve.sem_inc(sem["aux_used"], 1)

                def normalize(u, half):
                    dve.wait_ge(sem["weighted"], 2 + LT * (u + 1))
                    dve.reciprocal(rden[:, :], k.banks[:, 5, 0:NT]).then_inc(sem["recip"], 1)
                    dve.wait_ge(sem["recip"], u + 1)
                    dve.tensor_tensor(att[:, half, :], k.banks[:, 4, 0:NT], rden[:, :], ALU.mult).then_inc(sem["normed"], 1)

                def batch(b, base, last):
                    for s in range(STEPS):
                        if s == LT:
                            normalize(2 * b, 0)
                        if not last:
                            for n in range(2 * s, min(2 * s + 2, TASKS)):
                                top_task(base, n)
                                if n == TASKS - 1:
                                    combine(base)
                            if s == TURN:
                                make_shift(base, b + 1, False)
                    normalize(2 * b + 1, 1)
                    dve.wait_ge(sem["aux"], base + (0 if last else TASKS + 1))
                    dve.tensor_tensor(k.x[:, b, :], k.x[:, b, :], k.banks[0:S, 6, 0:D], ALU.add)\
                       .then_inc(sem["aux_used"], 1)

                for n in range(TASKS):
                    top_task(1, n)
                combine(1)
                make_shift(1, 0, True)
                with dve.Fori(0, B - 1) as b:
                    batch(b, (TASKS + 2) * (b + 1), False)
                batch(B - 1, (TASKS + 2) * B, True)
    k.clear("cross")


def router(k, name, experts, kind, top):
    nc, a, E = k.nc, k.a, experts
    with ExitStack() as ctx:
        def sb(nm, shape, dt=F32):
            return ctx.enter_context(nc.sbuf_tensor(f"{name}_{nm}", shape, dt))

        wr = sb("wr", [P, DC, E])
        lower = sb("lower", [S, E, E])
        score, ex = sb("score", [S, B, E]), sb("ex", [S, B, E])
        gt, eq = sb("gt", [S, B, E, E]), sb("eq", [S, B, E, E])
        rank, gate = sb("rank", [S, B, E]), sb("gate", [S, B, E])
        best, total = sb("best", [S, B]), sb("total", [S, B])
        high = sb("high", [S, B, E], F16)
        parts = sb("parts", [S, B, 2 * E])
        s = k.sems("router", ("loaded", "scored", "step", "less", "exped", "split", "turned"))

        def over_last(v):
            return v[:, :].unsqueeze(2).broadcast_to((S, B, E))

        with nc.Block() as block:
            @block.sync
            def _(sp):
                sp.dma_start(wr[:, :, :], a[f"{name}_wr"]).then_inc(s["loaded"], 16)
                sp.dma_start(lower[:, :, :], a[f"lower{E}"]).then_inc(s["loaded"], 16)

            @block.tensor
            def _(pe):
                pe.wait_ge(s["loaded"], 32)
                for b in range(B):
                    for c in range(DC):
                        ins = pe.matmul(k.banks[0:S, 0, b * E:(b + 1) * E], k.xnT[:, c, b * S:(b + 1) * S], wr[:, c, :],
                                        start=c == 0, stop=c == DC - 1)
                ins.then_inc(s["scored"], 1)
                pe.wait_ge(s["split"], 1)
                for b in range(B):
                    ins = pe.transpose(k.banks[0:2 * E, 1 + b // 4, (b % 4) * S:(b % 4 + 1) * S], parts[:, b, :],
                                       k.ident[0:S, 0:S])
                ins.then_inc(s["turned"], 1)

            @block.scalar
            def _(act):
                if kind != "choice":
                    act.wait_ge(s["less"], 1)
                    act.activation(ex[:, :, :], ex[:, :, :], ACT.Exp).then_inc(s["exped"], 1)
                act.wait_ge(s["turned"], 1)
                act.copy(k.gates[0:2 * E, :].rearrange("e (g t) -> e g t", g=2), k.banks[0:2 * E, 1:3, 0:NT])

            @block.vector
            def _(dve):
                steps = Steps(dve, s["step"])

                def choose(v):
                    own, others = v.unsqueeze(3).broadcast_to((S, B, E, E)), v.unsqueeze(2).broadcast_to((S, B, E, E))
                    steps.link(dve.tensor_tensor(gt[:, :, :, :], others, own, ALU.is_gt))
                    steps.link(dve.tensor_tensor(eq[:, :, :, :], others, own, ALU.is_equal))
                    steps.link(dve.tensor_tensor(eq[:, :, :, :], eq[:, :, :, :],
                                                 lower[:, :, :].unsqueeze(1).broadcast_to((S, B, E, E)), ALU.mult))
                    steps.link(dve.tensor_tensor(gt[:, :, :, :], gt[:, :, :, :], eq[:, :, :, :], ALU.add))
                    steps.link(dve.tensor_reduce(rank[:, :, :], gt[:, :, :, :], X, ALU.add))
                    steps.link(dve.tensor_scalar(rank[:, :, :], rank[:, :, :], float(top), None, ALU.is_lt))

                dve.wait_ge(s["loaded"], 32)
                dve.wait_ge(s["scored"], 1)
                steps.link(dve.tensor_copy(score[:, :, :].rearrange("s b e -> s (b e)"), k.banks[0:S, 0, 0:B * E]))
                if kind != "choice":
                    steps.link(dve.tensor_reduce(best[:, :], score[:, :, :], X, ALU.max))
                    dve.tensor_tensor(ex[:, :, :], score[:, :, :], over_last(best), ALU.subtract).then_inc(s["less"], 1)
                    dve.wait_ge(s["exped"], 1)
                if kind == "softmax_first":
                    steps.link(dve.tensor_reduce(total[:, :], ex[:, :, :], X, ALU.add))
                    steps.link(dve.reciprocal(total[:, :], total[:, :]))
                    steps.link(dve.tensor_tensor(score[:, :, :], ex[:, :, :], over_last(total), ALU.mult))
                choose(score[:, :, :])
                if kind == "choice":
                    steps.link(dve.tensor_copy(gate[:, :, :], rank[:, :, :]))
                elif kind == "softmax_first":
                    steps.link(dve.tensor_tensor(gate[:, :, :], score[:, :, :], rank[:, :, :], ALU.mult))
                else:
                    steps.link(dve.tensor_tensor(ex[:, :, :], ex[:, :, :], rank[:, :, :], ALU.mult))
                    steps.link(dve.tensor_reduce(total[:, :], ex[:, :, :], X, ALU.add))
                    steps.link(dve.reciprocal(total[:, :], total[:, :]))
                    steps.link(dve.tensor_tensor(gate[:, :, :], ex[:, :, :], over_last(total), ALU.mult))
                steps.link(dve.tensor_copy(high[:, :, :], gate[:, :, :]))
                dve.tensor_copy(parts[:, :, 0:E], high[:, :, :])
                dve.tensor_tensor(parts[:, :, E:2 * E], gate[:, :, :], high[:, :, :], ALU.subtract).then_inc(s["split"], 1)
    k.clear("router")


def feed_forward(k, name, src, tiles, down, experts=0, scales=None):
    nc, a = k.nc, k.a
    with ExitStack() as ctx:
        def sb(nm, shape, dt=F32):
            return ctx.enter_context(nc.sbuf_tensor(f"{name}_{nm}", shape, dt))

        gu = sb("gu", [P, 2, 2 * D])
        dn = sb("dn", [P, 2, D])
        act_g = sb("act_g", [P, 2, NT])
        prod = sb("prod", [P, 2, NT])
        hid = sb("hid", [P, 2, NT])
        yT = sb("yT", [P, DC, T])
        if experts:
            expert_of = sb("expert_of", [P, tiles * P], F16)
        if scales:
            sc_g, sc_u, sc_d = sb("sc_g", [P, tiles]), sb("sc_u", [P, tiles]), sb("sc_d", [P, DC])
        s = k.sems("ffn", ("gu0", "gu1", "dn0", "dn1", "extra", "gate", "up", "spread", "silu", "prod", "hid", "down",
                           "out", "turned", "added"))
        full = (tiles - 1) // 2

        with nc.Block() as block:
            @block.sync
            def _(sp):
                if experts:
                    sp.dma_start(expert_of[:, :], a[f"{name}_expert_of"]).then_inc(s["extra"], 16)
                if scales:
                    for dst, nm in ((sc_g, "sc_g"), (sc_u, "sc_u"), (sc_d, "sc_d")):
                        sp.dma_start(dst[:, :], a[f"{name}_{nm}"]).then_inc(s["extra"], 16)

                def load(m, j, again):
                    if again:
                        sp.wait_ge(s["up"], 2 * m - 2)
                    sp.dma_start(gu[:, j, :], a[f"{name}_gu"][m]).then_inc(s[f"gu{j}"], 16)
                    if again:
                        sp.wait_ge(s["down"], 2 * m - 2)
                    sp.dma_start(dn[:, j, :], down[m]).then_inc(s[f"dn{j}"], 16)
                load(0, 0, False)
                load(1, 1, False)
                with sp.Fori(1, tiles // 2) as i:
                    load(2 * i, 0, True)
                    load(2 * i + 1, 1, True)
                if tiles % 2:
                    load(tiles - 1, 0, True)

            @block.tensor
            def _(pe):
                if experts:
                    pe.wait_ge(s["extra"], 16)

                def rise(i, j, n, first):
                    t = 2 * (2 * i + j) + n
                    if n == 0:
                        pe.wait_ge(s[f"gu{j}"], 16 * i + 16)
                    if first < 2:
                        pe.wait_ge(s["silu"], t - 1)
                    for c in range(DC):
                        ins = pe.matmul(k.banks[:, 7 if n else 4, 0:NT], gu[:, j, c * P:(c + 1) * P],
                                        src[:, c, n * NT:(n + 1) * NT], start=c == 0, stop=c == DC - 1)
                    ins.then_inc(s["gate"], 1)
                    if first < 1 or n:
                        pe.wait_ge(s["prod"], t)
                    for c in range(DC):
                        ins = pe.matmul(k.banks[:, 5, 0:NT], gu[:, j, D + c * P:D + (c + 1) * P],
                                        src[:, c, n * NT:(n + 1) * NT], start=c == 0, stop=c == DC - 1)
                    ins.then_inc(s["up"], 1)
                    if experts:
                        if first < 1 or n:
                            pe.wait_ge(s["hid"], t)
                        pe.matmul(k.banks[:, 6, 0:NT], expert_of[:, bass.ds((2 * i + j) * P, P)],
                                  k.gates[:, n * NT:(n + 1) * NT], start=True, stop=True)\
                          .then_inc(s["spread"], 1)

                def fall(i, j, n, first, last):
                    t = 2 * (2 * i + j) + n
                    if n == 0:
                        pe.wait_ge(s[f"dn{j}"], 16 * i + 16)
                    pe.wait_ge(s["hid"], t + 1)
                    for c in range(DC):
                        ins = pe.matmul(k.banks[:, 2 * c + n, 0:NT], dn[:, j, c * P:(c + 1) * P], hid[:, n, :],
                                        start=first, stop=last)
                    ins.then_inc(s["down"], 1)

                def tile(i, j, first, last):
                    ni, nj = (i, 1) if j == 0 else (i + 1, 0)
                    rise(i, j, 1, 2 if first else 0)
                    fall(i, j, 0, first, last)
                    if not last:
                        rise(ni, nj, 0, 0)
                    fall(i, j, 1, first, last)
                rise(0, 0, 0, 2)
                tile(0, 0, True, False)
                tile(0, 1, False, False)
                with pe.Fori(1, full) as i:
                    tile(i, 0, False, False)
                    tile(i, 1, False, False)
                if tiles % 2 == 0:
                    tile(full, 0, False, False)
                    tile(full, 1, False, True)
                else:
                    tile(full, 0, False, True)
                pe.wait_ge(s["out"], 4)
                for b in range(B):
                    if b >= 4:
                        pe.wait_ge(s["added"], b - 3)
                    for c in range(DC):
                        ins = pe.transpose(k.banks[0:S, 4 + b % 4, c * P:(c + 1) * P], yT[:, c, b * S:(b + 1) * S],
                                           k.ident[:, :])
                    ins.then_inc(s["turned"], 1)

            @block.scalar
            def _(act):
                if scales:
                    act.wait_ge(s["extra"], 48)

                def unit(m, n, again):
                    t = 2 * m + n
                    act.wait_ge(s["gate"], t + 1)
                    if again:
                        act.wait_ge(s["prod"], t - 1)
                    how = {"scale": sc_g[:, m:m + 1]} if scales else {}
                    act.activation(act_g[:, n, :], k.banks[:, 7 if n else 4, 0:NT], ACT.Silu, **how).then_inc(s["silu"], 1)
                unit(0, 0, False)
                unit(0, 1, False)
                if scales:
                    for m in range(1, tiles):
                        unit(m, 0, True)
                        unit(m, 1, True)
                else:
                    with act.Fori(1, tiles) as m:
                        unit(m, 0, True)
                        unit(m, 1, True)
                act.wait_ge(s["down"], 2 * tiles)
                for c in range(DC):
                    for n in range(2):
                        dst, got = yT[:, c, n * NT:(n + 1) * NT], k.banks[:, 2 * c + n, 0:NT]
                        if scales:
                            act.activation(dst, got, ACT.Copy, scale=sc_d[:, c:c + 1]).then_inc(s["out"], 1)
                        else:
                            act.copy(dst, got).then_inc(s["out"], 1)

            @block.vector
            def _(dve):
                if scales:
                    dve.wait_ge(s["extra"], 48)

                def unit(m, n, again):
                    t = 2 * m + n
                    dve.wait_ge(s["silu"], t + 1)
                    dve.wait_ge(s["up"], t + 1)
                    if again:
                        dve.wait_ge(s["down"], t - 1)
                    if scales:
                        dve.scalar_tensor_tensor(hid[:, n, :], k.banks[:, 5, 0:NT], sc_u[:, bass.ds(m, 1)], act_g[:, n, :],
                                                 ALU.mult, ALU.mult).then_inc(s["prod"], 1)
                        dve.wait_ge(s["prod"], t + 1)
                        dve.sem_inc(s["hid"], 1)
                        return
                    dve.tensor_tensor(prod[:, n, :], act_g[:, n, :], k.banks[:, 5, 0:NT], ALU.mult).then_inc(s["prod"], 1)
                    dve.wait_ge(s["prod"], t + 1)
                    dve.wait_ge(s["spread"], t + 1)
                    dve.tensor_tensor(hid[:, n, :], prod[:, n, :], k.banks[:, 6, 0:NT], ALU.mult).then_inc(s["hid"], 1)
                unit(0, 0, False)
                unit(0, 1, False)
                with dve.Fori(1, tiles) as m:
                    unit(m, 0, True)
                    unit(m, 1, True)
                for b in range(B):
                    dve.wait_ge(s["turned"], b + 1)
                    dve.tensor_tensor(k.x[:, b, :], k.x[:, b, :], k.banks[0:S, 4 + b % 4, 0:D], ALU.add)\
                       .then_inc(s["added"], 1)
    k.clear("ffn")


FFN_TILES = 8


def hadamard_weights(k, name, down):
    nc, a, M = k.nc, k.a, FFN_TILES
    with ExitStack() as ctx:
        wd = ctx.enter_context(nc.sbuf_tensor(f"{name}_wd", [P, M, D], F32))
        z = [ctx.enter_context(nc.sbuf_tensor(f"{name}_z{j}", [P, M, D], F32)) for j in range(2)]
        h128 = ctx.enter_context(nc.sbuf_tensor(f"{name}_h128", [P, P], F32))
        su = ctx.enter_context(nc.sbuf_tensor(f"{name}_su", [P, M], F32))
        s = k.sems("hadamard", ("loaded", "turned", "copied", "step", "stored"))
        with nc.Block() as block:
            @block.sync
            def _(sp):
                sp.dma_start(wd[:, :, :], a[f"{name}_wd"]).then_inc(s["loaded"], 16)
                sp.dma_start(h128[:, :], a["h256"][0:P, 0:P]).then_inc(s["loaded"], 16)
                sp.dma_start(su[:, :], a[f"{name}_su_dp"]).then_inc(s["loaded"], 16)
                sp.wait_ge(s["step"], 6 + M)
                sp.dma_start(down.rearrange("m p d -> p m d"), z[0][:, :, :]).then_inc(s["stored"], 16)
                sp.wait_ge(s["stored"], 16)

            @block.tensor
            def _(pe):
                pe.wait_ge(s["loaded"], 48)
                for m in range(M):
                    pe.matmul(k.banks[:, m, 0:D], h128[:, :], wd[:, m, :], start=True, stop=True).then_inc(s["turned"], 1)

            @block.scalar
            def _(act):
                for m in range(M):
                    act.wait_ge(s["turned"], m + 1)
                    act.copy(z[0][:, m, :], k.banks[:, m, 0:D]).then_inc(s["copied"], 1)

            @block.vector
            def _(dve):
                dve.wait_ge(s["copied"], M)
                steps = Steps(dve, s["step"])
                for level in range(3):
                    src, dst = (t[:, :, :].rearrange("p (a two b) d -> p a two (b d)", two=2, b=1 << level)
                                for t in (z[level % 2], z[(level + 1) % 2]))
                    steps.link(dve.tensor_tensor(dst[:, :, 0], src[:, :, 0], src[:, :, 1], ALU.add))
                    steps.link(dve.tensor_tensor(dst[:, :, 1], src[:, :, 0], src[:, :, 1], ALU.subtract))
                for m in range(M):
                    steps.link(dve.tensor_scalar(z[0][:, m, :], z[1][:, m, :], su[:, m:m + 1], 1.0 / 32, ALU.mult, ALU.mult))
    k.clear("hadamard")


def hadamard_inputs(k, name, xh):
    nc, a = k.nc, k.a
    with ExitStack() as ctx:
        h256 = ctx.enter_context(nc.sbuf_tensor(f"{name}_h256", [P, DC, D], F32))
        su = ctx.enter_context(nc.sbuf_tensor(f"{name}_su_in", [P, DC], F32))
        signed = ctx.enter_context(nc.sbuf_tensor(f"{name}_signed", [P, DC, T], F32))
        s = k.sems("hadamard", ("loaded", "turned", "copied", "step", "stored"))
        with nc.Block() as block:
            @block.sync
            def _(sp):
                sp.dma_start(h256[:, :, :], a["h256"].rearrange("(c p) n -> p c n", p=P)).then_inc(s["loaded"], 16)
                sp.dma_start(su[:, :], a[f"{name}_su_ug"]).then_inc(s["loaded"], 16)

            @block.vector
            def _(dve):
                dve.wait_ge(s["loaded"], 32)
                for c in range(DC):
                    dve.tensor_scalar(signed[:, c, :], k.xnT[:, c, :], su[:, c:c + 1], None, ALU.mult).then_inc(s["step"], 1)

            @block.tensor
            def _(pe):
                pe.wait_ge(s["step"], DC)
                for c in range(DC):
                    for n in range(2):
                        for d in range(DC):
                            ins = pe.matmul(k.banks[:, 2 * c + n, 0:NT], h256[:, d, c * P:(c + 1) * P],
                                            signed[:, d, n * NT:(n + 1) * NT], start=d == 0, stop=d == DC - 1)
                        ins.then_inc(s["turned"], 1)

            @block.scalar
            def _(act):
                for c in range(DC):
                    for n in range(2):
                        act.wait_ge(s["turned"], 2 * c + n + 1)
                        act.activation(xh[:, c, n * NT:(n + 1) * NT], k.banks[:, 2 * c + n, 0:NT], ACT.Copy, scale=1.0 / 16)
    k.clear("hadamard")


FE = 8
HKV = H // 2
QK = H + HKV
MAGIC = 1.5 * 2.0 ** 23
INV_2PI = 0.15915494309189535


def feature_attention(k, name):
    nc, a = k.nc, k.a
    scratch = nc.dram_tensor(f"{name}_scratch", (B, S * D), F32).ap()
    with ExitStack() as ctx:
        def sb(nm, shape, dt=F32):
            return ctx.enter_context(nc.sbuf_tensor(f"{name}_{nm}", shape, dt))

        W = (QK + HKV) * HD
        half = HD // 2
        w = sb("w", [P, DC, W])
        bias = sb("bias", [S, W])
        wo, bo = sb("wo", [P, DC, D]), sb("bo", [S, D])
        rb = sb("rb", [P, HKV * FE])
        cos, sin = sb("cos", [S, HD]), sb("sin", [S, HD])
        qk = sb("qk", [S, B, QK, HD])
        v = sb("v", [S, B, HKV * HD])
        c_part, s_part = sb("c_part", [S, QK, HD]), sb("s_part", [S, QK, HD])
        norm = sb("norm", [S, B, QK])
        qkT = sb("qkT", [P, 2, 3, S])
        ph = sb("ph", [S, B, QK, 2 * FE])
        rnd = sb("rnd", [S, B, QK, 2 * FE])
        m1, m2 = sb("m1", [S, 2, H * HKV, 2 * FE]), sb("m2", [S, H * HD, HKV])
        dots = sb("dots", [S, 2, H, HKV])
        o = sb("o", [S, 2, H, HD])
        otok = sb("otok", [S, B, D])
        oT = sb("oT", [P, 2, DC, S])
        s = k.sems("feature", ("loaded", "proj", "biased", "step", "normed", "root", "unit", "turned", "copied", "angled",
                               "angles", "taken", "wrapped", "feat", "prod", "dot", "dotted", "summed", "stored0", "stored1", "back",
                               "oturned", "ocopied", "out", "added"))
        with nc.Block() as block:
            @block.sync
            def _(sp):
                for dst, nm in ((w, "w"), (wo, "wo")):
                    sp.dma_start(dst[:, :, :], a[f"{name}_{nm}"]).then_inc(s["loaded"], 16)
                for dst, nm in ((rb, "rb"), (cos, "cos"), (sin, "sin")):
                    sp.dma_start(dst[:, :], a[f"{name}_{nm}"]).then_inc(s["loaded"], 16)
                for dst, nm in ((bias, "bias"), (bo, "bo")):
                    sp.dma_start(dst[:, :], a[f"{name}_{nm}"].partition_broadcast(S)).then_inc(s["loaded"], 16)
                for b in range(B):
                    sp.wait_ge(s["summed"], b + 1)
                    sp.dma_start(scratch[b].rearrange("(h s d) -> s h d", h=H, s=S), o[:, b % 2])\
                      .then_inc(s[f"stored{b % 2}"], 16)
                for j in range(2):
                    sp.wait_ge(s[f"stored{j}"], 16 * B // 2)
                sp.dma_start(otok[:, :, :], scratch.rearrange("b (r c) -> r b c", c=D)).then_inc(s["back"], 16)

            @block.tensor
            def _(pe):
                pe.wait_ge(s["loaded"], 16 * 7)
                for b in range(B):
                    if b >= 4:
                        pe.wait_ge(s["biased"], b - 3)
                    for c in range(DC):
                        ins = pe.matmul(k.banks[0:S, b % 4, 0:W], k.xnT[:, c, b * S:(b + 1) * S], w[:, c, :],
                                        start=c == 0, stop=c == DC - 1)
                    ins.then_inc(s["proj"], 1)
                for b in range(B):
                    pe.wait_ge(s["unit"], b + 1)
                    if b >= 2:
                        pe.wait_ge(s["copied"], b - 1)
                    for g in range(3):
                        ins = pe.transpose(k.banks[:, 4 + b % 2, g * S:(g + 1) * S],
                                           qk[:, b, 8 * g:8 * g + 8, :].rearrange("s h d -> s (h d)"), k.ident[0:S, 0:S])
                    ins.then_inc(s["turned"], 1)
                    pe.wait_ge(s["copied"], b + 1)
                    if b >= 2:
                        pe.wait_ge(s["taken"], b - 1)
                    for g in range(3):
                        ins = pe.matmul(k.banks[0:S, 6 + b % 2, g * 64:(g + 1) * 64], qkT[:, b % 2, g, :], rb[:, :],
                                        start=True, stop=True)
                    ins.then_inc(s["angled"], 1)
                pe.wait_ge(s["back"], 16)
                for b in range(B):
                    if b >= 2:
                        pe.wait_ge(s["ocopied"], b - 1)
                    for c in range(DC):
                        ins = pe.transpose(k.banks[:, b % 2, c * S:(c + 1) * S], otok[:, b, c * P:(c + 1) * P],
                                           k.ident[0:S, 0:S])
                    ins.then_inc(s["oturned"], 1)
                    pe.wait_ge(s["ocopied"], b + 1)
                    if b >= 2:
                        pe.wait_ge(s["added"], b - 1)
                    for c in range(DC):
                        ins = pe.matmul(k.banks[0:S, 2 + b % 2, 0:D], oT[:, b % 2, c, :], wo[:, c, :],
                                        start=c == 0, stop=c == DC - 1)
                    ins.then_inc(s["out"], 1)

            @block.scalar
            def _(act):
                act.wait_ge(s["normed"], 1)
                act.activation(norm[:, :, :], norm[:, :, :], ACT.Sqrt).then_inc(s["root"], 1)
                for b in range(B):
                    act.wait_ge(s["turned"], b + 1)
                    if b >= 2:
                        act.wait_ge(s["angled"], b - 1)
                    act.copy(qkT[:, b % 2], k.banks[:, 4 + b % 2, 0:3 * S].rearrange("p (g s) -> p g s", g=3))\
                       .then_inc(s["copied"], 1)
                act.wait_ge(s["wrapped"], 1)
                act.activation(ph[:, :, :, :], ph[:, :, :, :], ACT.Sin, scale=6.283185).then_inc(s["feat"], 1)
                for b in range(B):
                    act.wait_ge(s["oturned"], b + 1)
                    if b >= 2:
                        act.wait_ge(s["out"], b - 1)
                    act.copy(oT[:, b % 2], k.banks[:, b % 2, 0:DC * S].rearrange("p (g s) -> p g s", g=DC))\
                       .then_inc(s["ocopied"], 1)

            @block.gpsimd
            def _(pool):
                pool.wait_ge(s["feat"], 1)
                for b in range(B):
                    if b >= 2:
                        pool.wait_ge(s["dot"], b - 1)
                    pool.tensor_tensor(m1[:, b % 2].rearrange("s (h g) f -> s h g f", h=H),
                                       ph[:, b, 0:H, :].unsqueeze(2).broadcast_to((S, H, HKV, 2 * FE)),
                                       ph[:, b, H:QK, :].unsqueeze(1).broadcast_to((S, H, HKV, 2 * FE)), ALU.mult)\
                        .then_inc(s["prod"], 1)

            @block.vector
            def _(dve):
                steps = Steps(dve, s["step"])
                dve.wait_ge(s["loaded"], 16 * 7)
                steps.link(dve.tensor_tensor(k.x[:, :, :], k.x[:, :, :], bo[:, :].unsqueeze(1).broadcast_to((S, B, D)), ALU.add))
                for b in range(B):
                    dve.wait_ge(s["proj"], b + 1)
                    dve.tensor_tensor(qk[:, b, :, :].rearrange("s h d -> s (h d)"), k.banks[0:S, b % 4, 0:QK * HD],
                                      bias[:, 0:QK * HD], ALU.add)
                    dve.tensor_tensor(v[:, b, :], k.banks[0:S, b % 4, QK * HD:W], bias[:, QK * HD:W], ALU.add)\
                       .then_inc(s["biased"], 1)
                    dve.wait_ge(s["biased"], b + 1)
                    def wide(t, at):
                        return t[:, at].unsqueeze(1).broadcast_to((S, QK, at.stop - at.start))
                    dve.tensor_tensor(c_part[:, :, :], qk[:, b], wide(cos, slice(0, HD)), ALU.mult)
                    dve.tensor_tensor(s_part[:, :, 0:half], qk[:, b, :, half:], wide(sin, slice(0, half)), ALU.mult)
                    steps.link(dve.tensor_tensor(s_part[:, :, half:], qk[:, b, :, 0:half], wide(sin, slice(half, HD)), ALU.mult))
                    steps.link(dve.tensor_tensor(qk[:, b], c_part[:, :, :], s_part[:, :, :], ALU.add))
                    steps.link(dve.tensor_tensor(c_part[:, :, :], qk[:, b], qk[:, b], ALU.mult))
                    steps.link(dve.tensor_reduce(norm[:, b, :], c_part[:, :, :], X, ALU.add))
                dve.sem_inc(s["normed"], 1)
                steps.link(dve.tensor_scalar(v[:, :, :], v[:, :, :], 1.0 / 8, None, ALU.mult))
                dve.wait_ge(s["root"], 1)
                steps.link(dve.tensor_scalar(norm[:, :, :], norm[:, :, :], 1e-6, None, ALU.max))
                steps.link(dve.reciprocal(norm[:, :, :], norm[:, :, :]))
                for b in range(B):
                    dve.tensor_tensor(qk[:, b], qk[:, b], norm[:, b, :].unsqueeze(2).broadcast_to((S, QK, HD)), ALU.mult)\
                       .then_inc(s["unit"], 1)
                for b in range(B):
                    dve.wait_ge(s["angled"], b + 1)
                    got = k.banks[0:S, 6 + b % 2, 0:QK * FE].rearrange("s (h e) -> s h e", e=FE)
                    dve.tensor_scalar(ph[:, b, :, 0:FE], got, INV_2PI, None, ALU.mult)
                    dve.tensor_scalar(ph[:, b, :, FE:], got, INV_2PI, 0.25, ALU.mult, ALU.add).then_inc(s["taken"], 1)
                dve.wait_ge(s["taken"], B)
                steps.link(dve.tensor_scalar(rnd[:, :, :, :], ph[:, :, :, :], MAGIC, None, ALU.add))
                steps.link(dve.tensor_scalar(rnd[:, :, :, :], rnd[:, :, :, :], MAGIC, None, ALU.subtract))
                dve.tensor_tensor(ph[:, :, :, :], ph[:, :, :, :], rnd[:, :, :, :], ALU.subtract).then_inc(s["wrapped"], 1)
                for b in range(B):
                    dve.wait_ge(s["prod"], b + 1)
                    dve.tensor_reduce(dots[:, b % 2].rearrange("s h g -> s (h g)"), m1[:, b % 2], X, ALU.add)\
                       .then_inc(s["dot"], 1)
                    dve.wait_ge(s["dot"], b + 1)
                    steps.link(dve.tensor_tensor(
                        m2[:, :, :].rearrange("s (h d) g -> s h d g", h=H),
                        dots[:, b % 2].unsqueeze(2).broadcast_to((S, H, HD, HKV)),
                        v[:, b, :].rearrange("s (g d) -> s d g", g=HKV).unsqueeze(1).broadcast_to((S, H, HD, HKV)),
                        ALU.mult))
                    if b >= 2:
                        dve.wait_ge(s[f"stored{b % 2}"], 16 * (b // 2))
                    dve.tensor_reduce(o[:, b % 2].rearrange("s h d -> s (h d)"), m2[:, :, :], X, ALU.add)\
                       .then_inc(s["summed"], 1)
                    dve.wait_ge(s["summed"], b + 1)
                for b in range(B):
                    dve.wait_ge(s["out"], b + 1)
                    dve.tensor_tensor(k.x[:, b, :], k.x[:, b, :], k.banks[0:S, 2 + b % 2, 0:D], ALU.add)\
                       .then_inc(s["added"], 1)
    k.clear("feature")


def first_context(k, first):
    nc = k.nc
    with ExitStack() as ctx:
        rows = ctx.enter_context(nc.sbuf_tensor("first_rows", [S, B, DL], F32))
        s = k.sems("hadamard", ("loaded", "turned", "copied", "step", "stored"))
        with nc.Block() as block:
            @block.sync
            def _(sp):
                sp.dma_start(rows[:, :, :], k.a["ctx"][:, 0:S, :].rearrange("b s d -> s b d")).then_inc(s["loaded"], 16)

            @block.tensor
            def _(pe):
                pe.wait_ge(s["loaded"], 16)
                for b in range(B):
                    pe.transpose(k.banks[0:DL, b // 4, (b % 4) * S:(b % 4 + 1) * S], rows[:, b, :], k.ident[0:S, 0:S])\
                      .then_inc(s["turned"], 1)

            @block.scalar
            def _(act):
                act.wait_ge(s["turned"], B)
                act.copy(first[:, 0, :].rearrange("d (g t) -> d g t", g=2), k.banks[0:DL, 0:2, 0:NT])
    k.clear("hadamard")


def program(nc, args, out, first, stages):
    k = Core()
    k.nc, k.a, k.kinds = nc, args, {}
    with ExitStack() as ctx:
        def sb(nm, shape, dt=F32):
            return ctx.enter_context(nc.sbuf_tensor(nm, shape, dt))

        k.sem = lambda nm: ctx.enter_context(nc.semaphore(nm))
        k.x = sb("x", [S, B, D])
        k.xnT = sb("xnT", [P, DC, T])
        k.ident = sb("ident", [P, P])
        k.ident16 = sb("ident16", [P, P], BF16)
        k.mask16 = sb("mask16", [S, 4 * S], BF16)
        k.ones64 = sb("ones64", [P, 64])
        k.eps = sb("eps", [P, 1])
        k.ln_stats = sb("ln_stats", [S, B, 6])
        k.ln_mv = sb("ln_mv", [S, B, 2])
        k.ln_root = sb("ln_root", [S, B])
        k.ln_rstd = sb("ln_rstd", [S, B])
        k.ln_xn = sb("ln_xn", [S, 2, D])
        k.kv_hl = sb("kv_hl", [2 * DL, B * L + P - L_LAST], F16)
        k.kv_h1 = sb("kv_h1", [DL + 2, B * L + P - L_LAST], F16)
        k.kv_tok = sb("kv_tok", [P, B, LT, DL])
        k.gates = sb("gates", [P, T], F16)
        k.banks = ctx.enter_context(nc.psum_tensor("banks", [P, 8, 512], F32))
        k.head_rows = sb("head_rows", [P, HH])
        k.ln_summed, k.ln_var, k.ln_std = k.sem("ln_summed"), k.sem("ln_var"), k.sem("ln_std")
        k.ln_recip, k.ln_normed = k.sem("ln_recip"), k.sem("ln_normed")
        k.ln_transposed, k.ln_copied = k.sem("ln_transposed"), k.sem("ln_copied")
        k.ln_calls = 0
        stored = k.sem("stored")
        setup(k)
        context(k)

        def cross(name, rope):
            with ExitStack() as inner:
                k.q_hh = inner.enter_context(nc.sbuf_tensor(f"{name}_q_hh", [2 * DL, B, QT * P], F16))
                k.q_l = inner.enter_context(nc.sbuf_tensor(f"{name}_q_l", [DL + 2, B, QT * P], F16))
                k.wvo = inner.enter_context(nc.sbuf_tensor(f"{name}_wvo", [P, PAIRS, D], F32))
                cross_queries(k, name, rope)
                cross_attention(k, name)

        def mixture(name, experts, hidden, kind, top):
            router(k, name, experts, kind, top)
            feed_forward(k, name, k.xnT, experts * hidden // P, args[f"{name}_dn"], experts)

        def hadamard(name):
            down = nc.dram_tensor(f"{name}_down", (FFN_TILES, P, D), F32).ap()
            hadamard_weights(k, name, down)
            with nc.sbuf_tensor(f"{name}_xh", [P, DC, T], F32) as xh:
                hadamard_inputs(k, name, xh)
                feed_forward(k, name, xh, FFN_TILES, down, scales=True)

        def last_cross(name):
            with nc.sbuf_tensor("first", [DL, 1, T], F32) as first:
                first_context(k, first)
                self_attention(k, name, first, 1, DL, 0.25, False)

        sublayers = [
            lambda: self_attention(k, "L0_attn", k.xnT, DC, P, 0.25, False),
            lambda: cross("L0_xattn", False),
            lambda: mixture("L0_ffn", 8, 512, "choice", 1),
            lambda: self_attention(k, "L1_attn", k.xnT, DC, P, 0.25, True),
            lambda: cross("L1_xattn", True),
            lambda: mixture("L1_ffn", 16, 176, "softmax_first", 6),
            lambda: self_attention(k, "L2_attn", k.xnT, DC, P, 0.25, True),
            lambda: cross("L2_xattn", True),
            lambda: hadamard("L2_ffn"),
            lambda: feature_attention(k, "L3_attn"),
            lambda: last_cross("L3_xattn"),
            lambda: mixture("L3_ffn", 8, 176, "softmax_last", 2),
        ]
        for sublayer in sublayers[first:stages]:
            layer_norm(k)
            sublayer()
        with nc.Block() as block:
            @block.sync
            def _(sp):
                sp.dma_start(out, k.x[:, :, :]).then_inc(stored, 16)
                sp.wait_ge(stored, 16)


def attn_layout(put, name, wq, wk, wv, wo, bq=None, bk=None, bv=None, bo=None):
    import numpy as np

    def tiles(w):
        rows = min(P, w.shape[0])
        return np.ascontiguousarray(w.reshape(-1, rows, w.shape[1]).transpose(1, 0, 2))
    for nm, w in (("wq", wq), ("wk", wk), ("wv", wv), ("wo", wo)):
        put(f"{name}_{nm}", tiles(w))
    if bq is not None:
        put(f"{name}_bq", np.ascontiguousarray(bq.reshape(DC, P).T))
        put(f"{name}_bk", np.ascontiguousarray(bk.reshape(DC, P).T))
        put(f"{name}_bv", bv)
        put(f"{name}_bo", bo)


def rope_tables(length, dim):
    import numpy as np
    inv = np.float32(1.0) / np.power(np.float32(10000.0), np.arange(0, dim, 2, dtype=np.float32) / np.float32(dim))
    f = np.arange(length, dtype=np.float32)[:, None] * inv[None, :]
    return np.repeat(np.cos(f), 2, axis=1), np.repeat(np.sin(f), 2, axis=1)


FIRST, STAGES = 0, 12


def kernel(**inputs):
    import ml_dtypes
    import numpy as np
    import concourse.bacc as bacc
    from concourse.bass_utils import run_bass_kernel_spmd

    i = {name: np.asarray(value) for name, value in inputs.items()}
    nc = bacc.Bacc("TRN2", target_bir_lowering=False, num_devices=1)
    arrays, args = {}, {}

    def put(name, value):
        value = np.ascontiguousarray(value)
        arrays[f"in_{name}"] = value
        args[name] = nc.dram_tensor(f"in_{name}", value.shape, mybir.dt.from_np(value.dtype), kind="ExternalInput").ap()

    bf16 = ml_dtypes.bfloat16
    put("ident", np.eye(P, dtype=np.float32))
    put("ident16", np.eye(P, dtype=bf16))
    put("mask16", np.tile(np.triu(np.full((S, S), -1e30, np.float32), 1), (1, 4)).astype(bf16))
    put("head_rows", np.repeat(np.eye(HH, dtype=np.float32), HD, axis=0))

    put("x", i["x"].transpose(1, 0, 2))
    qkv = i["L0_attn_Wqkv"]
    attn_layout(put, "L0_attn", qkv[:, 0:D], qkv[:, D:2 * D], qkv[:, 2 * D:3 * D], i["L0_attn_Wo"])

    put("ctx", i["ctx_512"])
    cos, sin = rope_tables(LT * P, DL)
    half = np.arange(DL) < DL // 2
    put("ctx_cos", cos.reshape(LT, P, DL).transpose(1, 0, 2))
    put("ctx_sin", np.where(half, -sin, sin).reshape(LT, P, DL).transpose(1, 0, 2))
    cos, sin = rope_tables(S, CQ)
    put("q_cos", cos.T.reshape(2, CH, S).transpose(1, 0, 2))
    put("q_sin", np.stack([sin.T[CH:], -sin.T[:CH]], 1))
    for layer in ("L0", "L1", "L2"):
        n = f"{layer}_xattn"
        wo = i[n + "_Wo"].T.reshape(H, HK, D)
        put(n + "_raw", np.concatenate([i[n + "_Wq"].reshape(H, HK, D), i[n + "_w_kc_q"], i[n + "_w_kc_kv"], wo], 2))
        wkr = i[n + "_W_kr"].transpose(0, 2, 1)
        put(n + "_rkr", np.concatenate([i[n + "_W_qr"].transpose(0, 2, 1), wkr, wkr], 2))

    def shared(w, columns):
        return np.repeat(w.reshape(-1, columns, HD), H // columns, axis=-2).reshape(w.shape[:-1] + (D,))
    n = "L1_attn"
    attn_layout(put, n, i[n + "_Wq"], shared(i[n + "_Wk"], 2), shared(i[n + "_Wv"], 2), i[n + "_Wo"],
                i[n + "_bq"], shared(i[n + "_bk"], 2), shared(i[n + "_bv"], 2), i[n + "_bo"])
    n = "L2_attn"
    attn_layout(put, n, i[n + "_wq"].T, i[n + "_wk"].T, i[n + "_wv"].T, i[n + "_wo"].T,
                i[n + "_bq"], i[n + "_bk"], i[n + "_bv"], i[n + "_bo"])
    n = "L3_xattn"
    kv = i[n + "_Wkv_expand"].T
    attn_layout(put, n, i[n + "_Wq"].T, kv[:, 0:D], kv[:, D:], i[n + "_Wout"].T)

    def tiles_of(w):
        return w.reshape(DC, P, -1, P).transpose(2, 1, 0, 3).reshape(-1, P, DC * P)

    def ffn_layout(n, gate, up, down):
        put(n + "_gu", np.concatenate([tiles_of(gate), tiles_of(up)], 2))
        if down is not None:
            put(n + "_dn", down.reshape(-1, P, D))

    def experts_layout(n, experts, hidden, router_w):
        put(n + "_wr", router_w.reshape(DC, P, experts).transpose(1, 0, 2))
        one = np.repeat(np.eye(experts, dtype=np.float16), hidden, axis=1)
        put(n + "_expert_of", np.concatenate([one, one, np.zeros((P - 2 * experts, experts * hidden), np.float16)]))

    for experts in (8, 16):
        put(f"lower{experts}", np.tile(np.tril(np.ones((experts, experts), np.float32), -1), (S, 1, 1)))
    n = "L0_ffn"
    ffn_layout(n, i[n + "_gate_w"].transpose(1, 0, 2).reshape(D, -1), i[n + "_up_w"].transpose(1, 0, 2).reshape(D, -1),
               i[n + "_down_w"].reshape(-1, D))
    experts_layout(n, 8, 512, i[n + "_router_w"])
    n = "L1_ffn"
    ffn_layout(n, i[n + "_w_gate"].reshape(-1, D).T, i[n + "_w_up"].reshape(-1, D).T,
               i[n + "_w_down"].transpose(0, 2, 1).reshape(-1, D))
    experts_layout(n, 16, 176, i[n + "_gate_w"].T)
    n = "L3_ffn"
    ffn_layout(n, i[n + "_W1"].reshape(-1, D).T, i[n + "_W2"].reshape(-1, D).T,
               i[n + "_W3"].transpose(0, 2, 1).reshape(-1, D))
    experts_layout(n, 8, 176, i[n + "_Wg"].T)
    n = "L2_ffn"
    ffn_layout(n, i[n + "_W_gate"].T, i[n + "_W_up"].T, None)
    hidden = FFN_TILES * P
    h = np.ones((1, 1), np.float32)
    while len(h) < D:
        h = np.block([[h, h], [h, -h]])
    put("h256", h)
    put(n + "_wd", i[n + "_W_down"].T.reshape(FFN_TILES, P, D).transpose(1, 0, 2))
    put(n + "_su_dp", i[n + "_SU_dp"].reshape(FFN_TILES, P).T)
    put(n + "_su_ug", i[n + "_SU_ug"].reshape(DC, P).T)
    put(n + "_sc_u", i[n + "_Wscale_ug"][:hidden].reshape(FFN_TILES, P).T)
    put(n + "_sc_g", i[n + "_Wscale_ug"][hidden:].reshape(FFN_TILES, P).T)
    put(n + "_sc_d", i[n + "_Wscale_dp"].reshape(DC, P).T)

    n = "L3_attn"
    w = np.concatenate([i[n + "_Wq"], i[n + "_Wk"], i[n + "_Wv"]], 0).T
    put(n + "_w", w.reshape(DC, P, -1).transpose(1, 0, 2))
    put(n + "_bias", np.concatenate([i[n + "_bq"], i[n + "_bk"], i[n + "_bv"]]))
    put(n + "_wo", i[n + "_Wo"].T.reshape(DC, P, D).transpose(1, 0, 2))
    put(n + "_bo", i[n + "_bo"])
    blocks = np.zeros((HKV, HD, HKV, FE), np.float32)
    for g in range(HKV):
        blocks[g, :, g, :] = i[n + "_rand_matrix"].T
    put(n + "_rb", blocks.reshape(P, HKV * FE))
    inv = np.float32(1.0) / np.power(np.float32(10000.0), np.arange(0, HD, 2, dtype=np.float32) / np.float32(HD))
    f = np.arange(S, dtype=np.float32)[:, None] * np.concatenate([inv, inv])[None, :]
    put(n + "_cos", np.cos(f))
    put(n + "_sin", np.where(np.arange(HD) < HD // 2, -np.sin(f), np.sin(f)))

    out = nc.dram_tensor("out", (S, B, D), F32, kind="ExternalOutput").ap()
    program(nc, args, out, FIRST, STAGES)
    r = run_bass_kernel_spmd(nc, [arrays], core_ids=[0])
    return np.ascontiguousarray(r.results[0]["out"].transpose(1, 0, 2))
```

```python
from contextlib import ExitStack

import concourse.bass as bass
from concourse import mybir

F32 = mybir.dt.float32
F16 = mybir.dt.float16
BF16 = mybir.dt.bfloat16
ALU = mybir.AluOpType
ACT = mybir.ActivationFunctionType
X = mybir.AxisListType.X

B, S, D = 8, 100, 256
T = B * S
P = 128
DC = D // P
NT = 400
H = 16
HD = D // H
HH = H // 2
L, DL = 1444, 64
LT = (L + P - 1) // P
EPS = 1e-5


class Core:

    def sems(self, kind, names):
        if kind not in self.kinds:
            self.kinds[kind] = {nm: self.sem(f"{kind}_{nm}") for nm in names}
        return self.kinds[kind]

    def clear(self, kind):
        self.used.append(kind)

    def cleared(self, pool):
        for kind in self.used:
            for s in self.kinds[kind].values():
                pool.sem_clear(s)
        self.used = []


class Steps:

    def __init__(self, eng, sem):
        self.eng, self.sem, self.base, self.n = eng, sem, 0, 0

    def link(self, ins):
        self.n += 1
        ins.then_inc(self.sem, 1)
        self.eng.wait_ge(self.sem, self.base + self.n)

    def inside(self, i, per):
        self.start, self.per = self.base + self.n, per
        self.base, self.n = self.start + i * per, 0

    def after(self, iterations):
        assert self.n == self.per, (self.n, self.per)
        self.base, self.n = self.start + iterations * self.per, 0


def banks_view(k, first, n, rows, cols):
    return k.banks[0:rows, first:first + n, 0:cols]


def setup(k):
    nc = k.nc
    s_load, s_credit = k.sem("setup_loaded"), k.sem("setup_made")
    with nc.Block() as block:
        @block.sync
        def _(sp):
            sp.dma_start(k.x[:, :, :], k.a["x"]).then_inc(s_load, 16)
            sp.dma_start(k.ident[:, :], k.a["ident"]).then_inc(s_load, 16)
            sp.dma_start(k.ident16[:, :], k.a["ident16"]).then_inc(s_load, 16)
            sp.dma_start(k.mask16[:, :], k.a["mask16"]).then_inc(s_load, 16)
            sp.dma_start(k.head_rows[:, :], k.a["head_rows"]).then_inc(s_load, 16)
            sp.wait_ge(s_load, 80)

        @block.vector
        def _(dve):
            dve.memset(k.ones64[:, :], 1.0).then_inc(s_credit, 1)
            dve.memset(k.eps[:, :], EPS).then_inc(s_credit, 1)
            dve.memset(k.gates[:, :], 0.0).then_inc(s_credit, 1)
            dve.wait_ge(s_credit, 3)

        @block.tensor
        def _(pe):
            pe.sem_inc(k.ln_transposed, 2)
            pe.wait_ge(k.ln_transposed, 2)

        @block.scalar
        def _(act):
            act.sem_inc(k.ln_copied, 2)
            act.wait_ge(k.ln_copied, 2)


def layer_norm(k, loads):
    nc = k.nc
    n = k.ln_calls
    k.ln_calls += 1
    sums, norm, tr, cp = B * n, B * n, 2 + B * n, 2 + B * n
    with nc.Block() as block:
        @block.sync
        def _(sp):
            loads(sp)

        @block.gpsimd
        def _(pool):
            k.cleared(pool)

        @block.vector
        def _(dve):
            with dve.Fori(0, B) as b:
                dve.bn_stats(k.ln_stats[:, b, :], k.x[:, b, :]).then_inc(k.ln_summed, 1)
            dve.wait_ge(k.ln_summed, sums + B)
            for b in range(B):
                dve.bn_aggr(k.ln_mv[:, b, :], k.ln_stats[:, b, :]).then_inc(k.ln_var, 1)
            dve.wait_ge(k.ln_std, n + 1)
            dve.reciprocal(k.ln_rstd[:, :], k.ln_root[:, :]).then_inc(k.ln_recip, 1)
            dve.wait_ge(k.ln_recip, n + 1)
            with dve.Fori(0, B // 2) as i:
                for j in range(2):
                    b = 2 * i + j
                    dve.wait_ge(k.ln_transposed, tr + b - 1)
                    dve.tensor_scalar(k.ln_xn[:, j, :], k.x[:, b, :], k.ln_mv[:, b, 0:1], k.ln_rstd[:, bass.ds(b, 1)],
                                      ALU.subtract, ALU.mult).then_inc(k.ln_normed, 1)

        @block.scalar
        def _(act):
            act.wait_ge(k.ln_var, B * (n + 1))
            act.activation(k.ln_root[:, :], k.ln_mv[:, :, 1], ACT.Sqrt, bias=k.eps[0:S, :]).then_inc(k.ln_std, 1)
            with act.Fori(0, B // 2) as i:
                for j in range(2):
                    b = 2 * i + j
                    act.wait_ge(k.ln_transposed, tr + b + 1)
                    act.copy(k.xnT[:, :, bass.ds(b * S, S)],
                             k.banks[:, j, 0:DC * S].rearrange("p (c s) -> p c s", c=DC)).then_inc(k.ln_copied, 1)

        @block.tensor
        def _(pe):
            with pe.Fori(0, B // 2) as i:
                for j in range(2):
                    b = 2 * i + j
                    pe.wait_ge(k.ln_normed, norm + b + 1)
                    pe.wait_ge(k.ln_copied, cp + b - 1)
                    for c in range(DC):
                        ins = pe.transpose(k.banks[:, j, c * S:(c + 1) * S], k.ln_xn[:, j, c * P:(c + 1) * P],
                                           k.ident[0:S, 0:S])
                    ins.then_inc(k.ln_transposed, 1)


def self_attention(k, name, src, chunks, rows, scale, bias):
    nc, a = k.nc, k.a
    with ExitStack() as ctx:
        def sb(nm, shape, dt=F32):
            return ctx.enter_context(nc.sbuf_tensor(f"{name}_{nm}", shape, dt))

        wq = sb("wq", [P, DC, D])
        wk = sb("wk", [rows, chunks, D])
        wv = sb("wv", [rows, chunks, D])
        wo = sb("wo", [P, DC, D])
        qT = sb("qT", [P, DC, T])
        kT = sb("kT", [P, DC, T])
        v = sb("v", [S, B, H, HD + 1])
        q_st = sb("q_st", [P, 2, S])
        k_st = sb("k_st", [P, 2, HH, S])
        sc = sb("sc", [S, 2, HH, S])
        pr = sb("pr", [S, 2, HH, S])
        prT = sb("prT", [S, HH, S])
        top = sb("top", [S, 2, HH])
        den = sb("den", [S, HH])
        o = sb("o", [S, HH, HD])
        oT = sb("oT", [P, S])
        if bias:
            bq, bk = sb("bq", [P, DC]), sb("bk", [P, DC])
            bv, bo = sb("bv", [S, D]), sb("bo", [S, D])
        sem = k.sems("attn", (
            "wq", "wk", "wv", "wo", "bias", "ones", "proj", "proj_qk", "proj_v", "staged", "scored", "maxed", "less",
            "exped", "transposed", "copied", "pv", "denom", "normed", "yready", "added"))
        qk_jobs = [(dst, w, s_, c, t, n) for dst, w, s_, c in (("q", wq, k.xnT, DC), ("k", wk, src, chunks))
                   for t in range(DC) for n in range(2)]
        nqk = len(qk_jobs)

        def loads(sp):
            sp.dma_start(wq[:, :, :], a[f"{name}_wq"]).then_inc(sem["wq"], 16)
            sp.dma_start(wk[:, :, :], a[f"{name}_wk"]).then_inc(sem["wk"], 16)
            sp.dma_start(wv[:, :, :], a[f"{name}_wv"]).then_inc(sem["wv"], 16)
            sp.dma_start(wo[:, :, :], a[f"{name}_wo"]).then_inc(sem["wo"], 16)
            if bias:
                sp.dma_start(bq[:, :], a[f"{name}_bq"]).then_inc(sem["bias"], 16)
                sp.dma_start(bk[:, :], a[f"{name}_bk"]).then_inc(sem["bias"], 16)
                for dst, nm in ((bv, "bv"), (bo, "bo")):
                    sp.dma_start(dst[:, :], a[f"{name}_{nm}"].partition_broadcast(S)).then_inc(sem["bias"], 16)
        layer_norm(k, loads)

        with nc.Block() as block:
            @block.tensor
            def _(pe):
                pe.wait_ge(sem["wq"], 16)
                for n_job, (_, w, s_, cc, t, n) in enumerate(qk_jobs):
                    if n_job == nqk // 2:
                        pe.wait_ge(sem["wk"], 16)
                    if n_job >= 4:
                        pe.wait_ge(sem["proj_qk"], n_job - 3)
                    for c in range(cc):
                        ins = pe.matmul(k.banks[:, n_job % 4, 0:NT], w[:, c, t * P:(t + 1) * P],
                                        s_[:, c, n * NT:(n + 1) * NT], start=c == 0, stop=c == cc - 1)
                    ins.then_inc(sem["proj"], 1)
                pe.wait_ge(sem["wv"], 16)
                for b in range(B):
                    if b >= 4:
                        pe.wait_ge(sem["proj_v"], b - 3)
                    for c in range(chunks):
                        ins = pe.matmul(k.banks[0:S, 4 + b % 4, 0:D], src[:, c, b * S:(b + 1) * S],
                                        wv[:, c, :], start=c == 0, stop=c == chunks - 1)
                    ins.then_inc(sem["proj"], 1)
                pe.wait_ge(sem["proj_qk"], nqk)
                pe.wait_ge(sem["proj_v"], B)
                pe.wait_ge(sem["wo"], 16)

                def scores(u, half):
                    pe.wait_ge(sem["staged"], u + 1)
                    for g in range(2):
                        bank = k.banks[0:S, 2 * half + g, 0:4 * S]
                        pe.matmul(bank, k.ident16[0:S, 0:S], k.mask16[:, :], start=True, stop=False)
                        ins = pe.matmul(bank, q_st[:, half, :], k_st[:, half, 4 * g:4 * g + 4, :],
                                        start=False, stop=True)
                    ins.then_inc(sem["scored"], 1)

                def project(half):
                    ins = pe.matmul(k.banks[0:S, 7, 0:D], oT[:, :], wo[:, half, :], start=half == 0, stop=half == 1)
                    ins.then_inc(sem["yready"], 1)

                def unit(b, half, following, previous):
                    u = 2 * b + half
                    if following:
                        scores(u + 1, 1 - half)
                    pe.wait_ge(sem["exped"], u + 1)
                    if previous:
                        pe.wait_ge(sem["copied"], 2 * u)
                    for h in range(HH):
                        ins = pe.transpose(k.banks[0:S, 4 + h // 4, (h % 4) * S:(h % 4 + 1) * S], pr[:, half, h, :],
                                           k.ident[0:S, 0:S])
                    if previous:
                        pe.wait_ge(sem["normed"], u)
                        ins = pe.transpose(k.banks[:, 5, 4 * S:5 * S], o[:, :, :].rearrange("s h d -> s (h d)"),
                                           k.ident[0:S, 0:S])
                    ins.then_inc(sem["transposed"], 1)
                    pe.wait_ge(sem["copied"], 2 * u + 2)
                    for h in range(HH):
                        ins = pe.matmul(k.banks[0:S, 6, h * (HD + 1):(h + 1) * (HD + 1)], prT[:, h, :],
                                        v[:, b, HH * half + h, :], start=True, stop=True)
                    ins.then_inc(sem["pv"], 1)
                    if previous:
                        if half == 1:
                            if not isinstance(b, int) or b >= 1:
                                pe.wait_ge(sem["added"], b)
                        project(1 - half)

                scores(0, 0)
                unit(0, 0, True, False)
                unit(0, 1, True, True)
                with pe.Fori(1, B - 1) as b:
                    unit(b, 0, True, True)
                    unit(b, 1, True, True)
                unit(B - 1, 0, True, True)
                unit(B - 1, 1, False, True)
                pe.wait_ge(sem["copied"], 4 * B)
                pe.wait_ge(sem["normed"], 2 * B)
                pe.transpose(k.banks[:, 5, 4 * S:5 * S], o[:, :, :].rearrange("s h d -> s (h d)"),
                             k.ident[0:S, 0:S]).then_inc(sem["transposed"], 1)
                pe.wait_ge(sem["copied"], 4 * B + 1)
                project(1)

            @block.scalar
            def _(act):
                if bias:
                    act.wait_ge(sem["bias"], 64)
                for n_job, (which, _, _, _, t, n) in enumerate(qk_jobs):
                    act.wait_ge(sem["proj"], n_job + 1)
                    dst = (qT if which == "q" else kT)[:, t, n * NT:(n + 1) * NT]
                    if bias:
                        bb = (bq if which == "q" else bk)[:, t:t + 1]
                        act.activation(dst, k.banks[:, n_job % 4, 0:NT], ACT.Identity, bias=bb).then_inc(sem["proj_qk"], 1)
                    else:
                        act.copy(dst, k.banks[:, n_job % 4, 0:NT]).then_inc(sem["proj_qk"], 1)

                def exponentials(u, half):
                    act.wait_ge(sem["less"], u + 1)
                    act.activation(pr[:, half], sc[:, half], ACT.Exp, scale=scale).then_inc(sem["exped"], 1)

                def unit(u, half, following, previous):
                    act.wait_ge(sem["transposed"], u + 1)
                    if previous:
                        act.wait_ge(sem["pv"], u)
                    act.copy(prT[:, :, :].rearrange("s (g h) t -> s g (h t)", g=2),
                             banks_view(k, 4, 2, S, 4 * S)).then_inc(sem["copied"], 1 if previous else 2)
                    if previous:
                        if isinstance(u, int) and u == 1:
                            pass
                        else:
                            act.wait_ge(sem["yready"], u - 1)
                        act.copy(oT[:, :], k.banks[:, 5, 4 * S:5 * S]).then_inc(sem["copied"], 1)
                    if following:
                        exponentials(u + 1, 1 - half)

                exponentials(0, 0)
                unit(0, 0, True, False)
                unit(1, 1, True, True)
                with act.Fori(1, B - 1) as b:
                    unit(2 * b, 0, True, True)
                    unit(2 * b + 1, 1, True, True)
                unit(2 * B - 2, 0, True, True)
                unit(2 * B - 1, 1, False, True)
                act.wait_ge(sem["transposed"], 2 * B + 1)
                act.wait_ge(sem["yready"], 2 * B - 1)
                act.copy(oT[:, :], k.banks[:, 5, 4 * S:5 * S]).then_inc(sem["copied"], 1)

            @block.gpsimd
            def _(pool):
                pool.wait_ge(sem["proj_qk"], nqk)
                def stage(b, half):
                    at = bass.ds(b * S, S)
                    pool.tensor_copy(q_st[:, half, :], qT[:, half, at])
                    pool.tensor_tensor(k_st[:, half], kT[:, half, at].unsqueeze(1).broadcast_to((P, HH, S)),
                                       k.head_rows[:, :].unsqueeze(2).broadcast_to((P, HH, S)), ALU.mult)\
                        .then_inc(sem["staged"], 1)
                stage(0, 0)
                stage(0, 1)
                with pool.Fori(1, B) as b:
                    for half in range(2):
                        pool.wait_ge(sem["scored"], 2 * b + half - 1)
                        stage(b, half)

            @block.vector
            def _(dve):
                dve.memset(v[:, :, :, HD:HD + 1], 1.0).then_inc(sem["ones"], 1)
                if bias:
                    dve.wait_ge(sem["bias"], 64)
                    dve.tensor_tensor(k.x[:, :, :], k.x[:, :, :],
                                      bo[:, :].unsqueeze(1).broadcast_to((S, B, D)), ALU.add).then_inc(sem["ones"], 1)
                for b in range(B):
                    dve.wait_ge(sem["proj"], nqk + b + 1)
                    dst, got = v[:, b, :, 0:HD], k.banks[0:S, 4 + b % 4, 0:D].rearrange("s (h d) -> s h d", h=H)
                    if bias:
                        dve.tensor_tensor(dst, got, bv[:, :].rearrange("s (h d) -> s h d", h=H), ALU.add)\
                           .then_inc(sem["proj_v"], 1)
                    else:
                        dve.tensor_copy(dst, got).then_inc(sem["proj_v"], 1)

                def subtract_max(u, half, first):
                    dve.wait_ge(sem["scored"], u + 1)
                    got = banks_view(k, 2 * half, 2, S, 4 * S).rearrange("s g (h t) -> s g h t", t=S)
                    tp = top[:, half, :].rearrange("s (g h) -> s g h", g=2)
                    dve.tensor_reduce(tp, got, X, ALU.max).then_inc(sem["maxed"], 1)
                    dve.wait_ge(sem["maxed"], u + 1)
                    if not first:
                        dve.wait_ge(sem["exped"], u - 1)
                    for g in range(2):
                        ins = dve.tensor_tensor(sc[:, half, 4 * g:4 * g + 4, :], got[:, g],
                                                tp[:, g].unsqueeze(2).broadcast_to((S, 4, S)), ALU.subtract)
                    ins.then_inc(sem["less"], 1)

                def normalize(u):
                    dve.wait_ge(sem["pv"], u + 1)
                    got = k.banks[0:S, 6, 0:HH * (HD + 1)].rearrange("s (h d) -> s h d", h=HH)
                    dve.reciprocal(den[:, :].unsqueeze(2), got[:, :, HD:HD + 1]).then_inc(sem["denom"], 1)
                    dve.wait_ge(sem["denom"], u + 1)
                    dve.tensor_tensor(o[:, :, :], got[:, :, 0:HD], den[:, :].unsqueeze(2).broadcast_to((S, HH, HD)),
                                      ALU.mult).then_inc(sem["normed"], 1)

                def add(b):
                    dve.wait_ge(sem["yready"], 2 * b + 2)
                    dve.tensor_tensor(k.x[:, b, :], k.x[:, b, :], k.banks[0:S, 7, 0:D], ALU.add)\
                       .then_inc(sem["added"], 1)

                dve.wait_ge(sem["ones"], 2 if bias else 1)
                subtract_max(0, 0, True)
                subtract_max(1, 1, True)
                normalize(0)
                with dve.Fori(1, B) as b:
                    subtract_max(2 * b, 0, False)
                    normalize(2 * b - 1)
                    subtract_max(2 * b + 1, 1, False)
                    add(b - 1)
                    normalize(2 * b)
                normalize(2 * B - 1)
                add(B - 1)
    k.clear("attn")


KV_BANKS = 3
L_LAST = L - (LT - 1) * P


def context(k):
    nc, a = k.nc, k.a
    HL = DL // 2
    with ExitStack() as ctx:
        def sb(nm, shape, dt=F32):
            return ctx.enter_context(nc.sbuf_tensor(f"ctx_{nm}", shape, dt))

        raw = sb("raw", [P, 2, LT, DL])
        cos, sin = sb("cos", [P, LT, DL]), sb("sin", [P, LT, DL])
        c_part, s_part = sb("c_part", [P, LT, DL]), sb("s_part", [P, LT, DL])
        twice = sb("twice", [P, 2, LT, 2, DL])
        loaded = [k.sem("ctx_loaded0"), k.sem("ctx_loaded1")]
        tables, cleared, parts, roped = k.sem("ctx_tables"), k.sem("ctx_cleared"), k.sem("ctx_parts"), k.sem("ctx_roped")
        doubled, turned = k.sem("ctx_doubled"), k.sem("ctx_turned")
        high, low = k.sem("ctx_high"), k.sem("ctx_low")

        with nc.Block() as block:
            @block.sync
            def _(sp):
                sp.dma_start(cos[:, :, :], a["ctx_cos"]).then_inc(tables, 16)
                sp.dma_start(sin[:, :, :], a["ctx_sin"]).then_inc(tables, 16)

                def load(b, j):
                    sp.dma_start(raw[:, j, 0:LT - 1, :],
                                 a["ctx"][b, 0:(LT - 1) * P, :].rearrange("(t p) d -> p t d", p=P)).then_inc(loaded[j], 16)
                    sp.dma_start(raw[0:L_LAST, j, LT - 1, :], a["ctx"][b, (LT - 1) * P:L, :]).then_inc(loaded[j], 16)
                sp.wait_ge(cleared, 1)
                load(0, 0)
                load(1, 1)
                with sp.Fori(1, B // 2) as i:
                    for j in range(2):
                        sp.wait_ge(roped, 2 * i + j - 1)
                        load(2 * i + j, j)

            @block.vector
            def _(dve):
                dve.memset(raw[:, :, LT - 1, :], 0.0).then_inc(cleared, 1)
                dve.memset(k.kv_h1[DL:DL + 2, :], 1.0).then_inc(cleared, 1)
                dve.memset(k.kv_h1[0:DL, B * L:], 0.0).then_inc(cleared, 1)
                dve.memset(k.kv_hl[:, B * L:], 0.0).then_inc(cleared, 1)
                dve.wait_ge(tables, 32)

                def rope(i, j):
                    b = 2 * i + j
                    dve.wait_ge(loaded[j], 32 * i + 32)
                    dve.tensor_tensor(c_part[:, :, :], raw[:, j], cos[:, :, :], ALU.mult).then_inc(parts, 1)
                    dve.tensor_tensor(s_part[:, :, 0:HL], raw[:, j, :, HL:DL], sin[:, :, 0:HL], ALU.mult).then_inc(parts, 1)
                    dve.tensor_tensor(s_part[:, :, HL:DL], raw[:, j, :, 0:HL], sin[:, :, HL:DL], ALU.mult).then_inc(parts, 1)
                    dve.wait_ge(parts, 3 * b + 3)
                    dve.tensor_tensor(k.kv_tok[:, b], c_part[:, :, :], s_part[:, :, :], ALU.add).then_inc(roped, 1)
                    dve.wait_ge(roped, b + 1)

                def split(i, j):
                    b = 2 * i + j
                    dve.wait_ge(high, b + 1)
                    at = bass.ds(b * L, L)
                    dve.tensor_copy(k.kv_h1[0:DL, at], k.kv_hl[0:DL, at])
                    got = k.banks[DL:2 * DL, KV_BANKS * j:KV_BANKS * (j + 1), :].rearrange("p a c -> p (a c)")[:, 0:L]
                    dve.tensor_tensor(k.kv_hl[DL:2 * DL, at], got, k.kv_hl[DL:2 * DL, at], ALU.subtract).then_inc(low, 1)
                rope(0, 0)
                with dve.Fori(0, B // 2 - 1) as i:
                    rope(i, 1)
                    split(i, 0)
                    rope(i + 1, 0)
                    split(i, 1)
                rope(B // 2 - 1, 1)
                split(B // 2 - 1, 0)
                split(B // 2 - 1, 1)

            @block.scalar
            def _(act):
                def double(i, j, first):
                    b = 2 * i + j
                    act.wait_ge(roped, b + 1)
                    if not first:
                        act.wait_ge(turned, b - 1)
                    act.copy(twice[:, j, :, :, :], k.kv_tok[:, b].unsqueeze(2).broadcast_to((P, LT, 2, DL)))\
                       .then_inc(doubled, 1)

                def keep_high(i, j):
                    b = 2 * i + j
                    act.wait_ge(turned, b + 1)
                    got = k.banks[:, KV_BANKS * j:KV_BANKS * (j + 1), :].rearrange("p a c -> p (a c)")[:, 0:L]
                    act.copy(k.kv_hl[:, bass.ds(b * L, L)], got).then_inc(high, 1)
                double(0, 0, True)
                double(0, 1, True)
                keep_high(0, 0)
                with act.Fori(1, B // 2) as i:
                    double(i, 0, False)
                    keep_high(i - 1, 1)
                    double(i, 1, False)
                    keep_high(i, 0)
                keep_high(B // 2 - 1, 1)

            @block.tensor
            def _(pe):
                def batch(b, j, first):
                    pe.wait_ge(doubled, b + 1)
                    if not first:
                        pe.wait_ge(low, b - 1)
                    for t in range(LT):
                        m = P if t < LT - 1 else L_LAST
                        bank = k.banks[:, KV_BANKS * j + t // 4, (t % 4) * P:(t % 4) * P + m]
                        ins = pe.transpose(bank, twice[0:m, j, t, :, :].rearrange("p a d -> p (a d)"), k.ident[0:m, 0:m])
                    ins.then_inc(turned, 1)
                batch(0, 0, True)
                batch(1, 1, True)
                with pe.Fori(1, B // 2) as i:
                    batch(2 * i, 0, False)
                    batch(2 * i + 1, 1, False)


HK, CQ, R = 128, 192, 64
CH = CQ // 2
PAIRS = H // 2


def cross_queries(k, name, rope):
    nc, a = k.nc, k.a
    with ExitStack() as ctx:
        def sb(nm, shape, dt=F32):
            return ctx.enter_context(nc.sbuf_tensor(f"{name}_{nm}", shape, dt))

        raw = sb("raw", [P, 2, D + CQ + DL + D])
        rkr = sb("rkr", [R, 2, CQ + 2 * DL])
        w1 = sb("w1", [P, 2, DC, CQ])
        w2 = sb("w2", [CH, 2, 2, P])
        q_rot = sb("q_rot", [CH, 2, 2, NT])
        if rope:
            prod = sb("prod", [CH, 2, 2, 2, NT])
            cos, sin = sb("cos", [CH, 2, S]), sb("sin", [CH, 2, S])
        sem = k.sems("queries", (
            "loaded0", "loaded1", "tables", "merged", "merged_copied", "w1_copied", "big", "taken", "rotated", "absorbed", "high", "low",
            "padded"))
        loaded = [sem["loaded0"], sem["loaded1"]]

        def load(sp, h, j):
            sp.dma_start(raw[:, j, :], a[f"{name}_raw"][h]).then_inc(loaded[j], 16)
            sp.dma_start(rkr[:, j, :], a[f"{name}_rkr"][h]).then_inc(loaded[j], 16)

        def loads(sp):
            load(sp, 0, 0)
            load(sp, 1, 1)
            if rope:
                sp.dma_start(cos[:, :, :], a["q_cos"]).then_inc(sem["tables"], 16)
                sp.dma_start(sin[:, :, :], a["q_sin"]).then_inc(sem["tables"], 16)
        layer_norm(k, loads)

        with nc.Block() as block:
            @block.sync
            def _(sp):
                with sp.Fori(1, PAIRS) as i:
                    for j in range(2):
                        sp.wait_ge(sem["merged"], 2 * i + j - 1)
                        load(sp, 2 * i + j, j)

            @block.tensor
            def _(pe):
                def merge(i, j, first):
                    h = 2 * i + j
                    pe.wait_ge(loaded[j], 32 * i + 32)
                    if not first:
                        pe.wait_ge(sem["merged_copied"], h)
                    for c in range(DC):
                        pe.matmul(k.banks[:, 0, c * CQ:(c + 1) * CQ], raw[:, j, c * P:(c + 1) * P],
                                  raw[:, j, D:D + CQ], start=True, stop=True)
                    for c in range(2):
                        pe.matmul(k.banks[0:CH, 1, c * P:(c + 1) * P], rkr[:, j, c * CH:(c + 1) * CH],
                                  rkr[:, j, CQ:CQ + 2 * DL], start=True, stop=True)
                    pe.matmul(k.banks[DL * j:DL * (j + 1), 2, 0:D], raw[:, j, D + CQ:D + CQ + DL],
                              raw[:, j, D + CQ + DL:], start=True, stop=True).then_inc(sem["merged"], 1)

                def compressed(i, j, n, first):
                    h = 2 * i + j
                    if n == 0:
                        pe.wait_ge(sem["w1_copied"], h + 1)
                    if not first:
                        pe.wait_ge(sem["taken"], 2 * h + n - 1)
                    for half in range(2):
                        for c in range(DC):
                            ins = pe.matmul(k.banks[0:CH, 3 + 2 * n + half, 0:NT], w1[:, j, c, half * CH:(half + 1) * CH],
                                            k.xnT[:, c, n * NT:(n + 1) * NT], start=c == 0, stop=c == DC - 1)
                    ins.then_inc(sem["big"], 1)

                def absorbed(i, j, n, first):
                    t = 2 * (2 * i + j) + n
                    pe.wait_ge(sem["rotated" if rope else "taken"], t + 1)
                    if n == 0:
                        pe.wait_ge(sem["merged_copied"], 2 * i + j + 1)
                    if not first:
                        pe.wait_ge(sem["low"], t)
                    for half in range(2):
                        ins = pe.matmul(k.banks[:, 7, 0:NT], w2[:, j, half, :], q_rot[:, n, half, :],
                                        start=half == 0, stop=half == 1)
                    ins.then_inc(sem["absorbed"], 1)

                def head(i, j, first, last):
                    ni, nj = (i, 1) if j == 0 else (i + 1, 0)
                    if not last:
                        merge(ni, nj, False)
                    for n in range(2):
                        if not last:
                            compressed(ni, nj, n, False)
                        absorbed(i, j, n, first and n == 0)
                merge(0, 0, True)
                compressed(0, 0, 0, True)
                compressed(0, 0, 1, True)
                head(0, 0, True, False)
                head(0, 1, False, False)
                with pe.Fori(1, PAIRS - 1) as i:
                    head(i, 0, False, False)
                    head(i, 1, False, False)
                head(PAIRS - 1, 0, False, False)
                head(PAIRS - 1, 1, False, True)

            @block.scalar
            def _(act):
                def copy_merged(i, j):
                    act.wait_ge(sem["merged"], 2 * i + j + 1)
                    act.copy(w1[:, j, :, :], k.banks[:, 0, 0:DC * CQ].rearrange("p (c q) -> p c q", c=DC))\
                       .then_inc(sem["w1_copied"], 1)
                    act.copy(w2[:, j, :, :], k.banks[0:CH, 1, 0:2 * P].rearrange("p (c q) -> p c q", c=2))
                    act.copy(k.wvo[DL * j:DL * (j + 1), i, :], k.banks[DL * j:DL * (j + 1), 2, 0:D])\
                       .then_inc(sem["merged_copied"], 1)

                def high(i, j, n):
                    t = 2 * (2 * i + j) + n
                    act.wait_ge(sem["absorbed"], t + 1)
                    act.copy(k.q_hh[:, 4 * n:4 * n + 4, bass.ds((2 * i + j) * S, S)],
                             k.banks[:, 7, 0:NT].rearrange("p (b s) -> p b s", b=4)).then_inc(sem["high"], 1)
                copy_merged(0, 0)
                with act.Fori(0, PAIRS - 1) as i:
                    for j in range(2):
                        copy_merged(*((i, 1) if j == 0 else (i + 1, 0)))
                        high(i, j, 0)
                        high(i, j, 1)
                copy_merged(PAIRS - 1, 1)
                for j in range(2):
                    high(PAIRS - 1, j, 0)
                    high(PAIRS - 1, j, 1)

            @block.vector
            def _(dve):
                def take(i, j, n, first):
                    t = 2 * (2 * i + j) + n
                    dve.wait_ge(sem["big"], t + 1)
                    got = k.banks[0:CH, 3 + 2 * n:5 + 2 * n, 0:NT]
                    if not rope:
                        if not first:
                            dve.wait_ge(sem["absorbed"], t - 1)
                        dve.tensor_copy(q_rot[:, n, :, :], got).then_inc(sem["taken"], 1)
                        return
                    if not first:
                        dve.wait_ge(sem["rotated"], t - 1)
                    g4 = got.rearrange("p a (b s) -> p a b s", s=S)
                    for half in range(2):
                        dve.tensor_tensor(prod[:, n, 0, half, :].rearrange("p (b s) -> p b s", s=S), g4[:, half],
                                          cos[:, half, :].unsqueeze(1).broadcast_to((CH, 4, S)), ALU.mult)
                        ins = dve.tensor_tensor(prod[:, n, 1, 1 - half, :].rearrange("p (b s) -> p b s", s=S), g4[:, half],
                                                sin[:, half, :].unsqueeze(1).broadcast_to((CH, 4, S)), ALU.mult)
                    ins.then_inc(sem["taken"], 1)

                def low(i, j, n):
                    t = 2 * (2 * i + j) + n
                    dve.wait_ge(sem["high"], t + 1)
                    at = (slice(0, DL), slice(4 * n, 4 * n + 4), bass.ds((2 * i + j) * S, S))
                    dve.tensor_tensor(k.q_l[at], k.banks[0:DL, 7, 0:NT].rearrange("p (b s) -> p b s", b=4),
                                      k.q_hh[at], ALU.subtract).then_inc(sem["low"], 1)
                dve.memset(k.q_hh[:, :, Q:], 0.0).then_inc(sem["padded"], 1)
                if rope:
                    dve.wait_ge(sem["tables"], 32)
                take(0, 0, 0, True)
                take(0, 0, 1, True)
                for n in range(2):
                    take(0, 1, n, False)
                    low(0, 0, n)
                for n in range(2):
                    take(1, 0, n, False)
                    low(0, 1, n)
                with dve.Fori(1, PAIRS - 1) as i:
                    for j in range(2):
                        for n in range(2):
                            take(*((i, 1) if j == 0 else (i + 1, 0)), n, False)
                            low(i, j, n)
                for n in range(2):
                    take(PAIRS - 1, 1, n, False)
                    low(PAIRS - 1, 0, n)
                low(PAIRS - 1, 1, 0)
                low(PAIRS - 1, 1, 1)

            @block.gpsimd
            def _(pool):
                def rotate(i, j, n, first):
                    t = 2 * (2 * i + j) + n
                    pool.wait_ge(sem["taken"], t + 1)
                    if not first:
                        pool.wait_ge(sem["absorbed"], t - 1)
                    pool.tensor_tensor(q_rot[:, n, :, :], prod[:, n, 0], prod[:, n, 1], ALU.add)\
                        .then_inc(sem["rotated"], 1)
                if rope:
                    for n in range(2):
                        rotate(0, 0, n, True)
                    for n in range(2):
                        rotate(0, 1, n, False)
                    with pool.Fori(1, PAIRS) as i:
                        for j in range(2):
                            for n in range(2):
                                rotate(i, j, n, False)
    k.clear("queries")


MAX_CHUNKS = [(0, 482), (482, 482), (964, 480)]
Q = H * S
QT = (Q + P - 1) // P
TASKS = QT * len(MAX_CHUNKS)
STEPS = 2 * LT
TURN = 21
OUTPUT = 5
SLOTS = 4


def aux_plan(tops, output):
    plan, last, place = [[] for _ in range(STEPS)], {}, 0
    for s in range(STEPS):
        todo = [("top", n, 6 + n % 2) for n in range(2 * s, min(2 * s + 2, TASKS))] if tops else []
        if tops and s == TURN:
            todo.append(("turn", 0, 7))
        if output and s == OUTPUT:
            todo.append(("output", 0, 6))
        for kind, n, bank in todo:
            plan[s].append((place, kind, n, bank, last.get(bank, 0)))
            place += 1
            last[bank] = place
    return plan, place


def cross_attention(k, name):
    nc = k.nc
    with ExitStack() as ctx:
        def sb(nm, shape, dt=F32):
            return ctx.enter_context(nc.sbuf_tensor(f"{name}_{nm}", shape, dt))

        kv = sb("kv", [P, LT, DL])
        pr = sb("pr", [P, SLOTS, 2 * NT])
        pr_last = sb("pr_last", [P, 2 * NT])
        pair = sb("pair", [P, 2, 2 * NT])
        quad = sb("quad", [P, 2, 2 * NT])
        raw = sb("att_raw", [P, 2, NT])
        rden = sb("rden", [P, NT])
        att = sb("att", [P, 2, NT])
        top3 = sb("top3", [P, QT, len(MAX_CHUNKS)])
        top = sb("top", [P, QT])
        shift = sb("shift", [QT, 2, P], F16)
        sem = k.sems("cross", (
            "staged", "scored", "exped", "weighted", "paired", "quaded", "summed", "raw", "recip", "normed", "aux",
            "aux_used", "topped", "shift_high", "shifted", "shift_in", "cleared"))
        first_plan, first_n = aux_plan(True, False)
        mid_plan, mid_n = aux_plan(True, True)
        last_plan, last_n = aux_plan(False, True)
        QUADS = STEPS // 4

        def body_of(b):
            ahead = TASKS + 1
            if isinstance(b, int) and b == 0:
                return first_plan, ahead
            base = ahead + first_n + (b - 1) * mid_n
            return (last_plan if isinstance(b, int) and b == B - 1 else mid_plan), base

        end = TASKS + 1 + first_n + (B - 2) * mid_n + last_n

        def weights_of(s):
            return pr[:, s % SLOTS, :] if s % LT < LT - 1 else pr_last[:, :]

        def queries(q, b, half, c):
            return q[:, b, half * 2 * NT:(half + 1) * 2 * NT].rearrange("p (i j s) -> p j i s", j=2, s=S)[:, c]

        def batches(eng, batch):
            batch(0)
            with eng.Fori(1, B - 1) as b:
                batch(b)
            batch(B - 1)

        with nc.Block() as block:
            @block.sync
            def _(sp):
                def place_shift(b, after):
                    sp.wait_ge(sem["shifted"], after)
                    for part in range(2):
                        sp.dma_start(k.q_l[DL + part:DL + part + 1, b, :].rearrange("o (t c) -> o t c", c=P),
                                     shift[:, part, :]).then_inc(sem["shift_in"], 16)
                place_shift(0, 1)
                with sp.Fori(1, B) as b:
                    place_shift(b, b + 1)

            @block.gpsimd
            def _(pool):
                pool.sem_inc(sem["paired"], 2)

                def stage(b, t):
                    pool.wait_ge(sem["weighted"], SLOTS + STEPS * b - LT + t + 1)
                    pool.tensor_copy(kv[:, t, :], k.kv_tok[:, b, t, :]).then_inc(sem["staged"], 1)

                def batch(b):
                    for n in range(STEPS // 2):
                        pool.wait_ge(sem["exped"], STEPS * b + 2 * n + 4)
                        if n >= 2 or not (isinstance(b, int) and b == 0):
                            pool.wait_ge(sem["quaded"], QUADS * b + n // 2)
                        pool.tensor_tensor(pair[:, n % 2, :], weights_of(2 * n), weights_of(2 * n + 1), ALU.add)\
                            .then_inc(sem["paired"], 1)
                        if not (isinstance(b, int) and b == B - 1) and n > LT // 2:
                            for t in range(2 * (n - LT // 2) - 2, 2 * (n - LT // 2)):
                                stage(b + 1, t)
                    if not (isinstance(b, int) and b == B - 1):
                        stage(b + 1, LT - 2)
                        stage(b + 1, LT - 1)
                pool.tensor_copy(kv[:, :, :], k.kv_tok[:, 0]).then_inc(sem["staged"], LT)
                batches(pool, batch)

            @block.tensor
            def _(pe):
                pe.sem_inc(sem["weighted"], SLOTS)

                def top_task(b, n):
                    t, (at, cols) = n // len(MAX_CHUNKS), MAX_CHUNKS[n % len(MAX_CHUNKS)]
                    pe.matmul(k.banks[:, 6 + n % 2, 0:cols], k.q_hh[:, b, t * P:(t + 1) * P],
                              k.kv_hl[:, bass.ds(b * L + at, cols)], start=True, stop=True).then_inc(sem["aux"], 1)

                def turn_tops(after):
                    pe.wait_ge(sem["topped"], after)
                    pe.transpose(k.banks[0:QT, 7, 0:P], top[:, :], k.ident[:, :]).then_inc(sem["aux"], 1)

                def scores(b, s):
                    half, t, bank = s // LT, s % LT, 2 * (s % 2)
                    pe.wait_ge(sem["exped"], STEPS * b + s + 1)
                    if s == 0:
                        pe.wait_ge(sem["shift_in"], 32 * b + 32)
                    at = bass.ds(b * L + t * P, P)
                    for c in range(2):
                        pe.matmul(k.banks[:, bank + c, 0:NT], k.kv_hl[:, at], queries(k.q_hh, b, half, c),
                                  start=True, stop=False)
                    for c in range(2):
                        ins = pe.matmul(k.banks[:, bank + c, 0:NT], k.kv_h1[:, at], queries(k.q_l, b, half, c),
                                        start=False, stop=True)
                    ins.then_inc(sem["scored"], 1)

                def weigh(b, s):
                    half, t = s // LT, s % LT
                    weights = weights_of(s)
                    pe.wait_ge(sem["exped"], STEPS * b + s + 3)
                    if half == 0:
                        pe.wait_ge(sem["staged"], LT * b + t + 1)
                    if t == 0 and not (isinstance(b, int) and b == 0 and half == 0):
                        pe.wait_ge(sem["raw"], 2 * b + half)
                    for c in range(2):
                        ins = pe.matmul(k.banks[DL * c:DL * (c + 1), 4, 0:NT], kv[:, t, :],
                                        weights[:, c * NT:(c + 1) * NT], start=t == 0, stop=t == LT - 1)
                    ins.then_inc(sem["weighted"], 1)

                def total(b, n):
                    pe.wait_ge(sem["quaded"], QUADS * b + n + 1)
                    if n % 3 == 0 and not (isinstance(b, int) and b == 0 and n == 0):
                        pe.wait_ge(sem["normed"], 2 * b + n // 3)
                    for c in range(2):
                        ins = pe.matmul(k.banks[DL * c:DL * (c + 1), 5, 0:NT], k.ones64[:, :],
                                        quad[:, n % 2, c * NT:(c + 1) * NT], start=n % 3 == 0, stop=n % 3 == 2)
                    ins.then_inc(sem["summed"], 1)

                def output(b):
                    pe.wait_ge(sem["normed"], 2 * b + 2)
                    for n in range(PAIRS):
                        ins = pe.matmul(k.banks[0:S, 6, 0:D], att[:, n // 4, (n % 4) * S:(n % 4 + 1) * S],
                                        k.wvo[:, n, :], start=n == 0, stop=n == PAIRS - 1)
                    ins.then_inc(sem["aux"], 1)

                def batch(b):
                    first, last = (isinstance(b, int) and b == e for e in (0, B - 1))
                    plan, base = body_of(b)
                    for s in range(STEPS):
                        if s + 1 < STEPS:
                            scores(b, s + 1)
                        elif not last:
                            scores(b + 1, 0)
                        for _, kind, n, _, need in plan[s]:
                            pe.wait_ge(sem["aux_used"], base + need)
                            if kind == "top":
                                top_task(b + 1, n)
                            elif kind == "turn":
                                turn_tops(b + 2)
                            else:
                                output(b - 1)
                        weigh(b, s)
                        if s % 4 == 2:
                            if s > 2:
                                total(b, s // 4 - 1)
                            elif not first:
                                total(b - 1, QUADS - 1)

                for n in range(TASKS):
                    if n >= 2:
                        pe.wait_ge(sem["aux_used"], n - 1)
                    top_task(0, n)
                turn_tops(1)
                scores(0, 0)
                batches(pe, batch)
                total(B - 1, QUADS - 1)
                pe.wait_ge(sem["aux_used"], end)
                output(B - 1)

            @block.scalar
            def _(act):
                act.sem_inc(sem["exped"], 2)
                act.wait_ge(sem["cleared"], 1)
                with act.Fori(0, B) as b:
                    for s in range(STEPS):
                        m = P if s % LT < LT - 1 else L_LAST
                        act.wait_ge(sem["scored"], STEPS * b + s + 1)
                        act.wait_ge(sem["weighted"], STEPS * b + s + 1)
                        act.wait_ge(sem["paired"], STEPS // 2 * b + s // 2 + 1)
                        act.activation(weights_of(s)[0:m, :].rearrange("p (c n) -> p c n", c=2),
                                       k.banks[0:m, 2 * (s % 2):2 * (s % 2) + 2, 0:NT], ACT.Exp).then_inc(sem["exped"], 1)

            @block.vector
            def _(dve):
                dve.memset(pr_last[:, :], 0.0).then_inc(sem["cleared"], 1)

                def top_task(base, place, n):
                    t = n // len(MAX_CHUNKS)
                    cols = MAX_CHUNKS[n % len(MAX_CHUNKS)][1]
                    dve.wait_ge(sem["aux"], base + place + 1)
                    dve.tensor_reduce(top3[:, t, n % len(MAX_CHUNKS):n % len(MAX_CHUNKS) + 1],
                                      k.banks[:, 6 + n % 2, 0:cols], X, ALU.max).then_inc(sem["aux_used"], 1)
                    if n == TASKS - 1:
                        dve.wait_ge(sem["aux_used"], base + place + 1)
                        dve.tensor_reduce(top[:, :], top3[:, :, :], X, ALU.max).then_inc(sem["topped"], 1)

                def make_shift(base, place, b):
                    dve.wait_ge(sem["aux"], base + place + 1)
                    if not (isinstance(b, int) and b == 0):
                        dve.wait_ge(sem["shift_in"], 32 * b)
                    got = k.banks[0:QT, 7, 0:P]
                    dve.tensor_scalar(shift[:, 0, :], got, -1.0, None, ALU.mult).then_inc(sem["shift_high"], 1)
                    dve.wait_ge(sem["shift_high"], b + 1)
                    dve.scalar_tensor_tensor(shift[:, 1, :], got, -1.0, shift[:, 0, :], ALU.mult, ALU.subtract)\
                       .then_inc(sem["shifted"], 1)
                    dve.wait_ge(sem["shifted"], b + 1)
                    dve.sem_inc(sem["aux_used"], 1)

                def empty(u, half):
                    dve.wait_ge(sem["weighted"], SLOTS + LT * (u + 1))
                    dve.tensor_copy(raw[:, half, :], k.banks[:, 4, 0:NT]).then_inc(sem["raw"], 1)

                def add_pairs(b, n):
                    dve.wait_ge(sem["paired"], 2 + STEPS // 2 * b + 2 * n + 2)
                    if n >= 2 or not (isinstance(b, int) and b == 0):
                        dve.wait_ge(sem["summed"], QUADS * b + n - 1)
                    dve.tensor_tensor(quad[:, n % 2, :], pair[:, 0, :], pair[:, 1, :], ALU.add).then_inc(sem["quaded"], 1)

                def normalize(u, half):
                    dve.wait_ge(sem["summed"], 3 * (u + 1))
                    dve.reciprocal(rden[:, :], k.banks[:, 5, 0:NT]).then_inc(sem["recip"], 1)
                    dve.wait_ge(sem["recip"], u + 1)
                    dve.tensor_tensor(att[:, half, :], raw[:, half, :], rden[:, :], ALU.mult).then_inc(sem["normed"], 1)

                def add_output(base, place, b):
                    dve.wait_ge(sem["aux"], base + place + 1)
                    dve.tensor_tensor(k.x[:, b, :], k.x[:, b, :], k.banks[0:S, 6, 0:D], ALU.add)\
                       .then_inc(sem["aux_used"], 1)

                def batch(b):
                    first = isinstance(b, int) and b == 0
                    plan, base = body_of(b)
                    for s in range(STEPS):
                        if s == 0 and not first:
                            empty(2 * b - 1, 1)
                        if s == LT:
                            empty(2 * b, 0)
                        for place, kind, n, _, _ in plan[s]:
                            if kind == "top":
                                top_task(base, place, n)
                            elif kind == "turn":
                                make_shift(base, place, b + 1)
                            else:
                                add_output(base, place, b - 1)
                        if s % 4 == 1:
                            if s > 1:
                                add_pairs(b, s // 4 - 1)
                            elif not first:
                                add_pairs(b - 1, QUADS - 1)
                        if s == 3 and not first:
                            normalize(2 * b - 1, 1)
                        if s == LT + 3:
                            normalize(2 * b, 0)

                for n in range(TASKS):
                    top_task(0, n, n)
                make_shift(0, TASKS, 0)
                batches(dve, batch)
                empty(2 * B - 1, 1)
                add_pairs(B - 1, QUADS - 1)
                normalize(2 * B - 1, 1)
                add_output(end, 0, B - 1)
    k.clear("cross")


def router(k, name, experts, kind, top, loads_after):
    nc, a, E = k.nc, k.a, experts
    with ExitStack() as ctx:
        def sb(nm, shape, dt=F32):
            return ctx.enter_context(nc.sbuf_tensor(f"{name}_{nm}", shape, dt))

        wr = sb("wr", [P, DC, E])
        lower = sb("lower", [S, E, E])
        score, ex = sb("score", [S, B, E]), sb("ex", [S, B, E])
        gt, eq = sb("gt", [S, B, E, E]), sb("eq", [S, B, E, E])
        rank, gate = sb("rank", [S, B, E]), sb("gate", [S, B, E])
        best, total = sb("best", [S, B]), sb("total", [S, B])
        high = sb("high", [S, B, E], F16)
        parts = sb("parts", [S, B, 2 * E])
        s = k.sems("router", ("loaded", "scored", "step", "less", "exped", "split", "turned"))

        def over_last(v):
            return v[:, :].unsqueeze(2).broadcast_to((S, B, E))

        def loads(sp):
            sp.dma_start(wr[:, :, :], a[f"{name}_wr"]).then_inc(s["loaded"], 16)
            sp.dma_start(lower[:, :, :], a[f"lower{E}"]).then_inc(s["loaded"], 16)
            loads_after(sp)
        layer_norm(k, loads)

        with nc.Block() as block:
            @block.tensor
            def _(pe):
                pe.wait_ge(s["loaded"], 32)
                for b in range(B):
                    for c in range(DC):
                        ins = pe.matmul(k.banks[0:S, 0, b * E:(b + 1) * E], k.xnT[:, c, b * S:(b + 1) * S], wr[:, c, :],
                                        start=c == 0, stop=c == DC - 1)
                ins.then_inc(s["scored"], 1)
                pe.wait_ge(s["split"], 1)
                for b in range(B):
                    ins = pe.transpose(k.banks[0:2 * E, 1 + b // 4, (b % 4) * S:(b % 4 + 1) * S], parts[:, b, :],
                                       k.ident[0:S, 0:S])
                ins.then_inc(s["turned"], 1)

            @block.scalar
            def _(act):
                if kind != "choice":
                    act.wait_ge(s["less"], 1)
                    act.activation(ex[:, :, :], ex[:, :, :], ACT.Exp).then_inc(s["exped"], 1)
                act.wait_ge(s["turned"], 1)
                act.copy(k.gates[0:2 * E, :].rearrange("e (g t) -> e g t", g=2), k.banks[0:2 * E, 1:3, 0:NT])

            @block.vector
            def _(dve):
                steps = Steps(dve, s["step"])

                def choose(v):
                    own, others = v.unsqueeze(3).broadcast_to((S, B, E, E)), v.unsqueeze(2).broadcast_to((S, B, E, E))
                    steps.link(dve.tensor_tensor(gt[:, :, :, :], others, own, ALU.is_gt))
                    steps.link(dve.tensor_tensor(eq[:, :, :, :], others, own, ALU.is_equal))
                    steps.link(dve.tensor_tensor(eq[:, :, :, :], eq[:, :, :, :],
                                                 lower[:, :, :].unsqueeze(1).broadcast_to((S, B, E, E)), ALU.mult))
                    steps.link(dve.tensor_tensor(gt[:, :, :, :], gt[:, :, :, :], eq[:, :, :, :], ALU.add))
                    steps.link(dve.tensor_reduce(rank[:, :, :], gt[:, :, :, :], X, ALU.add))
                    steps.link(dve.tensor_scalar(rank[:, :, :], rank[:, :, :], float(top), None, ALU.is_lt))

                dve.wait_ge(s["loaded"], 32)
                dve.wait_ge(s["scored"], 1)
                steps.link(dve.tensor_copy(score[:, :, :].rearrange("s b e -> s (b e)"), k.banks[0:S, 0, 0:B * E]))
                if kind != "choice":
                    steps.link(dve.tensor_reduce(best[:, :], score[:, :, :], X, ALU.max))
                    dve.tensor_tensor(ex[:, :, :], score[:, :, :], over_last(best), ALU.subtract).then_inc(s["less"], 1)
                    dve.wait_ge(s["exped"], 1)
                if kind == "softmax_first":
                    steps.link(dve.tensor_reduce(total[:, :], ex[:, :, :], X, ALU.add))
                    steps.link(dve.reciprocal(total[:, :], total[:, :]))
                    steps.link(dve.tensor_tensor(score[:, :, :], ex[:, :, :], over_last(total), ALU.mult))
                choose(score[:, :, :])
                if kind == "choice":
                    steps.link(dve.tensor_copy(gate[:, :, :], rank[:, :, :]))
                elif kind == "softmax_first":
                    steps.link(dve.tensor_tensor(gate[:, :, :], score[:, :, :], rank[:, :, :], ALU.mult))
                else:
                    steps.link(dve.tensor_tensor(ex[:, :, :], ex[:, :, :], rank[:, :, :], ALU.mult))
                    steps.link(dve.tensor_reduce(total[:, :], ex[:, :, :], X, ALU.add))
                    steps.link(dve.reciprocal(total[:, :], total[:, :]))
                    steps.link(dve.tensor_tensor(gate[:, :, :], ex[:, :, :], over_last(total), ALU.mult))
                steps.link(dve.tensor_copy(high[:, :, :], gate[:, :, :]))
                dve.tensor_copy(parts[:, :, 0:E], high[:, :, :])
                dve.tensor_tensor(parts[:, :, E:2 * E], gate[:, :, :], high[:, :, :], ALU.subtract).then_inc(s["split"], 1)
    k.clear("router")


class FeedForward:

    def __init__(self, k, ctx, name, tiles, down, experts=0, scales=False):
        def sb(nm, shape, dt=F32):
            return ctx.enter_context(k.nc.sbuf_tensor(f"{name}_{nm}", shape, dt))

        self.k, self.name, self.tiles, self.down, self.experts, self.scales = k, name, tiles, down, experts, scales
        self.gu = sb("gu", [P, 2, 2 * D])
        self.dn = sb("dn", [P, 2, D])
        self.act_g = sb("act_g", [P, 2, NT])
        self.prod = sb("prod", [P, 2, NT])
        self.hid = sb("hid", [P, 2, NT])
        self.yT = sb("yT", [P, DC, T])
        if experts:
            self.expert_of = sb("expert_of", [P, tiles * P], F16)
        if scales:
            self.sc_g, self.sc_u, self.sc_d = sb("sc_g", [P, tiles]), sb("sc_u", [P, tiles]), sb("sc_d", [P, DC])
        self.s = k.sems("ffn", ("gu0", "gu1", "dn0", "dn1", "extra", "gate", "up", "spread", "silu", "prod", "hid",
                                "down", "out", "turned", "added"))

    def load(self, sp, m, j, again):
        s, a = self.s, self.k.a
        if again:
            sp.wait_ge(s["up"], 2 * m - 2)
        sp.dma_start(self.gu[:, j, :], a[f"{self.name}_gu"][m]).then_inc(s[f"gu{j}"], 16)
        if again:
            sp.wait_ge(s["down"], 2 * m - 2)
        sp.dma_start(self.dn[:, j, :], self.down[m]).then_inc(s[f"dn{j}"], 16)

    def first_loads(self, sp):
        s, a, name = self.s, self.k.a, self.name
        self.load(sp, 0, 0, False)
        if self.experts:
            sp.dma_start(self.expert_of[:, :], a[f"{name}_expert_of"]).then_inc(s["extra"], 16)
        if self.scales:
            for dst, nm in ((self.sc_g, "sc_g"), (self.sc_u, "sc_u"), (self.sc_d, "sc_d")):
                sp.dma_start(dst[:, :], a[f"{name}_{nm}"]).then_inc(s["extra"], 16)
        self.load(sp, 1, 1, False)


def feed_forward(f, src):
    k, nc, s, tiles, experts, scales = f.k, f.k.nc, f.s, f.tiles, f.experts, f.scales
    gu, dn, act_g, prod, hid, yT = f.gu, f.dn, f.act_g, f.prod, f.hid, f.yT
    full = (tiles - 1) // 2
    with nc.Block() as block:
        @block.sync
        def _(sp):
            with sp.Fori(1, tiles // 2) as i:
                f.load(sp, 2 * i, 0, True)
                f.load(sp, 2 * i + 1, 1, True)
            if tiles % 2:
                f.load(sp, tiles - 1, 0, True)

        @block.tensor
        def _(pe):
            if experts:
                pe.wait_ge(s["extra"], 16)

            def rise(i, j, n, first):
                t = 2 * (2 * i + j) + n
                if n == 0:
                    pe.wait_ge(s[f"gu{j}"], 16 * i + 16)
                if first < 2:
                    pe.wait_ge(s["silu"], t - 1)
                for c in range(DC):
                    ins = pe.matmul(k.banks[:, 7 if n else 4, 0:NT], gu[:, j, c * P:(c + 1) * P],
                                    src[:, c, n * NT:(n + 1) * NT], start=c == 0, stop=c == DC - 1)
                ins.then_inc(s["gate"], 1)
                if first < 1 or n:
                    pe.wait_ge(s["prod"], t)
                for c in range(DC):
                    ins = pe.matmul(k.banks[:, 5, 0:NT], gu[:, j, D + c * P:D + (c + 1) * P],
                                    src[:, c, n * NT:(n + 1) * NT], start=c == 0, stop=c == DC - 1)
                ins.then_inc(s["up"], 1)
                if experts:
                    if first < 1 or n:
                        pe.wait_ge(s["hid"], t)
                    pe.matmul(k.banks[:, 6, 0:NT], f.expert_of[:, bass.ds((2 * i + j) * P, P)],
                              k.gates[:, n * NT:(n + 1) * NT], start=True, stop=True)\
                      .then_inc(s["spread"], 1)

            def fall(i, j, n, first, last):
                t = 2 * (2 * i + j) + n
                if n == 0:
                    pe.wait_ge(s[f"dn{j}"], 16 * i + 16)
                pe.wait_ge(s["hid"], t + 1)
                for c in range(DC):
                    ins = pe.matmul(k.banks[:, 2 * c + n, 0:NT], dn[:, j, c * P:(c + 1) * P], hid[:, n, :],
                                    start=first, stop=last)
                ins.then_inc(s["down"], 1)

            def tile(i, j, first, last):
                ni, nj = (i, 1) if j == 0 else (i + 1, 0)
                rise(i, j, 1, 2 if first else 0)
                fall(i, j, 0, first, last)
                if not last:
                    rise(ni, nj, 0, 0)
                fall(i, j, 1, first, last)
            rise(0, 0, 0, 2)
            tile(0, 0, True, False)
            tile(0, 1, False, False)
            with pe.Fori(1, full) as i:
                tile(i, 0, False, False)
                tile(i, 1, False, False)
            if tiles % 2 == 0:
                tile(full, 0, False, False)
                tile(full, 1, False, True)
            else:
                tile(full, 0, False, True)
            pe.wait_ge(s["out"], 4)
            for b in range(B):
                if b >= 4:
                    pe.wait_ge(s["added"], b - 3)
                for c in range(DC):
                    ins = pe.transpose(k.banks[0:S, 4 + b % 4, c * P:(c + 1) * P], yT[:, c, b * S:(b + 1) * S],
                                       k.ident[:, :])
                ins.then_inc(s["turned"], 1)

        @block.scalar
        def _(act):
            if scales:
                act.wait_ge(s["extra"], 48)

            def unit(m, n, again):
                t = 2 * m + n
                act.wait_ge(s["gate"], t + 1)
                if again:
                    act.wait_ge(s["prod"], t - 1)
                how = {"scale": f.sc_g[:, m:m + 1]} if scales else {}
                act.activation(act_g[:, n, :], k.banks[:, 7 if n else 4, 0:NT], ACT.Silu, **how).then_inc(s["silu"], 1)
            unit(0, 0, False)
            unit(0, 1, False)
            if scales:
                for m in range(1, tiles):
                    unit(m, 0, True)
                    unit(m, 1, True)
            else:
                with act.Fori(1, tiles) as m:
                    unit(m, 0, True)
                    unit(m, 1, True)
            act.wait_ge(s["down"], 2 * tiles)
            for c in range(DC):
                for n in range(2):
                    dst, got = yT[:, c, n * NT:(n + 1) * NT], k.banks[:, 2 * c + n, 0:NT]
                    if scales:
                        act.activation(dst, got, ACT.Copy, scale=f.sc_d[:, c:c + 1]).then_inc(s["out"], 1)
                    else:
                        act.copy(dst, got).then_inc(s["out"], 1)

        @block.vector
        def _(dve):
            if scales:
                dve.wait_ge(s["extra"], 48)

            def unit(m, n, again):
                t = 2 * m + n
                dve.wait_ge(s["silu"], t + 1)
                dve.wait_ge(s["up"], t + 1)
                if again:
                    dve.wait_ge(s["down"], t - 1)
                if scales:
                    dve.scalar_tensor_tensor(hid[:, n, :], k.banks[:, 5, 0:NT], f.sc_u[:, bass.ds(m, 1)], act_g[:, n, :],
                                             ALU.mult, ALU.mult).then_inc(s["prod"], 1)
                    dve.wait_ge(s["prod"], t + 1)
                    dve.sem_inc(s["hid"], 1)
                    return
                dve.tensor_tensor(prod[:, n, :], act_g[:, n, :], k.banks[:, 5, 0:NT], ALU.mult).then_inc(s["prod"], 1)
                dve.wait_ge(s["prod"], t + 1)
                dve.wait_ge(s["spread"], t + 1)
                dve.tensor_tensor(hid[:, n, :], prod[:, n, :], k.banks[:, 6, 0:NT], ALU.mult).then_inc(s["hid"], 1)
            unit(0, 0, False)
            unit(0, 1, False)
            with dve.Fori(1, tiles) as m:
                unit(m, 0, True)
                unit(m, 1, True)
            for b in range(B):
                dve.wait_ge(s["turned"], b + 1)
                dve.tensor_tensor(k.x[:, b, :], k.x[:, b, :], k.banks[0:S, 4 + b % 4, 0:D], ALU.add)\
                   .then_inc(s["added"], 1)
    k.clear("ffn")


FFN_TILES = 8


def hadamard_weights(k, name, down):
    nc, a, M = k.nc, k.a, FFN_TILES
    with ExitStack() as ctx:
        wd = ctx.enter_context(nc.sbuf_tensor(f"{name}_wd", [P, M, D], F32))
        z = [ctx.enter_context(nc.sbuf_tensor(f"{name}_z{j}", [P, M, D], F32)) for j in range(2)]
        h128 = ctx.enter_context(nc.sbuf_tensor(f"{name}_h128", [P, P], F32))
        su = ctx.enter_context(nc.sbuf_tensor(f"{name}_su", [P, M], F32))
        s = k.sems("hadamard", ("loaded", "turned", "copied", "step", "stored"))
        with nc.Block() as block:
            @block.sync
            def _(sp):
                sp.dma_start(wd[:, :, :], a[f"{name}_wd"]).then_inc(s["loaded"], 16)
                sp.dma_start(h128[:, :], a["h256"][0:P, 0:P]).then_inc(s["loaded"], 16)
                sp.dma_start(su[:, :], a[f"{name}_su_dp"]).then_inc(s["loaded"], 16)
                sp.wait_ge(s["step"], 6 + M)
                sp.dma_start(down.rearrange("m p d -> p m d"), z[0][:, :, :]).then_inc(s["stored"], 16)
                sp.wait_ge(s["stored"], 16)

            @block.tensor
            def _(pe):
                pe.wait_ge(s["loaded"], 48)
                for m in range(M):
                    pe.matmul(k.banks[:, m, 0:D], h128[:, :], wd[:, m, :], start=True, stop=True).then_inc(s["turned"], 1)

            @block.scalar
            def _(act):
                for m in range(M):
                    act.wait_ge(s["turned"], m + 1)
                    act.copy(z[0][:, m, :], k.banks[:, m, 0:D]).then_inc(s["copied"], 1)

            @block.vector
            def _(dve):
                dve.wait_ge(s["copied"], M)
                steps = Steps(dve, s["step"])
                for level in range(3):
                    src, dst = (t[:, :, :].rearrange("p (a two b) d -> p a two (b d)", two=2, b=1 << level)
                                for t in (z[level % 2], z[(level + 1) % 2]))
                    steps.link(dve.tensor_tensor(dst[:, :, 0], src[:, :, 0], src[:, :, 1], ALU.add))
                    steps.link(dve.tensor_tensor(dst[:, :, 1], src[:, :, 0], src[:, :, 1], ALU.subtract))
                for m in range(M):
                    steps.link(dve.tensor_scalar(z[0][:, m, :], z[1][:, m, :], su[:, m:m + 1], 1.0 / 32, ALU.mult, ALU.mult))


def hadamard_inputs(k, name, xh, loads_after):
    nc, a = k.nc, k.a
    with ExitStack() as ctx:
        h256 = ctx.enter_context(nc.sbuf_tensor(f"{name}_h256", [P, DC, D], F32))
        su = ctx.enter_context(nc.sbuf_tensor(f"{name}_su_in", [P, DC], F32))
        signed = ctx.enter_context(nc.sbuf_tensor(f"{name}_signed", [P, DC, T], F32))
        s = k.sems("inputs", ("loaded", "turned", "step"))

        def loads(sp):
            sp.dma_start(h256[:, :, :], a["h256"].rearrange("(c p) n -> p c n", p=P)).then_inc(s["loaded"], 16)
            sp.dma_start(su[:, :], a[f"{name}_su_ug"]).then_inc(s["loaded"], 16)
            loads_after(sp)
        layer_norm(k, loads)

        with nc.Block() as block:
            @block.vector
            def _(dve):
                dve.wait_ge(s["loaded"], 32)
                for c in range(DC):
                    dve.tensor_scalar(signed[:, c, :], k.xnT[:, c, :], su[:, c:c + 1], None, ALU.mult).then_inc(s["step"], 1)

            @block.tensor
            def _(pe):
                pe.wait_ge(s["loaded"], 32)
                pe.wait_ge(s["step"], DC)
                for c in range(DC):
                    for n in range(2):
                        for d in range(DC):
                            ins = pe.matmul(k.banks[:, 2 * c + n, 0:NT], h256[:, d, c * P:(c + 1) * P],
                                            signed[:, d, n * NT:(n + 1) * NT], start=d == 0, stop=d == DC - 1)
                        ins.then_inc(s["turned"], 1)

            @block.scalar
            def _(act):
                for c in range(DC):
                    for n in range(2):
                        act.wait_ge(s["turned"], 2 * c + n + 1)
                        act.activation(xh[:, c, n * NT:(n + 1) * NT], k.banks[:, 2 * c + n, 0:NT], ACT.Copy, scale=1.0 / 16)


FE = 8
HKV = H // 2
QK = H + HKV
MAGIC = 1.5 * 2.0 ** 23
INV_2PI = 0.15915494309189535


def feature_attention(k, name):
    nc, a = k.nc, k.a
    scratch = nc.dram_tensor(f"{name}_scratch", (B, S * D), F32).ap()
    with ExitStack() as ctx:
        def sb(nm, shape, dt=F32):
            return ctx.enter_context(nc.sbuf_tensor(f"{name}_{nm}", shape, dt))

        W = (QK + HKV) * HD
        half = HD // 2
        w = sb("w", [P, DC, W])
        bias = sb("bias", [S, W])
        wo, bo = sb("wo", [P, DC, D]), sb("bo", [S, D])
        rb = sb("rb", [P, HKV * FE])
        cos, sin = sb("cos", [S, HD]), sb("sin", [S, HD])
        qk = sb("qk", [S, B, QK, HD])
        v = sb("v", [S, B, HKV * HD])
        c_part, s_part = sb("c_part", [S, QK, HD]), sb("s_part", [S, QK, HD])
        norm = sb("norm", [S, B, QK])
        qkT = sb("qkT", [P, 2, 3, S])
        ph = sb("ph", [S, B, QK, 2 * FE])
        rnd = sb("rnd", [S, B, QK, 2 * FE])
        m1, m2 = sb("m1", [S, 2, H * HKV, 2 * FE]), sb("m2", [S, H * HD, HKV])
        dots = sb("dots", [S, 2, H, HKV])
        o = sb("o", [S, 2, H, HD])
        otok = sb("otok", [S, B, D])
        oT = sb("oT", [P, 2, DC, S])
        s = k.sems("feature", ("loaded", "proj", "biased", "step", "normed", "root", "unit", "turned", "copied", "angled",
                               "angles", "taken", "wrapped", "feat", "prod", "dot", "dotted", "summed", "stored0", "stored1", "back",
                               "oturned", "ocopied", "out", "added"))
        def loads(sp):
            for dst, nm in ((w, "w"), (wo, "wo")):
                sp.dma_start(dst[:, :, :], a[f"{name}_{nm}"]).then_inc(s["loaded"], 16)
            for dst, nm in ((rb, "rb"), (cos, "cos"), (sin, "sin")):
                sp.dma_start(dst[:, :], a[f"{name}_{nm}"]).then_inc(s["loaded"], 16)
            for dst, nm in ((bias, "bias"), (bo, "bo")):
                sp.dma_start(dst[:, :], a[f"{name}_{nm}"].partition_broadcast(S)).then_inc(s["loaded"], 16)
        layer_norm(k, loads)

        with nc.Block() as block:
            @block.sync
            def _(sp):
                for b in range(B):
                    sp.wait_ge(s["summed"], b + 1)
                    sp.dma_start(scratch[b].rearrange("(h s d) -> s h d", h=H, s=S), o[:, b % 2])\
                      .then_inc(s[f"stored{b % 2}"], 16)
                for j in range(2):
                    sp.wait_ge(s[f"stored{j}"], 16 * B // 2)
                sp.dma_start(otok[:, :, :], scratch.rearrange("b (r c) -> r b c", c=D)).then_inc(s["back"], 16)

            @block.tensor
            def _(pe):
                pe.wait_ge(s["loaded"], 16 * 7)
                for b in range(B):
                    if b >= 4:
                        pe.wait_ge(s["biased"], b - 3)
                    for c in range(DC):
                        ins = pe.matmul(k.banks[0:S, b % 4, 0:W], k.xnT[:, c, b * S:(b + 1) * S], w[:, c, :],
                                        start=c == 0, stop=c == DC - 1)
                    ins.then_inc(s["proj"], 1)
                for b in range(B):
                    pe.wait_ge(s["unit"], b + 1)
                    if b >= 2:
                        pe.wait_ge(s["copied"], b - 1)
                    for g in range(3):
                        ins = pe.transpose(k.banks[:, 4 + b % 2, g * S:(g + 1) * S],
                                           qk[:, b, 8 * g:8 * g + 8, :].rearrange("s h d -> s (h d)"), k.ident[0:S, 0:S])
                    ins.then_inc(s["turned"], 1)
                    pe.wait_ge(s["copied"], b + 1)
                    if b >= 2:
                        pe.wait_ge(s["taken"], b - 1)
                    for g in range(3):
                        ins = pe.matmul(k.banks[0:S, 6 + b % 2, g * 64:(g + 1) * 64], qkT[:, b % 2, g, :], rb[:, :],
                                        start=True, stop=True)
                    ins.then_inc(s["angled"], 1)
                pe.wait_ge(s["back"], 16)
                for b in range(B):
                    if b >= 2:
                        pe.wait_ge(s["ocopied"], b - 1)
                    for c in range(DC):
                        ins = pe.transpose(k.banks[:, b % 2, c * S:(c + 1) * S], otok[:, b, c * P:(c + 1) * P],
                                           k.ident[0:S, 0:S])
                    ins.then_inc(s["oturned"], 1)
                    pe.wait_ge(s["ocopied"], b + 1)
                    if b >= 2:
                        pe.wait_ge(s["added"], b - 1)
                    for c in range(DC):
                        ins = pe.matmul(k.banks[0:S, 2 + b % 2, 0:D], oT[:, b % 2, c, :], wo[:, c, :],
                                        start=c == 0, stop=c == DC - 1)
                    ins.then_inc(s["out"], 1)

            @block.scalar
            def _(act):
                act.wait_ge(s["normed"], 1)
                act.activation(norm[:, :, :], norm[:, :, :], ACT.Sqrt).then_inc(s["root"], 1)
                for b in range(B):
                    act.wait_ge(s["turned"], b + 1)
                    if b >= 2:
                        act.wait_ge(s["angled"], b - 1)
                    act.copy(qkT[:, b % 2], k.banks[:, 4 + b % 2, 0:3 * S].rearrange("p (g s) -> p g s", g=3))\
                       .then_inc(s["copied"], 1)
                act.wait_ge(s["wrapped"], 1)
                act.activation(ph[:, :, :, :], ph[:, :, :, :], ACT.Sin, scale=6.283185).then_inc(s["feat"], 1)
                for b in range(B):
                    act.wait_ge(s["oturned"], b + 1)
                    if b >= 2:
                        act.wait_ge(s["out"], b - 1)
                    act.copy(oT[:, b % 2], k.banks[:, b % 2, 0:DC * S].rearrange("p (g s) -> p g s", g=DC))\
                       .then_inc(s["ocopied"], 1)

            @block.gpsimd
            def _(pool):
                pool.wait_ge(s["feat"], 1)
                for b in range(B):
                    if b >= 2:
                        pool.wait_ge(s["dot"], b - 1)
                    pool.tensor_tensor(m1[:, b % 2].rearrange("s (h g) f -> s h g f", h=H),
                                       ph[:, b, 0:H, :].unsqueeze(2).broadcast_to((S, H, HKV, 2 * FE)),
                                       ph[:, b, H:QK, :].unsqueeze(1).broadcast_to((S, H, HKV, 2 * FE)), ALU.mult)\
                        .then_inc(s["prod"], 1)

            @block.vector
            def _(dve):
                steps = Steps(dve, s["step"])
                dve.wait_ge(s["loaded"], 16 * 7)
                steps.link(dve.tensor_tensor(k.x[:, :, :], k.x[:, :, :], bo[:, :].unsqueeze(1).broadcast_to((S, B, D)), ALU.add))
                for b in range(B):
                    dve.wait_ge(s["proj"], b + 1)
                    dve.tensor_tensor(qk[:, b, :, :].rearrange("s h d -> s (h d)"), k.banks[0:S, b % 4, 0:QK * HD],
                                      bias[:, 0:QK * HD], ALU.add)
                    dve.tensor_tensor(v[:, b, :], k.banks[0:S, b % 4, QK * HD:W], bias[:, QK * HD:W], ALU.add)\
                       .then_inc(s["biased"], 1)
                    dve.wait_ge(s["biased"], b + 1)
                    def wide(t, at):
                        return t[:, at].unsqueeze(1).broadcast_to((S, QK, at.stop - at.start))
                    dve.tensor_tensor(c_part[:, :, :], qk[:, b], wide(cos, slice(0, HD)), ALU.mult)
                    dve.tensor_tensor(s_part[:, :, 0:half], qk[:, b, :, half:], wide(sin, slice(0, half)), ALU.mult)
                    steps.link(dve.tensor_tensor(s_part[:, :, half:], qk[:, b, :, 0:half], wide(sin, slice(half, HD)), ALU.mult))
                    steps.link(dve.tensor_tensor(qk[:, b], c_part[:, :, :], s_part[:, :, :], ALU.add))
                    steps.link(dve.tensor_tensor(c_part[:, :, :], qk[:, b], qk[:, b], ALU.mult))
                    steps.link(dve.tensor_reduce(norm[:, b, :], c_part[:, :, :], X, ALU.add))
                dve.sem_inc(s["normed"], 1)
                steps.link(dve.tensor_scalar(v[:, :, :], v[:, :, :], 1.0 / 8, None, ALU.mult))
                dve.wait_ge(s["root"], 1)
                steps.link(dve.tensor_scalar(norm[:, :, :], norm[:, :, :], 1e-6, None, ALU.max))
                steps.link(dve.reciprocal(norm[:, :, :], norm[:, :, :]))
                for b in range(B):
                    dve.tensor_tensor(qk[:, b], qk[:, b], norm[:, b, :].unsqueeze(2).broadcast_to((S, QK, HD)), ALU.mult)\
                       .then_inc(s["unit"], 1)
                for b in range(B):
                    dve.wait_ge(s["angled"], b + 1)
                    got = k.banks[0:S, 6 + b % 2, 0:QK * FE].rearrange("s (h e) -> s h e", e=FE)
                    dve.tensor_scalar(ph[:, b, :, 0:FE], got, INV_2PI, None, ALU.mult)
                    dve.tensor_scalar(ph[:, b, :, FE:], got, INV_2PI, 0.25, ALU.mult, ALU.add).then_inc(s["taken"], 1)
                dve.wait_ge(s["taken"], B)
                steps.link(dve.tensor_scalar(rnd[:, :, :, :], ph[:, :, :, :], MAGIC, None, ALU.add))
                steps.link(dve.tensor_scalar(rnd[:, :, :, :], rnd[:, :, :, :], MAGIC, None, ALU.subtract))
                dve.tensor_tensor(ph[:, :, :, :], ph[:, :, :, :], rnd[:, :, :, :], ALU.subtract).then_inc(s["wrapped"], 1)
                for b in range(B):
                    dve.wait_ge(s["prod"], b + 1)
                    dve.tensor_reduce(dots[:, b % 2].rearrange("s h g -> s (h g)"), m1[:, b % 2], X, ALU.add)\
                       .then_inc(s["dot"], 1)
                    dve.wait_ge(s["dot"], b + 1)
                    steps.link(dve.tensor_tensor(
                        m2[:, :, :].rearrange("s (h d) g -> s h d g", h=H),
                        dots[:, b % 2].unsqueeze(2).broadcast_to((S, H, HD, HKV)),
                        v[:, b, :].rearrange("s (g d) -> s d g", g=HKV).unsqueeze(1).broadcast_to((S, H, HD, HKV)),
                        ALU.mult))
                    if b >= 2:
                        dve.wait_ge(s[f"stored{b % 2}"], 16 * (b // 2))
                    dve.tensor_reduce(o[:, b % 2].rearrange("s h d -> s (h d)"), m2[:, :, :], X, ALU.add)\
                       .then_inc(s["summed"], 1)
                    dve.wait_ge(s["summed"], b + 1)
                for b in range(B):
                    dve.wait_ge(s["out"], b + 1)
                    dve.tensor_tensor(k.x[:, b, :], k.x[:, b, :], k.banks[0:S, 2 + b % 2, 0:D], ALU.add)\
                       .then_inc(s["added"], 1)


def first_context(k, first):
    nc = k.nc
    with ExitStack() as ctx:
        rows = ctx.enter_context(nc.sbuf_tensor("first_rows", [S, B, DL], F32))
        s = k.sems("first", ("loaded", "turned"))
        with nc.Block() as block:
            @block.sync
            def _(sp):
                sp.dma_start(rows[:, :, :], k.a["ctx"][:, 0:S, :].rearrange("b s d -> s b d")).then_inc(s["loaded"], 16)

            @block.tensor
            def _(pe):
                pe.wait_ge(s["loaded"], 16)
                for b in range(B):
                    pe.transpose(k.banks[0:DL, b // 4, (b % 4) * S:(b % 4 + 1) * S], rows[:, b, :], k.ident[0:S, 0:S])\
                      .then_inc(s["turned"], 1)

            @block.scalar
            def _(act):
                act.wait_ge(s["turned"], B)
                act.copy(first[:, 0, :].rearrange("d (g t) -> d g t", g=2), k.banks[0:DL, 0:2, 0:NT])


def program(nc, args, out, first, stages):
    k = Core()
    k.nc, k.a, k.kinds, k.used = nc, args, {}, []
    with ExitStack() as ctx:
        def sb(nm, shape, dt=F32):
            return ctx.enter_context(nc.sbuf_tensor(nm, shape, dt))

        k.sem = lambda nm: ctx.enter_context(nc.semaphore(nm))
        k.x = sb("x", [S, B, D])
        k.xnT = sb("xnT", [P, DC, T])
        k.ident = sb("ident", [P, P])
        k.ident16 = sb("ident16", [P, P], BF16)
        k.mask16 = sb("mask16", [S, 4 * S], BF16)
        k.ones64 = sb("ones64", [P, 64])
        k.eps = sb("eps", [P, 1])
        k.ln_stats = sb("ln_stats", [S, B, 6])
        k.ln_mv = sb("ln_mv", [S, B, 2])
        k.ln_root = sb("ln_root", [S, B])
        k.ln_rstd = sb("ln_rstd", [S, B])
        k.ln_xn = sb("ln_xn", [S, 2, D])
        k.kv_hl = sb("kv_hl", [2 * DL, B * L + P - L_LAST], F16)
        k.kv_h1 = sb("kv_h1", [DL + 2, B * L + P - L_LAST], F16)
        k.kv_tok = sb("kv_tok", [P, B, LT, DL])
        k.gates = sb("gates", [P, T], F16)
        k.banks = ctx.enter_context(nc.psum_tensor("banks", [P, 8, 512], F32))
        k.head_rows = sb("head_rows", [P, HH])
        k.ln_summed, k.ln_var, k.ln_std = k.sem("ln_summed"), k.sem("ln_var"), k.sem("ln_std")
        k.ln_recip, k.ln_normed = k.sem("ln_recip"), k.sem("ln_normed")
        k.ln_transposed, k.ln_copied = k.sem("ln_transposed"), k.sem("ln_copied")
        k.ln_calls = 0
        stored = k.sem("stored")
        setup(k)
        context(k)

        def cross(name, rope):
            with ExitStack() as inner:
                k.q_hh = inner.enter_context(nc.sbuf_tensor(f"{name}_q_hh", [2 * DL, B, QT * P], F16))
                k.q_l = inner.enter_context(nc.sbuf_tensor(f"{name}_q_l", [DL + 2, B, QT * P], F16))
                k.wvo = inner.enter_context(nc.sbuf_tensor(f"{name}_wvo", [P, PAIRS, D], F32))
                cross_queries(k, name, rope)
                cross_attention(k, name)

        def mixture(name, experts, hidden, kind, top):
            with ExitStack() as inner:
                f = FeedForward(k, inner, name, experts * hidden // P, args[f"{name}_dn"], experts)
                router(k, name, experts, kind, top, f.first_loads)
                feed_forward(f, k.xnT)

        def hadamard(name):
            down = nc.dram_tensor(f"{name}_down", (FFN_TILES, P, D), F32).ap()
            hadamard_weights(k, name, down)
            with ExitStack() as inner:
                xh = inner.enter_context(nc.sbuf_tensor(f"{name}_xh", [P, DC, T], F32))
                f = FeedForward(k, inner, name, FFN_TILES, down, scales=True)
                hadamard_inputs(k, name, xh, f.first_loads)
                feed_forward(f, xh)

        def last_cross(name):
            with nc.sbuf_tensor("first", [DL, 1, T], F32) as first:
                first_context(k, first)
                self_attention(k, name, first, 1, DL, 0.25, False)

        sublayers = [
            lambda: self_attention(k, "L0_attn", k.xnT, DC, P, 0.25, False),
            lambda: cross("L0_xattn", False),
            lambda: mixture("L0_ffn", 8, 512, "choice", 1),
            lambda: self_attention(k, "L1_attn", k.xnT, DC, P, 0.25, True),
            lambda: cross("L1_xattn", True),
            lambda: mixture("L1_ffn", 16, 176, "softmax_first", 6),
            lambda: self_attention(k, "L2_attn", k.xnT, DC, P, 0.25, True),
            lambda: cross("L2_xattn", True),
            lambda: hadamard("L2_ffn"),
            lambda: feature_attention(k, "L3_attn"),
            lambda: last_cross("L3_xattn"),
            lambda: mixture("L3_ffn", 8, 176, "softmax_last", 2),
        ]
        for sublayer in sublayers[first:stages]:
            sublayer()
        with nc.Block() as block:
            @block.sync
            def _(sp):
                sp.dma_start(out, k.x[:, :, :]).then_inc(stored, 16)
                sp.wait_ge(stored, 16)


def attn_layout(put, name, wq, wk, wv, wo, bq=None, bk=None, bv=None, bo=None):
    import numpy as np

    def tiles(w):
        rows = min(P, w.shape[0])
        return np.ascontiguousarray(w.reshape(-1, rows, w.shape[1]).transpose(1, 0, 2))
    for nm, w in (("wq", wq), ("wk", wk), ("wv", wv), ("wo", wo)):
        put(f"{name}_{nm}", tiles(w))
    if bq is not None:
        put(f"{name}_bq", np.ascontiguousarray(bq.reshape(DC, P).T))
        put(f"{name}_bk", np.ascontiguousarray(bk.reshape(DC, P).T))
        put(f"{name}_bv", bv)
        put(f"{name}_bo", bo)


def rope_tables(length, dim):
    import numpy as np
    inv = np.float32(1.0) / np.power(np.float32(10000.0), np.arange(0, dim, 2, dtype=np.float32) / np.float32(dim))
    f = np.arange(length, dtype=np.float32)[:, None] * inv[None, :]
    return np.repeat(np.cos(f), 2, axis=1), np.repeat(np.sin(f), 2, axis=1)


FIRST, STAGES = 0, 12


def kernel(**inputs):
    import ml_dtypes
    import numpy as np
    import concourse.bacc as bacc
    from concourse.bass_utils import run_bass_kernel_spmd

    i = {name: np.asarray(value) for name, value in inputs.items()}
    nc = bacc.Bacc("TRN2", target_bir_lowering=False, num_devices=1)
    arrays, args = {}, {}

    def put(name, value):
        value = np.ascontiguousarray(value)
        arrays[f"in_{name}"] = value
        args[name] = nc.dram_tensor(f"in_{name}", value.shape, mybir.dt.from_np(value.dtype), kind="ExternalInput").ap()

    bf16 = ml_dtypes.bfloat16
    put("ident", np.eye(P, dtype=np.float32))
    put("ident16", np.eye(P, dtype=bf16))
    put("mask16", np.tile(np.triu(np.full((S, S), -1e30, np.float32), 1), (1, 4)).astype(bf16))
    put("head_rows", np.repeat(np.eye(HH, dtype=np.float32), HD, axis=0))

    put("x", i["x"].transpose(1, 0, 2))
    qkv = i["L0_attn_Wqkv"]
    attn_layout(put, "L0_attn", qkv[:, 0:D], qkv[:, D:2 * D], qkv[:, 2 * D:3 * D], i["L0_attn_Wo"])

    put("ctx", i["ctx_512"])
    cos, sin = rope_tables(LT * P, DL)
    half = np.arange(DL) < DL // 2
    put("ctx_cos", cos.reshape(LT, P, DL).transpose(1, 0, 2))
    put("ctx_sin", np.where(half, -sin, sin).reshape(LT, P, DL).transpose(1, 0, 2))
    cos, sin = rope_tables(S, CQ)
    put("q_cos", cos.T.reshape(2, CH, S).transpose(1, 0, 2))
    put("q_sin", np.stack([sin.T[CH:], -sin.T[:CH]], 1))
    for layer in ("L0", "L1", "L2"):
        n = f"{layer}_xattn"
        wo = i[n + "_Wo"].T.reshape(H, HK, D)
        put(n + "_raw", np.concatenate([i[n + "_Wq"].reshape(H, HK, D), i[n + "_w_kc_q"], i[n + "_w_kc_kv"], wo], 2))
        wkr = i[n + "_W_kr"].transpose(0, 2, 1)
        put(n + "_rkr", np.concatenate([i[n + "_W_qr"].transpose(0, 2, 1), wkr, wkr], 2))

    def shared(w, columns):
        return np.repeat(w.reshape(-1, columns, HD), H // columns, axis=-2).reshape(w.shape[:-1] + (D,))
    n = "L1_attn"
    attn_layout(put, n, i[n + "_Wq"], shared(i[n + "_Wk"], 2), shared(i[n + "_Wv"], 2), i[n + "_Wo"],
                i[n + "_bq"], shared(i[n + "_bk"], 2), shared(i[n + "_bv"], 2), i[n + "_bo"])
    n = "L2_attn"
    attn_layout(put, n, i[n + "_wq"].T, i[n + "_wk"].T, i[n + "_wv"].T, i[n + "_wo"].T,
                i[n + "_bq"], i[n + "_bk"], i[n + "_bv"], i[n + "_bo"])
    n = "L3_xattn"
    kv = i[n + "_Wkv_expand"].T
    attn_layout(put, n, i[n + "_Wq"].T, kv[:, 0:D], kv[:, D:], i[n + "_Wout"].T)

    def tiles_of(w):
        return w.reshape(DC, P, -1, P).transpose(2, 1, 0, 3).reshape(-1, P, DC * P)

    def ffn_layout(n, gate, up, down):
        put(n + "_gu", np.concatenate([tiles_of(gate), tiles_of(up)], 2))
        if down is not None:
            put(n + "_dn", down.reshape(-1, P, D))

    def experts_layout(n, experts, hidden, router_w):
        put(n + "_wr", router_w.reshape(DC, P, experts).transpose(1, 0, 2))
        one = np.repeat(np.eye(experts, dtype=np.float16), hidden, axis=1)
        put(n + "_expert_of", np.concatenate([one, one, np.zeros((P - 2 * experts, experts * hidden), np.float16)]))

    for experts in (8, 16):
        put(f"lower{experts}", np.tile(np.tril(np.ones((experts, experts), np.float32), -1), (S, 1, 1)))
    n = "L0_ffn"
    ffn_layout(n, i[n + "_gate_w"].transpose(1, 0, 2).reshape(D, -1), i[n + "_up_w"].transpose(1, 0, 2).reshape(D, -1),
               i[n + "_down_w"].reshape(-1, D))
    experts_layout(n, 8, 512, i[n + "_router_w"])
    n = "L1_ffn"
    ffn_layout(n, i[n + "_w_gate"].reshape(-1, D).T, i[n + "_w_up"].reshape(-1, D).T,
               i[n + "_w_down"].transpose(0, 2, 1).reshape(-1, D))
    experts_layout(n, 16, 176, i[n + "_gate_w"].T)
    n = "L3_ffn"
    ffn_layout(n, i[n + "_W1"].reshape(-1, D).T, i[n + "_W2"].reshape(-1, D).T,
               i[n + "_W3"].transpose(0, 2, 1).reshape(-1, D))
    experts_layout(n, 8, 176, i[n + "_Wg"].T)
    n = "L2_ffn"
    ffn_layout(n, i[n + "_W_gate"].T, i[n + "_W_up"].T, None)
    hidden = FFN_TILES * P
    h = np.ones((1, 1), np.float32)
    while len(h) < D:
        h = np.block([[h, h], [h, -h]])
    put("h256", h)
    put(n + "_wd", i[n + "_W_down"].T.reshape(FFN_TILES, P, D).transpose(1, 0, 2))
    put(n + "_su_dp", i[n + "_SU_dp"].reshape(FFN_TILES, P).T)
    put(n + "_su_ug", i[n + "_SU_ug"].reshape(DC, P).T)
    put(n + "_sc_u", i[n + "_Wscale_ug"][:hidden].reshape(FFN_TILES, P).T)
    put(n + "_sc_g", i[n + "_Wscale_ug"][hidden:].reshape(FFN_TILES, P).T)
    put(n + "_sc_d", i[n + "_Wscale_dp"].reshape(DC, P).T)

    n = "L3_attn"
    w = np.concatenate([i[n + "_Wq"], i[n + "_Wk"], i[n + "_Wv"]], 0).T
    put(n + "_w", w.reshape(DC, P, -1).transpose(1, 0, 2))
    put(n + "_bias", np.concatenate([i[n + "_bq"], i[n + "_bk"], i[n + "_bv"]]))
    put(n + "_wo", i[n + "_Wo"].T.reshape(DC, P, D).transpose(1, 0, 2))
    put(n + "_bo", i[n + "_bo"])
    blocks = np.zeros((HKV, HD, HKV, FE), np.float32)
    for g in range(HKV):
        blocks[g, :, g, :] = i[n + "_rand_matrix"].T
    put(n + "_rb", blocks.reshape(P, HKV * FE))
    inv = np.float32(1.0) / np.power(np.float32(10000.0), np.arange(0, HD, 2, dtype=np.float32) / np.float32(HD))
    f = np.arange(S, dtype=np.float32)[:, None] * np.concatenate([inv, inv])[None, :]
    put(n + "_cos", np.cos(f))
    put(n + "_sin", np.where(np.arange(HD) < HD // 2, -np.sin(f), np.sin(f)))

    out = nc.dram_tensor("out", (S, B, D), F32, kind="ExternalOutput").ap()
    program(nc, args, out, FIRST, STAGES)
    r = run_bass_kernel_spmd(nc, [arrays], core_ids=[0])
    return np.ascontiguousarray(r.results[0]["out"].transpose(1, 0, 2))
```

```python
from contextlib import ExitStack

import concourse.bass as bass
from concourse import mybir

F32 = mybir.dt.float32
F16 = mybir.dt.float16
BF16 = mybir.dt.bfloat16
ALU = mybir.AluOpType
ACT = mybir.ActivationFunctionType
X = mybir.AxisListType.X

B, S, D = 8, 100, 256
T = B * S
P = 128
DC = D // P
NT = 400
H = 16
HD = D // H
HH = H // 2
L, DL = 1444, 64
LT = (L + P - 1) // P
EPS = 1e-5
LN_SLOTS = 4
W_SCALE = 256.0
OUT_SCALE = 1.0 / W_SCALE


class Core:

    def sems(self, kind, names):
        if kind not in self.kinds:
            self.kinds[kind] = {nm: self.sem(f"{kind}_{nm}") for nm in names}
        return self.kinds[kind]

    def clear(self, kind):
        self.used.append(kind)

    def cleared(self, pool):
        for kind in self.used:
            for s in self.kinds[kind].values():
                pool.sem_clear(s)
        self.used = []


class Steps:

    def __init__(self, eng, sem):
        self.eng, self.sem, self.base, self.n = eng, sem, 0, 0

    def link(self, ins):
        self.n += 1
        ins.then_inc(self.sem, 1)
        self.eng.wait_ge(self.sem, self.base + self.n)


def banks_view(k, first, n, rows, cols):
    return k.banks[0:rows, first:first + n, 0:cols]


def setup(k, loads, clear):
    nc = k.nc
    s_load, s_credit = k.sem("setup_loaded"), k.sem("setup_made")
    with nc.Block() as block:
        @block.sync
        def _(sp):
            sp.dma_start(k.x[:, :, :], k.a["x"]).then_inc(s_load, 16)
            sp.dma_start(k.ident[:, :], k.a["ident"]).then_inc(s_load, 16)
            sp.dma_start(k.ident16[:, :], k.a["ident16"]).then_inc(s_load, 16)
            sp.dma_start(k.mask16[:, :], k.a["mask16"]).then_inc(s_load, 16)
            sp.dma_start(k.head_rows[:, :], k.a["head_rows"]).then_inc(s_load, 16)
            loads(sp)
            sp.wait_ge(s_load, 80)

        @block.vector
        def _(dve):
            clear(dve)
            dve.memset(k.ones64[:, :], 1.0).then_inc(s_credit, 1)
            dve.memset(k.eps[:, :], EPS).then_inc(s_credit, 1)
            dve.memset(k.gates[:, :], 0.0).then_inc(s_credit, 1)
            dve.wait_ge(s_credit, 3)

        @block.tensor
        def _(pe):
            pe.sem_inc(k.ln_transposed, LN_SLOTS)
            pe.wait_ge(k.ln_transposed, LN_SLOTS)

        @block.scalar
        def _(act):
            act.sem_inc(k.ln_copied, LN_SLOTS)
            act.wait_ge(k.ln_copied, LN_SLOTS)


def layer_norm(k, loads):
    nc = k.nc
    n = k.ln_calls
    k.ln_calls += 1
    sums, norm, tr, cp = B * n, B * n, LN_SLOTS + B * n, LN_SLOTS + B * n
    with nc.Block() as block:
        @block.sync
        def _(sp):
            loads(sp)

        @block.gpsimd
        def _(pool):
            k.cleared(pool)

        @block.vector
        def _(dve):
            with dve.Fori(0, B) as b:
                dve.bn_stats(k.ln_stats[:, b, :], k.x[:, b, :]).then_inc(k.ln_summed, 1)
            dve.wait_ge(k.ln_summed, sums + B)
            for b in range(B):
                dve.bn_aggr(k.ln_mv[:, b, :], k.ln_stats[:, b, :]).then_inc(k.ln_var, 1)
            dve.wait_ge(k.ln_std, n + 1)
            dve.reciprocal(k.ln_rstd[:, :], k.ln_root[:, :]).then_inc(k.ln_recip, 1)
            dve.wait_ge(k.ln_recip, n + 1)
            with dve.Fori(0, B // LN_SLOTS) as i:
                for j in range(LN_SLOTS):
                    b = LN_SLOTS * i + j
                    dve.wait_ge(k.ln_transposed, tr + b + 1 - LN_SLOTS)
                    dve.tensor_scalar(k.ln_xn[:, j, :], k.x[:, b, :], k.ln_mv[:, b, 0:1], k.ln_rstd[:, bass.ds(b, 1)],
                                      ALU.subtract, ALU.mult).then_inc(k.ln_normed, 1)

        @block.scalar
        def _(act):
            act.activation(k.ln_warm[:, n:n + 1], k.eps[0:S, :], ACT.Sqrt)
            act.wait_ge(k.ln_var, B * (n + 1))
            act.activation(k.ln_root[:, :], k.ln_mv[:, :, 1], ACT.Sqrt, bias=k.eps[0:S, :]).then_inc(k.ln_std, 1)
            with act.Fori(0, B // LN_SLOTS) as i:
                for j in range(LN_SLOTS):
                    b = LN_SLOTS * i + j
                    act.wait_ge(k.ln_transposed, tr + b + 1)
                    act.copy(k.xnT[:, :, bass.ds(b * S, S)],
                             k.banks[:, j, 0:DC * S].rearrange("p (c s) -> p c s", c=DC)).then_inc(k.ln_copied, 1)

        @block.tensor
        def _(pe):
            with pe.Fori(0, B // LN_SLOTS) as i:
                for j in range(LN_SLOTS):
                    b = LN_SLOTS * i + j
                    pe.wait_ge(k.ln_normed, norm + b + 1)
                    pe.wait_ge(k.ln_copied, cp + b + 1 - LN_SLOTS)
                    for c in range(DC):
                        ins = pe.transpose(k.banks[:, j, c * S:(c + 1) * S], k.ln_xn[:, j, c * P:(c + 1) * P],
                                           k.ident[0:S, 0:S])
                    ins.then_inc(k.ln_transposed, 1)


def self_attention(k, name, src, chunks, rows, scale, bias):
    nc, a = k.nc, k.a
    with ExitStack() as ctx:
        def sb(nm, shape, dt=F32):
            return ctx.enter_context(nc.sbuf_tensor(f"{name}_{nm}", shape, dt))

        wq = sb("wq", [P, DC, D])
        wk = sb("wk", [rows, chunks, D])
        wv = sb("wv", [rows, chunks, D])
        wo = sb("wo", [P, DC, D])
        qT = sb("qT", [P, DC, T])
        kT = sb("kT", [P, DC, T])
        v = sb("v", [S, B, H, HD + 1])
        q_st = sb("q_st", [P, 2, S])
        k_st = sb("k_st", [P, 2, HH, S])
        sc = sb("sc", [S, 2, HH, S])
        pr = sb("pr", [S, 2, HH, S])
        prT = sb("prT", [S, 2, HH, S])
        top = sb("top", [S, 2, HH])
        den = sb("den", [S, HH])
        o = sb("o", [S, HH, HD])
        oT = sb("oT", [P, S])
        if bias:
            bq, bk = sb("bq", [P, DC]), sb("bk", [P, DC])
            bv, bo = sb("bv", [S, D]), sb("bo", [S, D])
        sem = k.sems("attn", (
            "wq", "wk", "wv", "wo", "bias", "ones", "proj", "proj_qk", "proj_v", "staged", "scored", "maxed", "less",
            "exped", "transposed", "copied", "o_copied", "pv", "denom", "normed", "yready", "added"))
        qk_jobs = [(dst, w, s_, c, t, n) for dst, w, s_, c in (("q", wq, k.xnT, DC), ("k", wk, src, chunks))
                   for t in range(DC) for n in range(2)]
        nqk = len(qk_jobs)

        def loads(sp):
            sp.dma_start(wq[:, :, :], a[f"{name}_wq"]).then_inc(sem["wq"], 16)
            sp.dma_start(wk[:, :, :], a[f"{name}_wk"]).then_inc(sem["wk"], 16)
            sp.dma_start(wv[:, :, :], a[f"{name}_wv"]).then_inc(sem["wv"], 16)
            sp.dma_start(wo[:, :, :], a[f"{name}_wo"]).then_inc(sem["wo"], 16)
            if bias:
                sp.dma_start(bq[:, :], a[f"{name}_bq"]).then_inc(sem["bias"], 16)
                sp.dma_start(bk[:, :], a[f"{name}_bk"]).then_inc(sem["bias"], 16)
                for dst, nm in ((bv, "bv"), (bo, "bo")):
                    sp.dma_start(dst[:, :], a[f"{name}_{nm}"].partition_broadcast(S)).then_inc(sem["bias"], 16)
        layer_norm(k, loads)

        with nc.Block() as block:
            @block.tensor
            def _(pe):
                pe.wait_ge(sem["wq"], 16)
                for n_job, (_, w, s_, cc, t, n) in enumerate(qk_jobs):
                    if n_job == nqk // 2:
                        pe.wait_ge(sem["wk"], 16)
                    if n_job >= 4:
                        pe.wait_ge(sem["proj_qk"], n_job - 3)
                    for c in range(cc):
                        ins = pe.matmul(k.banks[:, n_job % 4, 0:NT], w[:, c, t * P:(t + 1) * P],
                                        s_[:, c, n * NT:(n + 1) * NT], start=c == 0, stop=c == cc - 1)
                    ins.then_inc(sem["proj"], 1)
                pe.wait_ge(sem["wv"], 16)
                for b in range(B):
                    if b >= 4:
                        pe.wait_ge(sem["proj_v"], b - 3)
                    for c in range(chunks):
                        ins = pe.matmul(k.banks[0:S, 4 + b % 4, 0:D], src[:, c, b * S:(b + 1) * S],
                                        wv[:, c, :], start=c == 0, stop=c == chunks - 1)
                    ins.then_inc(sem["proj"], 1)
                pe.wait_ge(sem["proj_qk"], nqk)
                pe.wait_ge(sem["proj_v"], B)
                pe.wait_ge(sem["wo"], 16)

                def scores(u, half):
                    pe.wait_ge(sem["staged"], u + 1)
                    for g in range(2):
                        bank = k.banks[0:S, 2 * half + g, 0:4 * S]
                        pe.matmul(bank, k.ident16[0:S, 0:S], k.mask16[:, :], start=True, stop=False)
                        ins = pe.matmul(bank, q_st[:, half, :], k_st[:, half, 4 * g:4 * g + 4, :],
                                        start=False, stop=True)
                    ins.then_inc(sem["scored"], 1)

                def turn_o():
                    ins = pe.transpose(k.banks[:, 5, 4 * S:5 * S], o[:, :, :].rearrange("s h d -> s (h d)"),
                                       k.ident[0:S, 0:S])
                    return ins

                def weigh(b, half):
                    for h in range(HH):
                        ins = pe.matmul(k.banks[0:S, 6, h * (HD + 1):(h + 1) * (HD + 1)], prT[:, half, h, :],
                                        v[:, b, HH * half + h, :], start=True, stop=True)
                    ins.then_inc(sem["pv"], 1)

                def project(b, half):
                    pe.wait_ge(sem["o_copied"], 2 * b + half + 1)
                    if half == 0 and (type(b) is not int or b >= 1):
                        pe.wait_ge(sem["added"], b)
                    ins = pe.matmul(k.banks[0:S, 7, 0:D], oT[:, :], wo[:, half, :], start=half == 0, stop=half == 1)
                    ins.then_inc(sem["yready"], 1)

                def step(b, half, last, behind):
                    u = 2 * b + half
                    if not last:
                        scores(u + 1, 1 - half)
                    pe.wait_ge(sem["exped"], u + 1)
                    if behind >= 1:
                        pe.wait_ge(sem["copied"], u)
                    if behind >= 2:
                        pe.wait_ge(sem["normed"], u - 1)
                        turn_o()
                    for h in range(HH):
                        ins = pe.transpose(k.banks[0:S, 4 + h // 4, (h % 4) * S:(h % 4 + 1) * S], pr[:, half, h, :],
                                           k.ident[0:S, 0:S])
                    ins.then_inc(sem["transposed"], 1)
                    if behind >= 1:
                        weigh(b if half else b - 1, 1 - half)
                    if behind >= 2:
                        project(b - 1, half)

                scores(0, 0)
                step(0, 0, False, 0)
                step(0, 1, False, 1)
                step(1, 0, False, 2)
                step(1, 1, False, 2)
                with pe.Fori(2, B - 1) as b:
                    step(b, 0, False, 2)
                    step(b, 1, False, 2)
                step(B - 1, 0, False, 2)
                step(B - 1, 1, True, 2)
                pe.wait_ge(sem["copied"], 2 * B)
                pe.wait_ge(sem["normed"], 2 * B - 1)
                turn_o().then_inc(sem["transposed"], 1)
                weigh(B - 1, 1)
                project(B - 1, 0)
                pe.wait_ge(sem["normed"], 2 * B)
                turn_o().then_inc(sem["transposed"], 1)
                project(B - 1, 1)

            @block.scalar
            def _(act):
                if bias:
                    act.wait_ge(sem["bias"], 64)
                for n_job, (which, _, _, _, t, n) in enumerate(qk_jobs):
                    act.wait_ge(sem["proj"], n_job + 1)
                    dst = (qT if which == "q" else kT)[:, t, n * NT:(n + 1) * NT]
                    if bias:
                        bb = (bq if which == "q" else bk)[:, t:t + 1]
                        act.activation(dst, k.banks[:, n_job % 4, 0:NT], ACT.Identity, bias=bb).then_inc(sem["proj_qk"], 1)
                    else:
                        act.copy(dst, k.banks[:, n_job % 4, 0:NT]).then_inc(sem["proj_qk"], 1)

                def exponentials(u, half):
                    act.wait_ge(sem["less"], u + 1)
                    act.activation(pr[:, half], sc[:, half], ACT.Exp, scale=scale).then_inc(sem["exped"], 1)

                def copy_o(u, free):
                    if free:
                        act.wait_ge(sem["yready"], u)
                    act.copy(oT[:, :], k.banks[:, 5, 4 * S:5 * S]).then_inc(sem["o_copied"], 1)

                def step(u, half, last, behind):
                    act.wait_ge(sem["transposed"], u + 1)
                    if behind >= 2:
                        copy_o(u - 2, behind >= 3)
                        act.wait_ge(sem["pv"], u - 1)
                    act.copy(prT[:, half, :, :].rearrange("s (g h) t -> s g (h t)", g=2),
                             banks_view(k, 4, 2, S, 4 * S)).then_inc(sem["copied"], 1)
                    if not last:
                        exponentials(u + 1, 1 - half)

                exponentials(0, 0)
                for u in range(4):
                    step(u, u % 2, False, u)
                with act.Fori(2, B - 1) as b:
                    step(2 * b, 0, False, 4)
                    step(2 * b + 1, 1, False, 4)
                step(2 * B - 2, 0, False, 4)
                step(2 * B - 1, 1, True, 4)
                for n in range(2):
                    act.wait_ge(sem["transposed"], 2 * B + 1 + n)
                    copy_o(2 * B - 2 + n, True)

            @block.gpsimd
            def _(pool):
                pool.wait_ge(sem["proj_qk"], nqk)
                def stage(b, half):
                    at = bass.ds(b * S, S)
                    pool.tensor_copy(q_st[:, half, :], qT[:, half, at])
                    pool.tensor_tensor(k_st[:, half], kT[:, half, at].unsqueeze(1).broadcast_to((P, HH, S)),
                                       k.head_rows[:, :].unsqueeze(2).broadcast_to((P, HH, S)), ALU.mult)\
                        .then_inc(sem["staged"], 1)
                stage(0, 0)
                stage(0, 1)
                with pool.Fori(1, B) as b:
                    for half in range(2):
                        pool.wait_ge(sem["scored"], 2 * b + half - 1)
                        stage(b, half)

            @block.vector
            def _(dve):
                dve.memset(v[:, :, :, HD:HD + 1], 1.0).then_inc(sem["ones"], 1)
                if bias:
                    dve.wait_ge(sem["bias"], 64)
                    dve.tensor_tensor(k.x[:, :, :], k.x[:, :, :],
                                      bo[:, :].unsqueeze(1).broadcast_to((S, B, D)), ALU.add).then_inc(sem["ones"], 1)
                for b in range(B):
                    dve.wait_ge(sem["proj"], nqk + b + 1)
                    dst, got = v[:, b, :, 0:HD], k.banks[0:S, 4 + b % 4, 0:D].rearrange("s (h d) -> s h d", h=H)
                    if bias:
                        dve.tensor_tensor(dst, got, bv[:, :].rearrange("s (h d) -> s h d", h=H), ALU.add)\
                           .then_inc(sem["proj_v"], 1)
                    else:
                        dve.tensor_copy(dst, got).then_inc(sem["proj_v"], 1)

                def subtract_max(u, half, first):
                    dve.wait_ge(sem["scored"], u + 1)
                    got = banks_view(k, 2 * half, 2, S, 4 * S).rearrange("s g (h t) -> s g h t", t=S)
                    tp = top[:, half, :].rearrange("s (g h) -> s g h", g=2)
                    dve.tensor_reduce(tp, got, X, ALU.max).then_inc(sem["maxed"], 1)
                    dve.wait_ge(sem["maxed"], u + 1)
                    if not first:
                        dve.wait_ge(sem["exped"], u - 1)
                    for g in range(2):
                        ins = dve.tensor_tensor(sc[:, half, 4 * g:4 * g + 4, :], got[:, g],
                                                tp[:, g].unsqueeze(2).broadcast_to((S, 4, S)), ALU.subtract)
                    ins.then_inc(sem["less"], 1)

                def normalize(u):
                    dve.wait_ge(sem["pv"], u + 1)
                    got = k.banks[0:S, 6, 0:HH * (HD + 1)].rearrange("s (h d) -> s h d", h=HH)
                    dve.reciprocal(den[:, :].unsqueeze(2), got[:, :, HD:HD + 1]).then_inc(sem["denom"], 1)
                    dve.wait_ge(sem["denom"], u + 1)
                    dve.tensor_tensor(o[:, :, :], got[:, :, 0:HD], den[:, :].unsqueeze(2).broadcast_to((S, HH, HD)),
                                      ALU.mult).then_inc(sem["normed"], 1)

                def add(b):
                    dve.wait_ge(sem["yready"], 2 * b + 2)
                    dve.tensor_tensor(k.x[:, b, :], k.x[:, b, :], k.banks[0:S, 7, 0:D], ALU.add)\
                       .then_inc(sem["added"], 1)

                dve.wait_ge(sem["ones"], 2 if bias else 1)
                subtract_max(0, 0, True)
                subtract_max(1, 1, True)
                subtract_max(2, 0, False)
                normalize(0)
                with dve.Fori(1, B - 1) as b:
                    subtract_max(2 * b + 1, 1, False)
                    normalize(2 * b - 1)
                    subtract_max(2 * b + 2, 0, False)
                    normalize(2 * b)
                    add(b - 1)
                subtract_max(2 * B - 1, 1, False)
                normalize(2 * B - 3)
                normalize(2 * B - 2)
                add(B - 2)
                normalize(2 * B - 1)
                add(B - 1)
    k.clear("attn")


CTX_SLOTS = 4
KV_BANKS = 3
L_LAST = L - (LT - 1) * P


def context(k):
    nc, a = k.nc, k.a
    HL = DL // 2
    with ExitStack() as ctx:
        def sb(nm, shape, dt=F32):
            return ctx.enter_context(nc.sbuf_tensor(f"ctx_{nm}", shape, dt))

        raw = sb("raw", [P, CTX_SLOTS, LT, DL])
        cos, sin = sb("cos", [P, LT, DL]), sb("sin", [P, LT, DL])
        c_part, s_part = sb("c_part", [P, 2, LT, DL]), sb("s_part", [P, LT, DL])
        twice = sb("twice", [P, 2, LT, 2, DL])
        loaded = [k.sem(f"ctx_loaded{j}") for j in range(CTX_SLOTS)]
        tables, cleared, parts, roped = k.sem("ctx_tables"), k.sem("ctx_cleared"), k.sem("ctx_parts"), k.sem("ctx_roped")
        doubled, turned = k.sem("ctx_doubled"), k.sem("ctx_turned")
        high, low, scaled = k.sem("ctx_high"), k.sem("ctx_low"), k.sem("ctx_scaled")

        def load(sp, b, j):
            sp.dma_start(raw[:, j, 0:LT - 1, :],
                         a["ctx"][b, 0:(LT - 1) * P, :].rearrange("(t p) d -> p t d", p=P)).then_inc(loaded[j], 16)
            sp.dma_start(raw[0:L_LAST, j, LT - 1, :], a["ctx"][b, (LT - 1) * P:L, :]).then_inc(loaded[j], 16)

        def first_loads(sp):
            sp.dma_start(cos[:, :, :], a["ctx_cos"]).then_inc(tables, 16)
            sp.dma_start(sin[:, :, :], a["ctx_sin"]).then_inc(tables, 16)
            sp.wait_ge(cleared, 1)
            for j in range(CTX_SLOTS):
                load(sp, j, j)

        def clear(dve):
            dve.memset(raw[:, :, LT - 1, :], 0.0).then_inc(cleared, 1)
        setup(k, first_loads, clear)

        with nc.Block() as block:
            @block.sync
            def _(sp):
                with sp.Fori(1, B // CTX_SLOTS) as i:
                    for j in range(CTX_SLOTS):
                        b = CTX_SLOTS * i + j
                        sp.wait_ge(roped, b + 1 - CTX_SLOTS)
                        load(sp, b, j)

            @block.gpsimd
            def _(pool):
                pool.wait_ge(tables, 32)

                def scale(i, j, first):
                    pool.wait_ge(loaded[j], 32 * i + 32)
                    if not first:
                        pool.wait_ge(roped, CTX_SLOTS * i + j - 1)
                    pool.tensor_tensor(c_part[:, j % 2], raw[:, j], cos[:, :, :], ALU.mult).then_inc(scaled, 1)
                for j in range(CTX_SLOTS):
                    scale(0, j, j < 2)
                with pool.Fori(1, B // CTX_SLOTS) as i:
                    for j in range(CTX_SLOTS):
                        scale(i, j, False)

            @block.vector
            def _(dve):
                dve.memset(k.kv_h1[DL:DL + 2, :], 1.0).then_inc(cleared, 1)
                dve.memset(k.kv_h1[0:DL, B * L:], 0.0).then_inc(cleared, 1)
                dve.memset(k.kv_hl[:, B * L:], 0.0).then_inc(cleared, 1)
                dve.wait_ge(tables, 32)

                def rope(i, j):
                    b = CTX_SLOTS * i + j
                    dve.wait_ge(loaded[j], 32 * i + 32)
                    dve.tensor_tensor(s_part[:, :, 0:HL], raw[:, j, :, HL:DL], sin[:, :, 0:HL], ALU.mult).then_inc(parts, 1)
                    dve.tensor_tensor(s_part[:, :, HL:DL], raw[:, j, :, 0:HL], sin[:, :, HL:DL], ALU.mult).then_inc(parts, 1)
                    dve.wait_ge(parts, 2 * b + 2)
                    dve.wait_ge(scaled, b + 1)
                    dve.tensor_tensor(k.kv_tok[:, b], c_part[:, j % 2], s_part[:, :, :], ALU.add).then_inc(roped, 1)
                    dve.wait_ge(roped, b + 1)

                def split(i, j):
                    b = CTX_SLOTS * i + j
                    dve.wait_ge(high, b + 1)
                    at = bass.ds(b * L, L)
                    dve.tensor_copy(k.kv_h1[0:DL, at], k.kv_hl[0:DL, at])
                    bank = KV_BANKS * (j % 2)
                    got = k.banks[DL:2 * DL, bank:bank + KV_BANKS, :].rearrange("p a c -> p (a c)")[:, 0:L]
                    dve.tensor_tensor(k.kv_hl[DL:2 * DL, at], got, k.kv_hl[DL:2 * DL, at], ALU.subtract).then_inc(low, 1)
                def slots(i, last):
                    for j in range(CTX_SLOTS):
                        if j + 1 < CTX_SLOTS:
                            rope(i, j + 1)
                        elif not last:
                            rope(i + 1, 0)
                        split(i, j)
                rope(0, 0)
                with dve.Fori(0, B // CTX_SLOTS - 1) as i:
                    slots(i, False)
                slots(B // CTX_SLOTS - 1, True)

            @block.scalar
            def _(act):
                def double(i, j, first):
                    b = 2 * i + j
                    act.wait_ge(roped, b + 1)
                    if not first:
                        act.wait_ge(turned, b - 1)
                    act.copy(twice[:, j, :, :, :], k.kv_tok[:, b].unsqueeze(2).broadcast_to((P, LT, 2, DL)))\
                       .then_inc(doubled, 1)

                def keep_high(i, j):
                    b = 2 * i + j
                    act.wait_ge(turned, b + 1)
                    got = k.banks[:, KV_BANKS * j:KV_BANKS * (j + 1), :].rearrange("p a c -> p (a c)")[:, 0:L]
                    act.copy(k.kv_hl[:, bass.ds(b * L, L)], got).then_inc(high, 1)
                double(0, 0, True)
                double(0, 1, True)
                keep_high(0, 0)
                with act.Fori(1, B // 2) as i:
                    double(i, 0, False)
                    keep_high(i - 1, 1)
                    double(i, 1, False)
                    keep_high(i, 0)
                keep_high(B // 2 - 1, 1)

            @block.tensor
            def _(pe):
                def batch(b, j, first):
                    pe.wait_ge(doubled, b + 1)
                    if not first:
                        pe.wait_ge(low, b - 1)
                    for t in range(LT):
                        m = P if t < LT - 1 else L_LAST
                        bank = k.banks[:, KV_BANKS * j + t // 4, (t % 4) * P:(t % 4) * P + m]
                        ins = pe.transpose(bank, twice[0:m, j, t, :, :].rearrange("p a d -> p (a d)"), k.ident[0:m, 0:m])
                    ins.then_inc(turned, 1)
                batch(0, 0, True)
                batch(1, 1, True)
                with pe.Fori(1, B // 2) as i:
                    batch(2 * i, 0, False)
                    batch(2 * i + 1, 1, False)


HK, CQ, R = 128, 192, 64
CH = CQ // 2
PAIRS = H // 2


QUERY_SEMS = ("loaded0", "loaded1", "tables", "x_high", "x_low", "merged", "copied", "combined", "w_high", "w_low", "big",
              "taken", "rotated", "absorbed", "high", "low", "padded")


class Queries:

    def __init__(self, k, ctx, name):
        def sb(nm, shape, dt=F32):
            return ctx.enter_context(k.nc.sbuf_tensor(f"{name}_{nm}", shape, dt))

        self.k, self.name, self.sb = k, name, sb
        self.raw = sb("raw", [P, 2, D + CQ + DL + D])
        self.rkr = sb("rkr", [R, 2, CQ + 2 * DL])
        self.x_h, self.x_l = sb("x_h", [P, DC, T], F16), sb("x_l", [P, DC, T], F16)
        self.sem = k.sems("queries", QUERY_SEMS)
        self.loaded = [self.sem["loaded0"], self.sem["loaded1"]]

    def load(self, sp, h, j):
        a = self.k.a
        sp.dma_start(self.raw[:, j, :], a[f"{self.name}_raw"][h]).then_inc(self.loaded[j], 16)
        sp.dma_start(self.rkr[:, j, :], a[f"{self.name}_rkr"][h]).then_inc(self.loaded[j], 16)

    def later_loads(self, sp):
        with sp.Fori(1, PAIRS) as i:
            for j in range(2):
                sp.wait_ge(self.sem["merged"], 2 * i + j - 1)
                self.load(sp, 2 * i + j, j)

    def merge_last(self, pe, j):
        banks, raw, rkr = self.k.banks, self.raw, self.rkr
        for c in range(2):
            pe.matmul(banks[0:CH, 1, c * P:(c + 1) * P], rkr[:, j, c * CH:(c + 1) * CH],
                      rkr[:, j, CQ:CQ + 2 * DL], start=True, stop=True)
        pe.matmul(banks[DL * j:DL * (j + 1), 2, 0:D], raw[:, j, D + CQ:D + CQ + DL],
                  raw[:, j, D + CQ + DL:], start=True, stop=True).then_inc(self.sem["merged"], 1)

    def split_x_high(self, act):
        for n in range(2):
            at = slice(n * NT, (n + 1) * NT)
            act.copy(self.x_h[:, :, at], self.k.xnT[:, :, at]).then_inc(self.sem["x_high"], 1)

    def split_x_low(self, dve):
        for n in range(2):
            at = slice(n * NT, (n + 1) * NT)
            dve.wait_ge(self.sem["x_high"], n + 1)
            dve.tensor_tensor(self.x_l[:, :, at], self.k.xnT[:, :, at], self.x_h[:, :, at], ALU.subtract)\
               .then_inc(self.sem["x_low"], 1)

    def high(self, act, i, j, n, produced, bank, scale):
        k, t = self.k, 2 * (2 * i + j) + n
        act.wait_ge(produced, t + 1)
        act.activation(k.q_hh[:, 4 * n:4 * n + 4, bass.ds((2 * i + j) * S, S)],
                       k.banks[:, bank, 0:NT].rearrange("p (b s) -> p b s", b=4), ACT.Copy, scale=scale)\
           .then_inc(self.sem["high"], 1)

    def low(self, dve, i, j, n, bank, scale):
        k, t = self.k, 2 * (2 * i + j) + n
        dve.wait_ge(self.sem["high"], t + 1)
        at = (slice(0, DL), slice(4 * n, 4 * n + 4), bass.ds((2 * i + j) * S, S))
        dve.scalar_tensor_tensor(k.q_l[at], k.banks[0:DL, bank, 0:NT].rearrange("p (b s) -> p b s", b=4), scale,
                                 k.q_hh[at], ALU.mult, ALU.subtract).then_inc(self.sem["low"], 1)


def three_products(pe, out, w_h, w_l, v_h, v_l):
    parts = [p for wh, wl, vh, vl in zip(w_h, w_l, v_h, v_l) for p in ((wh, vh), (wh, vl), (wl, vh))]
    for n, (w, v) in enumerate(parts):
        ins = pe.matmul(out, w, v, start=n == 0, stop=n == len(parts) - 1)
    return ins


def over_heads(eng, head):
    def pair(i, first, last):
        head(i, 0, first, (i, 1), None if last else (i + 1, 0))
        head(i, 1, False, None if last else (i + 1, 0), None if last else (i + 1, 1))
    pair(0, True, False)
    with eng.Fori(1, PAIRS - 1) as i:
        pair(i, False, False)
    pair(PAIRS - 1, False, True)


def plain_queries(k, name):
    nc = k.nc
    with ExitStack() as ctx:
        q = Queries(k, ctx, name)
        w1T = q.sb("w1T", [CH, 2, D])
        w2 = q.sb("w2", [CH, 2, P])
        w0_h, w0_l = q.sb("w0_h", [P, 2, DC, P], F16), q.sb("w0_l", [P, 2, DC, P], F16)
        sem, raw = q.sem, q.raw

        def loads(sp):
            q.load(sp, 0, 0)
            q.load(sp, 1, 1)
        layer_norm(k, loads)

        with nc.Block() as block:
            @block.sync
            def _(sp):
                q.later_loads(sp)

            @block.tensor
            def _(pe):
                def merge(i, j, first):
                    pe.wait_ge(q.loaded[j], 32 * i + 32)
                    if not first:
                        pe.wait_ge(sem["copied"], 2 * i + j)
                    for half in range(2):
                        pe.matmul(k.banks[0:CH, 0, half * D:(half + 1) * D], raw[:, j, D + half * CH:D + (half + 1) * CH],
                                  raw[:, j, 0:D], start=True, stop=True)
                    q.merge_last(pe, j)

                def combine(i, j, first):
                    pe.wait_ge(sem["copied"], 2 * i + j + 1)
                    if not first:
                        pe.wait_ge(sem["w_low"], 2 * i + j)
                    for c in range(DC):
                        for half in range(2):
                            ins = pe.matmul(k.banks[:, 3, c * P:(c + 1) * P], w1T[:, half, c * P:(c + 1) * P], w2[:, half, :],
                                            start=half == 0, stop=half == 1)
                    ins.then_inc(sem["combined"], 1)

                def head(i, j, first, following, after):
                    if after:
                        merge(*after, False)
                    if following:
                        combine(*following, False)
                    pe.wait_ge(sem["w_low"], 2 * i + j + 1)
                    for n in range(2):
                        if first:
                            pe.wait_ge(sem["x_low"], n + 1)
                        if type(i) is not int or i > 0:
                            pe.wait_ge(sem["low"], 2 * (2 * i + j) + n - 3)
                        three_products(pe, k.banks[:, 4 + 2 * j + n, 0:NT],
                                       [w0_h[:, j, c, :] for c in range(DC)], [w0_l[:, j, c, :] for c in range(DC)],
                                       [q.x_h[:, c, n * NT:(n + 1) * NT] for c in range(DC)],
                                       [q.x_l[:, c, n * NT:(n + 1) * NT] for c in range(DC)]).then_inc(sem["big"], 1)
                merge(0, 0, True)
                merge(0, 1, False)
                combine(0, 0, True)
                over_heads(pe, head)

            @block.scalar
            def _(act):
                def copy_merged(i, j, first):
                    act.wait_ge(sem["merged"], 2 * i + j + 1)
                    if not first:
                        act.wait_ge(sem["combined"], 2 * i + j)
                    act.copy(w1T[:, :, :], k.banks[0:CH, 0, :].rearrange("p (c q) -> p c q", c=2))
                    act.copy(w2[:, :, :], k.banks[0:CH, 1, 0:2 * P].rearrange("p (c q) -> p c q", c=2))
                    act.copy(k.wvo[DL * j:DL * (j + 1), i, :], k.banks[DL * j:DL * (j + 1), 2, 0:D])\
                       .then_inc(sem["copied"], 1)

                def high_w(i, j, again):
                    act.wait_ge(sem["combined"], 2 * i + j + 1)
                    if again:
                        act.wait_ge(sem["big"], 2 * (2 * i + j) - 2)
                    act.activation(w0_h[:, j, :, :], k.banks[:, 3, 0:DC * P].rearrange("p (c q) -> p c q", c=DC), ACT.Copy,
                                   scale=W_SCALE).then_inc(sem["w_high"], 1)

                def head(i, j, first, following, after):
                    if following:
                        high_w(*following, not first)
                    if after:
                        copy_merged(*after, False)
                    for n in range(2):
                        q.high(act, i, j, n, sem["big"], 4 + 2 * j + n, OUT_SCALE)
                copy_merged(0, 0, True)
                q.split_x_high(act)
                high_w(0, 0, False)
                copy_merged(0, 1, False)
                over_heads(act, head)

            @block.vector
            def _(dve):
                def low_w(i, j):
                    dve.wait_ge(sem["w_high"], 2 * i + j + 1)
                    dve.scalar_tensor_tensor(w0_l[:, j, :, :], k.banks[:, 3, 0:DC * P].rearrange("p (c q) -> p c q", c=DC),
                                             W_SCALE, w0_h[:, j, :, :], ALU.mult, ALU.subtract).then_inc(sem["w_low"], 1)

                def head(i, j, first, following, after):
                    if following:
                        low_w(*following)
                    for n in range(2):
                        q.low(dve, i, j, n, 4 + 2 * j + n, OUT_SCALE)
                dve.memset(k.q_hh[:, :, Q:], 0.0).then_inc(sem["padded"], 1)
                q.split_x_low(dve)
                low_w(0, 0)
                over_heads(dve, head)
    k.clear("queries")


def rope_queries(k, name):
    nc, a = k.nc, k.a
    with ExitStack() as ctx:
        q = Queries(k, ctx, name)
        w1_h, w1_l = q.sb("w1_h", [P, 2, DC, CQ], F16), q.sb("w1_l", [P, 2, DC, CQ], F16)
        w2 = q.sb("w2", [CH, 2, 2, P])
        q_rot = q.sb("q_rot", [CH, 2, 2, NT])
        prod = q.sb("prod", [CH, 2, 2, 2, NT])
        cos, sin = q.sb("cos", [CH, 2, S]), q.sb("sin", [CH, 2, S])
        sem, raw = q.sem, q.raw

        def loads(sp):
            q.load(sp, 0, 0)
            q.load(sp, 1, 1)
            sp.dma_start(cos[:, :, :], a["q_cos"]).then_inc(sem["tables"], 16)
            sp.dma_start(sin[:, :, :], a["q_sin"]).then_inc(sem["tables"], 16)
        layer_norm(k, loads)

        with nc.Block() as block:
            @block.sync
            def _(sp):
                q.later_loads(sp)

            @block.tensor
            def _(pe):
                def merge(i, j, first):
                    pe.wait_ge(q.loaded[j], 32 * i + 32)
                    if not first:
                        pe.wait_ge(sem["w_low"], 2 * i + j)
                        pe.wait_ge(sem["copied"], 2 * i + j)
                    for c in range(DC):
                        pe.matmul(k.banks[:, 0, c * CQ:(c + 1) * CQ], raw[:, j, c * P:(c + 1) * P],
                                  raw[:, j, D:D + CQ], start=True, stop=True)
                    q.merge_last(pe, j)

                def compressed(i, j, n, first):
                    h = 2 * i + j
                    if n == 0:
                        pe.wait_ge(sem["w_low"], h + 1)
                    if first:
                        pe.wait_ge(sem["x_low"], n + 1)
                    else:
                        pe.wait_ge(sem["taken"], 2 * h + n - 1)
                    for half in range(2):
                        cols = slice(half * CH, (half + 1) * CH)
                        ins = three_products(pe, k.banks[0:CH, 3 + 2 * n + half, 0:NT],
                                             [w1_h[:, j, c, cols] for c in range(DC)], [w1_l[:, j, c, cols] for c in range(DC)],
                                             [q.x_h[:, c, n * NT:(n + 1) * NT] for c in range(DC)],
                                             [q.x_l[:, c, n * NT:(n + 1) * NT] for c in range(DC)])
                    ins.then_inc(sem["big"], 1)

                def absorbed(i, j, n, first):
                    t = 2 * (2 * i + j) + n
                    pe.wait_ge(sem["rotated"], t + 1)
                    if n == 0:
                        pe.wait_ge(sem["copied"], 2 * i + j + 1)
                    if not first:
                        pe.wait_ge(sem["low"], t)
                    for half in range(2):
                        ins = pe.matmul(k.banks[:, 7, 0:NT], w2[:, j, half, :], q_rot[:, n, half, :],
                                        start=half == 0, stop=half == 1)
                    ins.then_inc(sem["absorbed"], 1)

                def head(i, j, first, following, after):
                    if following:
                        compressed(*following, 0, False)
                    if after:
                        merge(*after, False)
                    absorbed(i, j, 0, first)
                    if following:
                        compressed(*following, 1, False)
                    absorbed(i, j, 1, False)
                merge(0, 0, True)
                merge(0, 1, False)
                compressed(0, 0, 0, True)
                compressed(0, 0, 1, True)
                over_heads(pe, head)

            @block.scalar
            def _(act):
                def high_w(i, j):
                    act.wait_ge(sem["merged"], 2 * i + j + 1)
                    act.activation(w1_h[:, j, :, :], k.banks[:, 0, 0:DC * CQ].rearrange("p (c q) -> p c q", c=DC), ACT.Copy,
                                   scale=W_SCALE).then_inc(sem["w_high"], 1)

                def copy_merged(i, j):
                    act.activation(w2[:, j, :, :], k.banks[0:CH, 1, 0:2 * P].rearrange("p (c q) -> p c q", c=2), ACT.Copy,
                                   scale=OUT_SCALE)
                    act.copy(k.wvo[DL * j:DL * (j + 1), i, :], k.banks[DL * j:DL * (j + 1), 2, 0:D])\
                       .then_inc(sem["copied"], 1)

                def head(i, j, first, following, after):
                    if after:
                        high_w(*after)
                    for n in range(2):
                        q.high(act, i, j, n, sem["absorbed"], 7, 1.0)
                    if after:
                        copy_merged(*after)
                high_w(0, 0)
                copy_merged(0, 0)
                q.split_x_high(act)
                high_w(0, 1)
                copy_merged(0, 1)
                over_heads(act, head)

            @block.vector
            def _(dve):
                def low_w(i, j):
                    dve.wait_ge(sem["w_high"], 2 * i + j + 1)
                    dve.scalar_tensor_tensor(w1_l[:, j, :, :], k.banks[:, 0, 0:DC * CQ].rearrange("p (c q) -> p c q", c=DC),
                                             W_SCALE, w1_h[:, j, :, :], ALU.mult, ALU.subtract).then_inc(sem["w_low"], 1)

                def take(i, j, n, first):
                    t = 2 * (2 * i + j) + n
                    dve.wait_ge(sem["big"], t + 1)
                    if not first:
                        dve.wait_ge(sem["rotated"], t - 1)
                    got = k.banks[0:CH, 3 + 2 * n:5 + 2 * n, 0:NT].rearrange("p a (b s) -> p a b s", s=S)
                    for half in range(2):
                        dve.tensor_tensor(prod[:, n, 0, half, :].rearrange("p (b s) -> p b s", s=S), got[:, half],
                                          cos[:, half, :].unsqueeze(1).broadcast_to((CH, 4, S)), ALU.mult)
                        ins = dve.tensor_tensor(prod[:, n, 1, 1 - half, :].rearrange("p (b s) -> p b s", s=S), got[:, half],
                                                sin[:, half, :].unsqueeze(1).broadcast_to((CH, 4, S)), ALU.mult)
                    ins.then_inc(sem["taken"], 1)

                def head(i, j, first, following, after):
                    for n in range(2):
                        if following:
                            take(*following, n, False)
                        if after and n == 0:
                            low_w(*after)
                        q.low(dve, i, j, n, 7, 1.0)
                dve.memset(k.q_hh[:, :, Q:], 0.0).then_inc(sem["padded"], 1)
                low_w(0, 0)
                q.split_x_low(dve)
                low_w(0, 1)
                dve.wait_ge(sem["tables"], 32)
                take(0, 0, 0, True)
                take(0, 0, 1, True)
                over_heads(dve, head)

            @block.gpsimd
            def _(pool):
                def rotate(i, j, n, first):
                    t = 2 * (2 * i + j) + n
                    pool.wait_ge(sem["taken"], t + 1)
                    if not first:
                        pool.wait_ge(sem["absorbed"], t - 1)
                    pool.tensor_tensor(q_rot[:, n, :, :], prod[:, n, 0], prod[:, n, 1], ALU.add)\
                        .then_inc(sem["rotated"], 1)
                for n in range(2):
                    rotate(0, 0, n, True)
                for n in range(2):
                    rotate(0, 1, n, False)
                with pool.Fori(1, PAIRS) as i:
                    for j in range(2):
                        for n in range(2):
                            rotate(i, j, n, False)
    k.clear("queries")


MAX_CHUNKS = [(0, 482), (482, 482), (964, 480)]
Q = H * S
QT = (Q + P - 1) // P
TASKS = QT * len(MAX_CHUNKS)
STEPS = 2 * LT
TURN = 21
OUTPUT = 5
SLOTS = 4


def aux_plan(tops, output):
    plan, last, place = [[] for _ in range(STEPS)], {}, 0
    for s in range(STEPS):
        todo = [("top", n, 6 + n % 2) for n in range(2 * s, min(2 * s + 2, TASKS))] if tops else []
        if tops and s == TURN:
            todo.append(("turn", 0, 7))
        if output and s == OUTPUT:
            todo.append(("output", 0, 6))
        for kind, n, bank in todo:
            plan[s].append((place, kind, n, bank, last.get(bank, 0)))
            place += 1
            last[bank] = place
    return plan, place


def cross_attention(k, name):
    nc = k.nc
    with ExitStack() as ctx:
        def sb(nm, shape, dt=F32):
            return ctx.enter_context(nc.sbuf_tensor(f"{name}_{nm}", shape, dt))

        kv = sb("kv", [P, LT, DL])
        pr = sb("pr", [P, SLOTS, 2 * NT])
        pr_last = sb("pr_last", [P, 2 * NT])
        pair = sb("pair", [P, 2, 2 * NT])
        quad = sb("quad", [P, 2, 2 * NT])
        raw = sb("att_raw", [P, 2, NT])
        rden = sb("rden", [P, NT])
        att = sb("att", [P, 2, NT])
        top3 = sb("top3", [P, QT, len(MAX_CHUNKS)])
        top = sb("top", [P, QT])
        shift = sb("shift", [QT, 2, P], F16)
        sem = k.sems("cross", (
            "staged", "scored", "exped", "weighted", "paired", "quaded", "summed", "raw", "recip", "normed", "aux",
            "aux_used", "topped", "shift_high", "shifted", "shift_in", "cleared"))
        first_plan, first_n = aux_plan(True, False)
        mid_plan, mid_n = aux_plan(True, True)
        last_plan, last_n = aux_plan(False, True)
        QUADS = STEPS // 4

        def body_of(b):
            ahead = TASKS + 1
            if isinstance(b, int) and b == 0:
                return first_plan, ahead
            base = ahead + first_n + (b - 1) * mid_n
            return (last_plan if isinstance(b, int) and b == B - 1 else mid_plan), base

        end = TASKS + 1 + first_n + (B - 2) * mid_n + last_n

        def weights_of(s):
            return pr[:, s % SLOTS, :] if s % LT < LT - 1 else pr_last[:, :]

        def queries(q, b, half, c):
            return q[:, b, half * 2 * NT:(half + 1) * 2 * NT].rearrange("p (i j s) -> p j i s", j=2, s=S)[:, c]

        def batches(eng, batch):
            batch(0)
            with eng.Fori(1, B - 1) as b:
                batch(b)
            batch(B - 1)

        with nc.Block() as block:
            @block.sync
            def _(sp):
                def place_shift(b, after):
                    sp.wait_ge(sem["shifted"], after)
                    for part in range(2):
                        sp.dma_start(k.q_l[DL + part:DL + part + 1, b, :].rearrange("o (t c) -> o t c", c=P),
                                     shift[:, part, :]).then_inc(sem["shift_in"], 16)
                place_shift(0, 1)
                with sp.Fori(1, B) as b:
                    place_shift(b, b + 1)

            @block.gpsimd
            def _(pool):
                pool.sem_inc(sem["paired"], 2)

                def stage(b, t):
                    pool.wait_ge(sem["weighted"], SLOTS + STEPS * b - LT + t + 1)
                    pool.tensor_copy(kv[:, t, :], k.kv_tok[:, b, t, :]).then_inc(sem["staged"], 1)

                def batch(b):
                    for n in range(STEPS // 2):
                        pool.wait_ge(sem["exped"], STEPS * b + 2 * n + 4)
                        if n >= 2 or not (isinstance(b, int) and b == 0):
                            pool.wait_ge(sem["quaded"], QUADS * b + n // 2)
                        pool.tensor_tensor(pair[:, n % 2, :], weights_of(2 * n), weights_of(2 * n + 1), ALU.add)\
                            .then_inc(sem["paired"], 1)
                        if not (isinstance(b, int) and b == B - 1) and n > LT // 2:
                            for t in range(2 * (n - LT // 2) - 2, 2 * (n - LT // 2)):
                                stage(b + 1, t)
                    if not (isinstance(b, int) and b == B - 1):
                        stage(b + 1, LT - 2)
                        stage(b + 1, LT - 1)
                pool.tensor_copy(kv[:, :, :], k.kv_tok[:, 0]).then_inc(sem["staged"], LT)
                batches(pool, batch)

            @block.tensor
            def _(pe):
                pe.sem_inc(sem["weighted"], SLOTS)

                def top_task(b, n):
                    t, (at, cols) = n // len(MAX_CHUNKS), MAX_CHUNKS[n % len(MAX_CHUNKS)]
                    pe.matmul(k.banks[:, 6 + n % 2, 0:cols], k.q_hh[:, b, t * P:(t + 1) * P],
                              k.kv_hl[:, bass.ds(b * L + at, cols)], start=True, stop=True).then_inc(sem["aux"], 1)

                def turn_tops(after):
                    pe.wait_ge(sem["topped"], after)
                    pe.transpose(k.banks[0:QT, 7, 0:P], top[:, :], k.ident[:, :]).then_inc(sem["aux"], 1)

                def scores(b, s):
                    half, t, bank = s // LT, s % LT, 2 * (s % 2)
                    pe.wait_ge(sem["exped"], STEPS * b + s + 1)
                    if s == 0:
                        pe.wait_ge(sem["shift_in"], 32 * b + 32)
                    at = bass.ds(b * L + t * P, P)
                    for c in range(2):
                        pe.matmul(k.banks[:, bank + c, 0:NT], k.kv_hl[:, at], queries(k.q_hh, b, half, c),
                                  start=True, stop=False)
                    for c in range(2):
                        ins = pe.matmul(k.banks[:, bank + c, 0:NT], k.kv_h1[:, at], queries(k.q_l, b, half, c),
                                        start=False, stop=True)
                    ins.then_inc(sem["scored"], 1)

                def weigh(b, s):
                    half, t = s // LT, s % LT
                    weights = weights_of(s)
                    pe.wait_ge(sem["exped"], STEPS * b + s + 3)
                    if half == 0:
                        pe.wait_ge(sem["staged"], LT * b + t + 1)
                    if t == 0 and not (isinstance(b, int) and b == 0 and half == 0):
                        pe.wait_ge(sem["raw"], 2 * b + half)
                    for c in range(2):
                        ins = pe.matmul(k.banks[DL * c:DL * (c + 1), 4, 0:NT], kv[:, t, :],
                                        weights[:, c * NT:(c + 1) * NT], start=t == 0, stop=t == LT - 1)
                    ins.then_inc(sem["weighted"], 1)

                def total(b, n):
                    pe.wait_ge(sem["quaded"], QUADS * b + n + 1)
                    if n % 3 == 0 and not (isinstance(b, int) and b == 0 and n == 0):
                        pe.wait_ge(sem["normed"], 2 * b + n // 3)
                    for c in range(2):
                        ins = pe.matmul(k.banks[DL * c:DL * (c + 1), 5, 0:NT], k.ones64[:, :],
                                        quad[:, n % 2, c * NT:(c + 1) * NT], start=n % 3 == 0, stop=n % 3 == 2)
                    ins.then_inc(sem["summed"], 1)

                def output(b):
                    pe.wait_ge(sem["normed"], 2 * b + 2)
                    for n in range(PAIRS):
                        ins = pe.matmul(k.banks[0:S, 6, 0:D], att[:, n // 4, (n % 4) * S:(n % 4 + 1) * S],
                                        k.wvo[:, n, :], start=n == 0, stop=n == PAIRS - 1)
                    ins.then_inc(sem["aux"], 1)

                def batch(b):
                    first, last = (isinstance(b, int) and b == e for e in (0, B - 1))
                    plan, base = body_of(b)
                    for s in range(STEPS):
                        if s + 1 < STEPS:
                            scores(b, s + 1)
                        elif not last:
                            scores(b + 1, 0)
                        for _, kind, n, _, need in plan[s]:
                            pe.wait_ge(sem["aux_used"], base + need)
                            if kind == "top":
                                top_task(b + 1, n)
                            elif kind == "turn":
                                turn_tops(b + 2)
                            else:
                                output(b - 1)
                        weigh(b, s)
                        if s % 4 == 2:
                            if s > 2:
                                total(b, s // 4 - 1)
                            elif not first:
                                total(b - 1, QUADS - 1)

                for n in range(TASKS):
                    if n >= 2:
                        pe.wait_ge(sem["aux_used"], n - 1)
                    top_task(0, n)
                turn_tops(1)
                scores(0, 0)
                batches(pe, batch)
                total(B - 1, QUADS - 1)
                pe.wait_ge(sem["aux_used"], end)
                output(B - 1)

            @block.scalar
            def _(act):
                act.sem_inc(sem["exped"], 2)
                act.wait_ge(sem["cleared"], 1)
                with act.Fori(0, B) as b:
                    for s in range(STEPS):
                        m = P if s % LT < LT - 1 else L_LAST
                        act.wait_ge(sem["scored"], STEPS * b + s + 1)
                        act.wait_ge(sem["weighted"], STEPS * b + s + 1)
                        act.wait_ge(sem["paired"], STEPS // 2 * b + s // 2 + 1)
                        act.activation(weights_of(s)[0:m, :].rearrange("p (c n) -> p c n", c=2),
                                       k.banks[0:m, 2 * (s % 2):2 * (s % 2) + 2, 0:NT], ACT.Exp).then_inc(sem["exped"], 1)

            @block.vector
            def _(dve):
                dve.memset(pr_last[:, :], 0.0).then_inc(sem["cleared"], 1)

                def top_task(base, place, n):
                    t = n // len(MAX_CHUNKS)
                    cols = MAX_CHUNKS[n % len(MAX_CHUNKS)][1]
                    dve.wait_ge(sem["aux"], base + place + 1)
                    dve.tensor_reduce(top3[:, t, n % len(MAX_CHUNKS):n % len(MAX_CHUNKS) + 1],
                                      k.banks[:, 6 + n % 2, 0:cols], X, ALU.max).then_inc(sem["aux_used"], 1)
                    if n == TASKS - 1:
                        dve.wait_ge(sem["aux_used"], base + place + 1)
                        dve.tensor_reduce(top[:, :], top3[:, :, :], X, ALU.max).then_inc(sem["topped"], 1)

                def make_shift(base, place, b):
                    dve.wait_ge(sem["aux"], base + place + 1)
                    if not (isinstance(b, int) and b == 0):
                        dve.wait_ge(sem["shift_in"], 32 * b)
                    got = k.banks[0:QT, 7, 0:P]
                    dve.tensor_scalar(shift[:, 0, :], got, -1.0, None, ALU.mult).then_inc(sem["shift_high"], 1)
                    dve.wait_ge(sem["shift_high"], b + 1)
                    dve.scalar_tensor_tensor(shift[:, 1, :], got, -1.0, shift[:, 0, :], ALU.mult, ALU.subtract)\
                       .then_inc(sem["shifted"], 1)
                    dve.wait_ge(sem["shifted"], b + 1)
                    dve.sem_inc(sem["aux_used"], 1)

                def empty(u, half):
                    dve.wait_ge(sem["weighted"], SLOTS + LT * (u + 1))
                    dve.tensor_copy(raw[:, half, :], k.banks[:, 4, 0:NT]).then_inc(sem["raw"], 1)

                def add_pairs(b, n):
                    dve.wait_ge(sem["paired"], 2 + STEPS // 2 * b + 2 * n + 2)
                    if n >= 2 or not (isinstance(b, int) and b == 0):
                        dve.wait_ge(sem["summed"], QUADS * b + n - 1)
                    dve.tensor_tensor(quad[:, n % 2, :], pair[:, 0, :], pair[:, 1, :], ALU.add).then_inc(sem["quaded"], 1)

                def normalize(u, half):
                    dve.wait_ge(sem["summed"], 3 * (u + 1))
                    dve.reciprocal(rden[:, :], k.banks[:, 5, 0:NT]).then_inc(sem["recip"], 1)
                    dve.wait_ge(sem["recip"], u + 1)
                    dve.tensor_tensor(att[:, half, :], raw[:, half, :], rden[:, :], ALU.mult).then_inc(sem["normed"], 1)

                def add_output(base, place, b):
                    dve.wait_ge(sem["aux"], base + place + 1)
                    dve.tensor_tensor(k.x[:, b, :], k.x[:, b, :], k.banks[0:S, 6, 0:D], ALU.add)\
                       .then_inc(sem["aux_used"], 1)

                def batch(b):
                    first = isinstance(b, int) and b == 0
                    plan, base = body_of(b)
                    for s in range(STEPS):
                        if s == 0 and not first:
                            empty(2 * b - 1, 1)
                        if s == LT:
                            empty(2 * b, 0)
                        for place, kind, n, _, _ in plan[s]:
                            if kind == "top":
                                top_task(base, place, n)
                            elif kind == "turn":
                                make_shift(base, place, b + 1)
                            else:
                                add_output(base, place, b - 1)
                        if s % 4 == 1:
                            if s > 1:
                                add_pairs(b, s // 4 - 1)
                            elif not first:
                                add_pairs(b - 1, QUADS - 1)
                        if s == 3 and not first:
                            normalize(2 * b - 1, 1)
                        if s == LT + 3:
                            normalize(2 * b, 0)

                for n in range(TASKS):
                    top_task(0, n, n)
                make_shift(0, TASKS, 0)
                batches(dve, batch)
                empty(2 * B - 1, 1)
                add_pairs(B - 1, QUADS - 1)
                normalize(2 * B - 1, 1)
                add_output(end, 0, B - 1)
    k.clear("cross")


def router(k, name, experts, kind, top, loads_after):
    nc, a, E = k.nc, k.a, experts
    with ExitStack() as ctx:
        def sb(nm, shape, dt=F32):
            return ctx.enter_context(nc.sbuf_tensor(f"{name}_{nm}", shape, dt))

        wr = sb("wr", [P, DC, E])
        lower = sb("lower", [S, E, E])
        score, ex = sb("score", [S, B, E]), sb("ex", [S, B, E])
        gt, eq = sb("gt", [S, B, E, E]), sb("eq", [S, B, E, E])
        rank, gate = sb("rank", [S, B, E]), sb("gate", [S, B, E])
        best, total = sb("best", [S, B]), sb("total", [S, B])
        high = sb("high", [S, B, E], F16)
        parts = sb("parts", [S, B, 2 * E])
        s = k.sems("router", ("loaded", "scored", "step", "less", "exped", "split", "turned"))

        def over_last(v):
            return v[:, :].unsqueeze(2).broadcast_to((S, B, E))

        def loads(sp):
            sp.dma_start(wr[:, :, :], a[f"{name}_wr"]).then_inc(s["loaded"], 16)
            sp.dma_start(lower[:, :, :], a[f"lower{E}"]).then_inc(s["loaded"], 16)
            loads_after(sp)
        layer_norm(k, loads)

        with nc.Block() as block:
            @block.tensor
            def _(pe):
                pe.wait_ge(s["loaded"], 32)
                for b in range(B):
                    for c in range(DC):
                        ins = pe.matmul(k.banks[0:S, 0, b * E:(b + 1) * E], k.xnT[:, c, b * S:(b + 1) * S], wr[:, c, :],
                                        start=c == 0, stop=c == DC - 1)
                ins.then_inc(s["scored"], 1)
                pe.wait_ge(s["split"], 1)
                for b in range(B):
                    ins = pe.transpose(k.banks[0:2 * E, 1 + b // 4, (b % 4) * S:(b % 4 + 1) * S], parts[:, b, :],
                                       k.ident[0:S, 0:S])
                ins.then_inc(s["turned"], 1)

            @block.scalar
            def _(act):
                if kind != "choice":
                    act.wait_ge(s["less"], 1)
                    act.activation(ex[:, :, :], ex[:, :, :], ACT.Exp).then_inc(s["exped"], 1)
                act.wait_ge(s["turned"], 1)
                act.copy(k.gates[0:2 * E, :].rearrange("e (g t) -> e g t", g=2), k.banks[0:2 * E, 1:3, 0:NT])

            @block.vector
            def _(dve):
                steps = Steps(dve, s["step"])

                def choose(v):
                    own, others = v.unsqueeze(3).broadcast_to((S, B, E, E)), v.unsqueeze(2).broadcast_to((S, B, E, E))
                    steps.link(dve.tensor_tensor(gt[:, :, :, :], others, own, ALU.is_gt))
                    steps.link(dve.tensor_tensor(eq[:, :, :, :], others, own, ALU.is_equal))
                    steps.link(dve.tensor_tensor(eq[:, :, :, :], eq[:, :, :, :],
                                                 lower[:, :, :].unsqueeze(1).broadcast_to((S, B, E, E)), ALU.mult))
                    steps.link(dve.tensor_tensor(gt[:, :, :, :], gt[:, :, :, :], eq[:, :, :, :], ALU.add))
                    steps.link(dve.tensor_reduce(rank[:, :, :], gt[:, :, :, :], X, ALU.add))
                    steps.link(dve.tensor_scalar(rank[:, :, :], rank[:, :, :], float(top), None, ALU.is_lt))

                dve.wait_ge(s["loaded"], 32)
                dve.wait_ge(s["scored"], 1)
                steps.link(dve.tensor_copy(score[:, :, :].rearrange("s b e -> s (b e)"), k.banks[0:S, 0, 0:B * E]))
                if kind != "choice":
                    steps.link(dve.tensor_reduce(best[:, :], score[:, :, :], X, ALU.max))
                    dve.tensor_tensor(ex[:, :, :], score[:, :, :], over_last(best), ALU.subtract).then_inc(s["less"], 1)
                    dve.wait_ge(s["exped"], 1)
                if kind == "softmax_first":
                    steps.link(dve.tensor_reduce(total[:, :], ex[:, :, :], X, ALU.add))
                    steps.link(dve.reciprocal(total[:, :], total[:, :]))
                    steps.link(dve.tensor_tensor(score[:, :, :], ex[:, :, :], over_last(total), ALU.mult))
                choose(score[:, :, :])
                if kind == "choice":
                    steps.link(dve.tensor_copy(gate[:, :, :], rank[:, :, :]))
                elif kind == "softmax_first":
                    steps.link(dve.tensor_tensor(gate[:, :, :], score[:, :, :], rank[:, :, :], ALU.mult))
                else:
                    steps.link(dve.tensor_tensor(ex[:, :, :], ex[:, :, :], rank[:, :, :], ALU.mult))
                    steps.link(dve.tensor_reduce(total[:, :], ex[:, :, :], X, ALU.add))
                    steps.link(dve.reciprocal(total[:, :], total[:, :]))
                    steps.link(dve.tensor_tensor(gate[:, :, :], ex[:, :, :], over_last(total), ALU.mult))
                steps.link(dve.tensor_copy(high[:, :, :], gate[:, :, :]))
                dve.tensor_copy(parts[:, :, 0:E], high[:, :, :])
                dve.tensor_tensor(parts[:, :, E:2 * E], gate[:, :, :], high[:, :, :], ALU.subtract).then_inc(s["split"], 1)
    k.clear("router")


def over_tiles(eng, tiles, tile):
    full = (tiles - 1) // 2
    tile(0, 0, True, False)
    tile(0, 1, False, False)
    with eng.Fori(1, full) as i:
        tile(i, 0, False, False)
        tile(i, 1, False, False)
    tile(full, 0, False, tiles % 2 == 1)
    if tiles % 2 == 0:
        tile(full, 1, False, True)


class FeedForward:

    def __init__(self, k, ctx, name, tiles, down, experts=0, scales=False):
        def sb(nm, shape, dt=F32):
            return ctx.enter_context(k.nc.sbuf_tensor(f"{name}_{nm}", shape, dt))

        self.k, self.name, self.tiles, self.down, self.experts, self.scales = k, name, tiles, down, experts, scales
        self.gu = sb("gu", [P, 2, 2 * D])
        self.dn = sb("dn", [P, 2, D])
        self.gu_h, self.gu_l = sb("gu_h", [P, 2, 2 * D], F16), sb("gu_l", [P, 2, 2 * D], F16)
        self.dn_h, self.dn_l = sb("dn_h", [P, 2, D], F16), sb("dn_l", [P, 2, D], F16)
        self.src_h, self.src_l = sb("src_h", [P, DC, T], F16), sb("src_l", [P, DC, T], F16)
        self.act_g = sb("act_g", [P, 2, NT])
        self.prod = sb("prod", [P, 2, NT])
        self.hid = sb("hid", [P, 2, NT])
        self.hid_h, self.hid_l = sb("hid_h", [P, 2, NT], F16), sb("hid_l", [P, 2, NT], F16)
        self.yT = sb("yT", [P, DC, T])
        if experts:
            self.expert_of = sb("expert_of", [P, tiles * P], F16)
        if scales:
            self.sc_g, self.sc_u, self.sc_d = sb("sc_g", [P, tiles]), sb("sc_u", [P, tiles]), sb("sc_d", [P, DC])
        self.s = k.sems("ffn", ("gu0", "gu1", "dn0", "dn1", "extra", "scaled", "src_high", "src_low", "gu_high", "gu_low",
                                "dn_high", "dn_low", "gate", "up", "spread", "silu", "prod", "hid", "hid_high",
                                "hid_low", "down", "out", "turned", "added"))

    def load(self, sp, m, j, again):
        s, a = self.s, self.k.a
        if again:
            sp.wait_ge(s["gu_low"], m - 1)
        sp.dma_start(self.gu[:, j, :], a[f"{self.name}_gu"][m]).then_inc(s[f"gu{j}"], 16)
        if again:
            sp.wait_ge(s["dn_low"], m - 1)
        sp.dma_start(self.dn[:, j, :], self.down[m]).then_inc(s[f"dn{j}"], 16)

    def first_loads(self, sp):
        s, a, name = self.s, self.k.a, self.name
        self.load(sp, 0, 0, False)
        if self.experts:
            sp.dma_start(self.expert_of[:, :], a[f"{name}_expert_of"]).then_inc(s["extra"], 16)
        if self.scales:
            for dst, nm in ((self.sc_g, "sc_g"), (self.sc_u, "sc_u"), (self.sc_d, "sc_d")):
                sp.dma_start(dst[:, :], a[f"{name}_{nm}"]).then_inc(s["extra"], 16)
        self.load(sp, 1, 1, False)


def feed_forward(f, src):
    k, nc, s, tiles, experts, scales = f.k, f.k.nc, f.s, f.tiles, f.experts, f.scales
    act_g, prod, hid, yT = f.act_g, f.prod, f.hid, f.yT
    with nc.Block() as block:
        @block.sync
        def _(sp):
            with sp.Fori(1, tiles // 2) as i:
                f.load(sp, 2 * i, 0, True)
                f.load(sp, 2 * i + 1, 1, True)
            if tiles % 2:
                f.load(sp, tiles - 1, 0, True)

        @block.tensor
        def _(pe):
            if experts:
                pe.wait_ge(s["extra"], 16)

            def product(bank, w_h, w_l, v_h, v_l, chunks, start, stop):
                parts = [(w, v, cols, at) for cols, at in chunks for w, v in ((w_h, v_h), (w_h, v_l), (w_l, v_h))]
                for p, (w, v, cols, at) in enumerate(parts):
                    ins = pe.matmul(k.banks[:, bank, 0:NT], w[:, cols[0], cols[1]:cols[1] + P], v[:, at[0], at[1]:at[1] + NT],
                                    start=start and p == 0, stop=stop and p == len(parts) - 1)
                return ins

            def rise(i, j, n, begin):
                t = 2 * (2 * i + j) + n
                if n == 0:
                    pe.wait_ge(s["gu_low"], 2 * i + j + 1)
                if begin:
                    pe.wait_ge(s["src_low"], n + 1)
                else:
                    pe.wait_ge(s["silu"], t - 1)
                product(7 if n else 4, f.gu_h, f.gu_l, f.src_h, f.src_l,
                        [((j, c * P), (c, n * NT)) for c in range(DC)], True, True).then_inc(s["gate"], 1)
                if not begin or n:
                    pe.wait_ge(s["prod"], t)
                product(5, f.gu_h, f.gu_l, f.src_h, f.src_l,
                        [((j, D + c * P), (c, n * NT)) for c in range(DC)], True, True).then_inc(s["up"], 1)
                if experts:
                    if not begin or n:
                        pe.wait_ge(s["hid"], t)
                    pe.matmul(k.banks[:, 6, 0:NT], f.expert_of[:, bass.ds((2 * i + j) * P, P)],
                              k.gates[:, n * NT:(n + 1) * NT], start=True, stop=True)\
                      .then_inc(s["spread"], 1)

            def fall(i, j, n, first, last):
                t = 2 * (2 * i + j) + n
                if n == 0:
                    pe.wait_ge(s["dn_low"], 2 * i + j + 1)
                pe.wait_ge(s["hid_low"], t + 1)
                for c in range(DC):
                    ins = product(2 * c + n, f.dn_h, f.dn_l, f.hid_h, f.hid_l, [((j, c * P), (n, 0))], first, last)
                ins.then_inc(s["down"], 1)

            def tile(i, j, first, last):
                for n in range(2):
                    if not last:
                        rise(*((i, 1) if j == 0 else (i + 1, 0)), n, False)
                    fall(i, j, n, first, last)
            rise(0, 0, 0, True)
            rise(0, 0, 1, True)
            over_tiles(pe, tiles, tile)
            pe.wait_ge(s["out"], 4)
            for b in range(B):
                if b >= 4:
                    pe.wait_ge(s["added"], b - 3)
                for c in range(DC):
                    ins = pe.transpose(k.banks[0:S, 4 + b % 4, c * P:(c + 1) * P], yT[:, c, b * S:(b + 1) * S],
                                       k.ident[:, :])
                ins.then_inc(s["turned"], 1)

        @block.scalar
        def _(act):
            def high_gu(i, j, again):
                act.wait_ge(s[f"gu{j}"], 16 * i + 16)
                if again:
                    act.wait_ge(s["up"], 2 * (2 * i + j) - 2)
                act.activation(f.gu_h[:, j, :], f.gu[:, j, :], ACT.Copy, scale=W_SCALE).then_inc(s["gu_high"], 1)

            def high_dn(i, j, again):
                act.wait_ge(s[f"dn{j}"], 16 * i + 16)
                if again:
                    act.wait_ge(s["down"], 2 * (2 * i + j) - 2)
                act.activation(f.dn_h[:, j, :], f.dn[:, j, :], ACT.Copy, scale=W_SCALE).then_inc(s["dn_high"], 1)

            def tile(i, j, first, last):
                m = 2 * i + j
                following = (i, 1) if j == 0 else (i + 1, 0)
                for n in range(2):
                    t = 2 * m + n
                    act.wait_ge(s["gate"], t + 1)
                    if not first:
                        act.wait_ge(s["prod"], t - 1)
                    act.activation(act_g[:, n, :], k.banks[:, 7 if n else 4, 0:NT], ACT.Silu,
                                   scale=f.sc_g[:, m:m + 1] if scales else OUT_SCALE).then_inc(s["silu"], 1)
                    if not last and n == 0:
                        high_gu(*following, not first)
                    act.wait_ge(s["hid"], t + 1)
                    if not first:
                        act.wait_ge(s["down"], t - 1)
                    act.copy(f.hid_h[:, n, :], hid[:, n, :]).then_inc(s["hid_high"], 1)
                    if not last and n == 1:
                        high_dn(*following, not first)
            high_gu(0, 0, False)
            for n in range(2):
                act.copy(f.src_h[:, :, n * NT:(n + 1) * NT], src[:, :, n * NT:(n + 1) * NT]).then_inc(s["src_high"], 1)
            high_dn(0, 0, False)
            if scales:
                act.wait_ge(s["scaled"], 3)
                for m in range(tiles):
                    tile(m // 2, m % 2, m == 0, m == tiles - 1)
            else:
                over_tiles(act, tiles, tile)
            act.wait_ge(s["down"], 2 * tiles)
            for c in range(DC):
                for n in range(2):
                    act.activation(yT[:, c, n * NT:(n + 1) * NT], k.banks[:, 2 * c + n, 0:NT], ACT.Copy,
                                   scale=f.sc_d[:, c:c + 1] if scales else OUT_SCALE).then_inc(s["out"], 1)

        @block.vector
        def _(dve):
            def low_gu(i, j):
                dve.wait_ge(s["gu_high"], 2 * i + j + 1)
                dve.scalar_tensor_tensor(f.gu_l[:, j, :], f.gu[:, j, :], W_SCALE, f.gu_h[:, j, :], ALU.mult, ALU.subtract)\
                   .then_inc(s["gu_low"], 1)

            def low_dn(i, j):
                dve.wait_ge(s["dn_high"], 2 * i + j + 1)
                dve.scalar_tensor_tensor(f.dn_l[:, j, :], f.dn[:, j, :], W_SCALE, f.dn_h[:, j, :], ALU.mult, ALU.subtract)\
                   .then_inc(s["dn_low"], 1)

            def tile(i, j, first, last):
                m = 2 * i + j
                following = (i, 1) if j == 0 else (i + 1, 0)
                for n in range(2):
                    t = 2 * m + n
                    dve.wait_ge(s["silu"], t + 1)
                    dve.wait_ge(s["up"], t + 1)
                    if not first:
                        dve.wait_ge(s["hid_low"], t - 1)
                    if scales:
                        dve.scalar_tensor_tensor(hid[:, n, :], k.banks[:, 5, 0:NT], f.sc_u[:, bass.ds(m, 1)],
                                                 act_g[:, n, :], ALU.mult, ALU.mult).then_inc(s["prod"], 1)
                        dve.wait_ge(s["prod"], t + 1)
                        dve.sem_inc(s["hid"], 1)
                    else:
                        dve.tensor_tensor(prod[:, n, :], act_g[:, n, :], k.banks[:, 5, 0:NT], ALU.mult)\
                           .then_inc(s["prod"], 1)
                        dve.wait_ge(s["prod"], t + 1)
                        dve.wait_ge(s["spread"], t + 1)
                        dve.tensor_tensor(hid[:, n, :], prod[:, n, :], k.banks[:, 6, 0:NT], ALU.mult)\
                           .then_inc(s["hid"], 1)
                    if not last and n == 0:
                        low_gu(*following)
                    dve.wait_ge(s["hid_high"], t + 1)
                    dve.tensor_tensor(f.hid_l[:, n, :], hid[:, n, :], f.hid_h[:, n, :], ALU.subtract)\
                       .then_inc(s["hid_low"], 1)
                    if not last and n == 1:
                        low_dn(*following)
            if scales:
                dve.wait_ge(s["extra"], 48)
                for scale in (f.sc_g, f.sc_u, f.sc_d):
                    dve.tensor_scalar(scale[:, :], scale[:, :], OUT_SCALE, None, ALU.mult).then_inc(s["scaled"], 1)
            low_gu(0, 0)
            for n in range(2):
                dve.wait_ge(s["src_high"], n + 1)
                dve.tensor_tensor(f.src_l[:, :, n * NT:(n + 1) * NT], src[:, :, n * NT:(n + 1) * NT],
                                  f.src_h[:, :, n * NT:(n + 1) * NT], ALU.subtract).then_inc(s["src_low"], 1)
            low_dn(0, 0)
            if scales:
                dve.wait_ge(s["scaled"], 3)
            over_tiles(dve, tiles, tile)
            for b in range(B):
                dve.wait_ge(s["turned"], b + 1)
                dve.tensor_tensor(k.x[:, b, :], k.x[:, b, :], k.banks[0:S, 4 + b % 4, 0:D], ALU.add)\
                   .then_inc(s["added"], 1)
    k.clear("ffn")


FFN_TILES = 8


def hadamard_weights(k, name, down):
    nc, a, M = k.nc, k.a, FFN_TILES
    with ExitStack() as ctx:
        wd = ctx.enter_context(nc.sbuf_tensor(f"{name}_wd", [P, M, D], F32))
        z = [ctx.enter_context(nc.sbuf_tensor(f"{name}_z{j}", [P, M, D], F32)) for j in range(2)]
        h128 = ctx.enter_context(nc.sbuf_tensor(f"{name}_h128", [P, P], F32))
        su = ctx.enter_context(nc.sbuf_tensor(f"{name}_su", [P, M], F32))
        s = k.sems("hadamard", ("loaded", "turned", "copied", "step", "stored"))
        with nc.Block() as block:
            @block.sync
            def _(sp):
                sp.dma_start(wd[:, :, :], a[f"{name}_wd"]).then_inc(s["loaded"], 16)
                sp.dma_start(h128[:, :], a["h256"][0:P, 0:P]).then_inc(s["loaded"], 16)
                sp.dma_start(su[:, :], a[f"{name}_su_dp"]).then_inc(s["loaded"], 16)
                sp.wait_ge(s["step"], 6 + M)
                sp.dma_start(down.rearrange("m p d -> p m d"), z[0][:, :, :]).then_inc(s["stored"], 16)
                sp.wait_ge(s["stored"], 16)

            @block.tensor
            def _(pe):
                pe.wait_ge(s["loaded"], 48)
                for m in range(M):
                    pe.matmul(k.banks[:, m, 0:D], h128[:, :], wd[:, m, :], start=True, stop=True).then_inc(s["turned"], 1)

            @block.scalar
            def _(act):
                for m in range(M):
                    act.wait_ge(s["turned"], m + 1)
                    act.copy(z[0][:, m, :], k.banks[:, m, 0:D]).then_inc(s["copied"], 1)

            @block.vector
            def _(dve):
                dve.wait_ge(s["copied"], M)
                steps = Steps(dve, s["step"])
                for level in range(3):
                    src, dst = (t[:, :, :].rearrange("p (a two b) d -> p a two (b d)", two=2, b=1 << level)
                                for t in (z[level % 2], z[(level + 1) % 2]))
                    steps.link(dve.tensor_tensor(dst[:, :, 0], src[:, :, 0], src[:, :, 1], ALU.add))
                    steps.link(dve.tensor_tensor(dst[:, :, 1], src[:, :, 0], src[:, :, 1], ALU.subtract))
                for m in range(M):
                    steps.link(dve.tensor_scalar(z[0][:, m, :], z[1][:, m, :], su[:, m:m + 1], 1.0 / 32, ALU.mult, ALU.mult))


def hadamard_inputs(k, name, xh, loads_after):
    nc, a = k.nc, k.a
    with ExitStack() as ctx:
        h256 = ctx.enter_context(nc.sbuf_tensor(f"{name}_h256", [P, DC, D], F32))
        su = ctx.enter_context(nc.sbuf_tensor(f"{name}_su_in", [P, DC], F32))
        signed = ctx.enter_context(nc.sbuf_tensor(f"{name}_signed", [P, DC, T], F32))
        s = k.sems("inputs", ("loaded", "turned", "step"))

        def loads(sp):
            sp.dma_start(h256[:, :, :], a["h256"].rearrange("(c p) n -> p c n", p=P)).then_inc(s["loaded"], 16)
            sp.dma_start(su[:, :], a[f"{name}_su_ug"]).then_inc(s["loaded"], 16)
            loads_after(sp)
        layer_norm(k, loads)

        with nc.Block() as block:
            @block.vector
            def _(dve):
                dve.wait_ge(s["loaded"], 32)
                for c in range(DC):
                    dve.tensor_scalar(signed[:, c, :], k.xnT[:, c, :], su[:, c:c + 1], None, ALU.mult).then_inc(s["step"], 1)

            @block.tensor
            def _(pe):
                pe.wait_ge(s["loaded"], 32)
                pe.wait_ge(s["step"], DC)
                for c in range(DC):
                    for n in range(2):
                        for d in range(DC):
                            ins = pe.matmul(k.banks[:, 2 * c + n, 0:NT], h256[:, d, c * P:(c + 1) * P],
                                            signed[:, d, n * NT:(n + 1) * NT], start=d == 0, stop=d == DC - 1)
                        ins.then_inc(s["turned"], 1)

            @block.scalar
            def _(act):
                for c in range(DC):
                    for n in range(2):
                        act.wait_ge(s["turned"], 2 * c + n + 1)
                        act.activation(xh[:, c, n * NT:(n + 1) * NT], k.banks[:, 2 * c + n, 0:NT], ACT.Copy, scale=1.0 / 16)


FE = 8
HKV = H // 2
QK = H + HKV
MAGIC = 1.5 * 2.0 ** 23
INV_2PI = 0.15915494309189535


def feature_attention(k, name):
    nc, a = k.nc, k.a
    scratch = nc.dram_tensor(f"{name}_scratch", (B, S * D), F32).ap()
    with ExitStack() as ctx:
        def sb(nm, shape, dt=F32):
            return ctx.enter_context(nc.sbuf_tensor(f"{name}_{nm}", shape, dt))

        W = (QK + HKV) * HD
        half = HD // 2
        w = sb("w", [P, DC, W])
        bias = sb("bias", [S, W])
        wo, bo = sb("wo", [P, DC, D]), sb("bo", [S, D])
        rb = sb("rb", [P, HKV * FE])
        cos, sin = sb("cos", [S, HD]), sb("sin", [S, HD])
        qk = sb("qk", [S, B, QK, HD])
        v = sb("v", [S, B, HKV * HD])
        c_part, s_part = sb("c_part", [S, QK, HD]), sb("s_part", [S, QK, HD])
        norm = sb("norm", [S, B, QK])
        qkT = sb("qkT", [P, 2, 3, S])
        ph = sb("ph", [S, B, QK, 2 * FE])
        rnd = sb("rnd", [S, B, QK, 2 * FE])
        m1, m2 = sb("m1", [S, 2, H * HKV, 2 * FE]), sb("m2", [S, H * HD, HKV])
        dots = sb("dots", [S, 2, H, HKV])
        o = sb("o", [S, 2, H, HD])
        otok = sb("otok", [S, B, D])
        oT = sb("oT", [P, 2, DC, S])
        s = k.sems("feature", ("loaded", "proj", "biased", "step", "normed", "root", "unit", "turned", "copied", "angled",
                               "angles", "taken", "wrapped", "feat", "prod", "dot", "dotted", "summed", "stored0", "stored1", "back",
                               "oturned", "ocopied", "out", "added"))
        def loads(sp):
            for dst, nm in ((w, "w"), (wo, "wo")):
                sp.dma_start(dst[:, :, :], a[f"{name}_{nm}"]).then_inc(s["loaded"], 16)
            for dst, nm in ((rb, "rb"), (cos, "cos"), (sin, "sin")):
                sp.dma_start(dst[:, :], a[f"{name}_{nm}"]).then_inc(s["loaded"], 16)
            for dst, nm in ((bias, "bias"), (bo, "bo")):
                sp.dma_start(dst[:, :], a[f"{name}_{nm}"].partition_broadcast(S)).then_inc(s["loaded"], 16)
        layer_norm(k, loads)

        with nc.Block() as block:
            @block.sync
            def _(sp):
                for b in range(B):
                    sp.wait_ge(s["summed"], b + 1)
                    sp.dma_start(scratch[b].rearrange("(h s d) -> s h d", h=H, s=S), o[:, b % 2])\
                      .then_inc(s[f"stored{b % 2}"], 16)
                for j in range(2):
                    sp.wait_ge(s[f"stored{j}"], 16 * B // 2)
                sp.dma_start(otok[:, :, :], scratch.rearrange("b (r c) -> r b c", c=D)).then_inc(s["back"], 16)

            @block.tensor
            def _(pe):
                pe.wait_ge(s["loaded"], 16 * 7)
                for b in range(B):
                    if b >= 4:
                        pe.wait_ge(s["biased"], b - 3)
                    for c in range(DC):
                        ins = pe.matmul(k.banks[0:S, b % 4, 0:W], k.xnT[:, c, b * S:(b + 1) * S], w[:, c, :],
                                        start=c == 0, stop=c == DC - 1)
                    ins.then_inc(s["proj"], 1)
                for b in range(B):
                    pe.wait_ge(s["unit"], b + 1)
                    if b >= 2:
                        pe.wait_ge(s["copied"], b - 1)
                    for g in range(3):
                        ins = pe.transpose(k.banks[:, 4 + b % 2, g * S:(g + 1) * S],
                                           qk[:, b, 8 * g:8 * g + 8, :].rearrange("s h d -> s (h d)"), k.ident[0:S, 0:S])
                    ins.then_inc(s["turned"], 1)
                    pe.wait_ge(s["copied"], b + 1)
                    if b >= 2:
                        pe.wait_ge(s["taken"], b - 1)
                    for g in range(3):
                        ins = pe.matmul(k.banks[0:S, 6 + b % 2, g * 64:(g + 1) * 64], qkT[:, b % 2, g, :], rb[:, :],
                                        start=True, stop=True)
                    ins.then_inc(s["angled"], 1)
                pe.wait_ge(s["back"], 16)
                for b in range(B):
                    if b >= 2:
                        pe.wait_ge(s["ocopied"], b - 1)
                    for c in range(DC):
                        ins = pe.transpose(k.banks[:, b % 2, c * S:(c + 1) * S], otok[:, b, c * P:(c + 1) * P],
                                           k.ident[0:S, 0:S])
                    ins.then_inc(s["oturned"], 1)
                    pe.wait_ge(s["ocopied"], b + 1)
                    if b >= 2:
                        pe.wait_ge(s["added"], b - 1)
                    for c in range(DC):
                        ins = pe.matmul(k.banks[0:S, 2 + b % 2, 0:D], oT[:, b % 2, c, :], wo[:, c, :],
                                        start=c == 0, stop=c == DC - 1)
                    ins.then_inc(s["out"], 1)

            @block.scalar
            def _(act):
                act.wait_ge(s["normed"], 1)
                act.activation(norm[:, :, :], norm[:, :, :], ACT.Sqrt).then_inc(s["root"], 1)
                for b in range(B):
                    act.wait_ge(s["turned"], b + 1)
                    if b >= 2:
                        act.wait_ge(s["angled"], b - 1)
                    act.copy(qkT[:, b % 2], k.banks[:, 4 + b % 2, 0:3 * S].rearrange("p (g s) -> p g s", g=3))\
                       .then_inc(s["copied"], 1)
                act.wait_ge(s["wrapped"], 1)
                act.activation(ph[:, :, :, :], ph[:, :, :, :], ACT.Sin, scale=6.283185).then_inc(s["feat"], 1)
                for b in range(B):
                    act.wait_ge(s["oturned"], b + 1)
                    if b >= 2:
                        act.wait_ge(s["out"], b - 1)
                    act.copy(oT[:, b % 2], k.banks[:, b % 2, 0:DC * S].rearrange("p (g s) -> p g s", g=DC))\
                       .then_inc(s["ocopied"], 1)

            @block.gpsimd
            def _(pool):
                pool.wait_ge(s["feat"], 1)
                for b in range(B):
                    if b >= 2:
                        pool.wait_ge(s["dot"], b - 1)
                    pool.tensor_tensor(m1[:, b % 2].rearrange("s (h g) f -> s h g f", h=H),
                                       ph[:, b, 0:H, :].unsqueeze(2).broadcast_to((S, H, HKV, 2 * FE)),
                                       ph[:, b, H:QK, :].unsqueeze(1).broadcast_to((S, H, HKV, 2 * FE)), ALU.mult)\
                        .then_inc(s["prod"], 1)

            @block.vector
            def _(dve):
                steps = Steps(dve, s["step"])
                dve.wait_ge(s["loaded"], 16 * 7)
                steps.link(dve.tensor_tensor(k.x[:, :, :], k.x[:, :, :], bo[:, :].unsqueeze(1).broadcast_to((S, B, D)), ALU.add))
                for b in range(B):
                    dve.wait_ge(s["proj"], b + 1)
                    dve.tensor_tensor(qk[:, b, :, :].rearrange("s h d -> s (h d)"), k.banks[0:S, b % 4, 0:QK * HD],
                                      bias[:, 0:QK * HD], ALU.add)
                    dve.tensor_tensor(v[:, b, :], k.banks[0:S, b % 4, QK * HD:W], bias[:, QK * HD:W], ALU.add)\
                       .then_inc(s["biased"], 1)
                    dve.wait_ge(s["biased"], b + 1)
                    def wide(t, at):
                        return t[:, at].unsqueeze(1).broadcast_to((S, QK, at.stop - at.start))
                    dve.tensor_tensor(c_part[:, :, :], qk[:, b], wide(cos, slice(0, HD)), ALU.mult)
                    dve.tensor_tensor(s_part[:, :, 0:half], qk[:, b, :, half:], wide(sin, slice(0, half)), ALU.mult)
                    steps.link(dve.tensor_tensor(s_part[:, :, half:], qk[:, b, :, 0:half], wide(sin, slice(half, HD)), ALU.mult))
                    steps.link(dve.tensor_tensor(qk[:, b], c_part[:, :, :], s_part[:, :, :], ALU.add))
                    steps.link(dve.tensor_tensor(c_part[:, :, :], qk[:, b], qk[:, b], ALU.mult))
                    steps.link(dve.tensor_reduce(norm[:, b, :], c_part[:, :, :], X, ALU.add))
                dve.sem_inc(s["normed"], 1)
                steps.link(dve.tensor_scalar(v[:, :, :], v[:, :, :], 1.0 / 8, None, ALU.mult))
                dve.wait_ge(s["root"], 1)
                steps.link(dve.tensor_scalar(norm[:, :, :], norm[:, :, :], 1e-6, None, ALU.max))
                steps.link(dve.reciprocal(norm[:, :, :], norm[:, :, :]))
                for b in range(B):
                    dve.tensor_tensor(qk[:, b], qk[:, b], norm[:, b, :].unsqueeze(2).broadcast_to((S, QK, HD)), ALU.mult)\
                       .then_inc(s["unit"], 1)
                for b in range(B):
                    dve.wait_ge(s["angled"], b + 1)
                    got = k.banks[0:S, 6 + b % 2, 0:QK * FE].rearrange("s (h e) -> s h e", e=FE)
                    dve.tensor_scalar(ph[:, b, :, 0:FE], got, INV_2PI, None, ALU.mult)
                    dve.tensor_scalar(ph[:, b, :, FE:], got, INV_2PI, 0.25, ALU.mult, ALU.add).then_inc(s["taken"], 1)
                dve.wait_ge(s["taken"], B)
                steps.link(dve.tensor_scalar(rnd[:, :, :, :], ph[:, :, :, :], MAGIC, None, ALU.add))
                steps.link(dve.tensor_scalar(rnd[:, :, :, :], rnd[:, :, :, :], MAGIC, None, ALU.subtract))
                dve.tensor_tensor(ph[:, :, :, :], ph[:, :, :, :], rnd[:, :, :, :], ALU.subtract).then_inc(s["wrapped"], 1)
                for b in range(B):
                    dve.wait_ge(s["prod"], b + 1)
                    dve.tensor_reduce(dots[:, b % 2].rearrange("s h g -> s (h g)"), m1[:, b % 2], X, ALU.add)\
                       .then_inc(s["dot"], 1)
                    dve.wait_ge(s["dot"], b + 1)
                    steps.link(dve.tensor_tensor(
                        m2[:, :, :].rearrange("s (h d) g -> s h d g", h=H),
                        dots[:, b % 2].unsqueeze(2).broadcast_to((S, H, HD, HKV)),
                        v[:, b, :].rearrange("s (g d) -> s d g", g=HKV).unsqueeze(1).broadcast_to((S, H, HD, HKV)),
                        ALU.mult))
                    if b >= 2:
                        dve.wait_ge(s[f"stored{b % 2}"], 16 * (b // 2))
                    dve.tensor_reduce(o[:, b % 2].rearrange("s h d -> s (h d)"), m2[:, :, :], X, ALU.add)\
                       .then_inc(s["summed"], 1)
                    dve.wait_ge(s["summed"], b + 1)
                for b in range(B):
                    dve.wait_ge(s["out"], b + 1)
                    dve.tensor_tensor(k.x[:, b, :], k.x[:, b, :], k.banks[0:S, 2 + b % 2, 0:D], ALU.add)\
                       .then_inc(s["added"], 1)


def first_context(k, first):
    nc = k.nc
    with ExitStack() as ctx:
        rows = ctx.enter_context(nc.sbuf_tensor("first_rows", [S, B, DL], F32))
        s = k.sems("first", ("loaded", "turned"))
        with nc.Block() as block:
            @block.sync
            def _(sp):
                sp.dma_start(rows[:, :, :], k.a["ctx"][:, 0:S, :].rearrange("b s d -> s b d")).then_inc(s["loaded"], 16)

            @block.tensor
            def _(pe):
                pe.wait_ge(s["loaded"], 16)
                for b in range(B):
                    pe.transpose(k.banks[0:DL, b // 4, (b % 4) * S:(b % 4 + 1) * S], rows[:, b, :], k.ident[0:S, 0:S])\
                      .then_inc(s["turned"], 1)

            @block.scalar
            def _(act):
                act.wait_ge(s["turned"], B)
                act.copy(first[:, 0, :].rearrange("d (g t) -> d g t", g=2), k.banks[0:DL, 0:2, 0:NT])


def program(nc, args, out, first, stages):
    k = Core()
    k.nc, k.a, k.kinds, k.used = nc, args, {}, []
    with ExitStack() as ctx:
        def sb(nm, shape, dt=F32):
            return ctx.enter_context(nc.sbuf_tensor(nm, shape, dt))

        k.sem = lambda nm: ctx.enter_context(nc.semaphore(nm))
        k.x = sb("x", [S, B, D])
        k.xnT = sb("xnT", [P, DC, T])
        k.ident = sb("ident", [P, P])
        k.ident16 = sb("ident16", [P, P], BF16)
        k.mask16 = sb("mask16", [S, 4 * S], BF16)
        k.ones64 = sb("ones64", [P, 64])
        k.eps = sb("eps", [P, 1])
        k.ln_stats = sb("ln_stats", [S, B, 6])
        k.ln_mv = sb("ln_mv", [S, B, 2])
        k.ln_root = sb("ln_root", [S, B])
        k.ln_warm = sb("ln_warm", [S, stages - first])
        k.ln_rstd = sb("ln_rstd", [S, B])
        k.ln_xn = sb("ln_xn", [S, LN_SLOTS, D])
        k.kv_hl = sb("kv_hl", [2 * DL, B * L + P - L_LAST], F16)
        k.kv_h1 = sb("kv_h1", [DL + 2, B * L + P - L_LAST], F16)
        k.kv_tok = sb("kv_tok", [P, B, LT, DL])
        k.gates = sb("gates", [P, T], F16)
        k.banks = ctx.enter_context(nc.psum_tensor("banks", [P, 8, 512], F32))
        k.head_rows = sb("head_rows", [P, HH])
        k.ln_summed, k.ln_var, k.ln_std = k.sem("ln_summed"), k.sem("ln_var"), k.sem("ln_std")
        k.ln_recip, k.ln_normed = k.sem("ln_recip"), k.sem("ln_normed")
        k.ln_transposed, k.ln_copied = k.sem("ln_transposed"), k.sem("ln_copied")
        k.ln_calls = 0
        stored = k.sem("stored")
        context(k)

        def cross(name, rope):
            with ExitStack() as inner:
                k.q_hh = inner.enter_context(nc.sbuf_tensor(f"{name}_q_hh", [2 * DL, B, QT * P], F16))
                k.q_l = inner.enter_context(nc.sbuf_tensor(f"{name}_q_l", [DL + 2, B, QT * P], F16))
                k.wvo = inner.enter_context(nc.sbuf_tensor(f"{name}_wvo", [P, PAIRS, D], F32))
                (rope_queries if rope else plain_queries)(k, name)
                cross_attention(k, name)

        def mixture(name, experts, hidden, kind, top):
            with ExitStack() as inner:
                f = FeedForward(k, inner, name, experts * hidden // P, args[f"{name}_dn"], experts)
                router(k, name, experts, kind, top, f.first_loads)
                feed_forward(f, k.xnT)

        def hadamard(name):
            down = nc.dram_tensor(f"{name}_down", (FFN_TILES, P, D), F32).ap()
            hadamard_weights(k, name, down)
            with ExitStack() as inner:
                xh = inner.enter_context(nc.sbuf_tensor(f"{name}_xh", [P, DC, T], F32))
                f = FeedForward(k, inner, name, FFN_TILES, down, scales=True)
                hadamard_inputs(k, name, xh, f.first_loads)
                feed_forward(f, xh)

        def last_cross(name):
            with nc.sbuf_tensor("first", [DL, 1, T], F32) as first:
                first_context(k, first)
                self_attention(k, name, first, 1, DL, 0.25, False)

        sublayers = [
            lambda: self_attention(k, "L0_attn", k.xnT, DC, P, 0.25, False),
            lambda: cross("L0_xattn", False),
            lambda: mixture("L0_ffn", 8, 512, "choice", 1),
            lambda: self_attention(k, "L1_attn", k.xnT, DC, P, 0.25, True),
            lambda: cross("L1_xattn", True),
            lambda: mixture("L1_ffn", 16, 176, "softmax_first", 6),
            lambda: self_attention(k, "L2_attn", k.xnT, DC, P, 0.25, True),
            lambda: cross("L2_xattn", True),
            lambda: hadamard("L2_ffn"),
            lambda: feature_attention(k, "L3_attn"),
            lambda: last_cross("L3_xattn"),
            lambda: mixture("L3_ffn", 8, 176, "softmax_last", 2),
        ]
        for sublayer in sublayers[first:stages]:
            sublayer()
        with nc.Block() as block:
            @block.sync
            def _(sp):
                sp.dma_start(out, k.x[:, :, :]).then_inc(stored, 16)
                sp.wait_ge(stored, 16)


def attn_layout(put, name, wq, wk, wv, wo, bq=None, bk=None, bv=None, bo=None):
    import numpy as np

    def tiles(w):
        rows = min(P, w.shape[0])
        return np.ascontiguousarray(w.reshape(-1, rows, w.shape[1]).transpose(1, 0, 2))
    for nm, w in (("wq", wq), ("wk", wk), ("wv", wv), ("wo", wo)):
        put(f"{name}_{nm}", tiles(w))
    if bq is not None:
        put(f"{name}_bq", np.ascontiguousarray(bq.reshape(DC, P).T))
        put(f"{name}_bk", np.ascontiguousarray(bk.reshape(DC, P).T))
        put(f"{name}_bv", bv)
        put(f"{name}_bo", bo)


def rope_tables(length, dim):
    import numpy as np
    inv = np.float32(1.0) / np.power(np.float32(10000.0), np.arange(0, dim, 2, dtype=np.float32) / np.float32(dim))
    f = np.arange(length, dtype=np.float32)[:, None] * inv[None, :]
    return np.repeat(np.cos(f), 2, axis=1), np.repeat(np.sin(f), 2, axis=1)


FIRST, STAGES = 0, 12


def kernel(**inputs):
    import ml_dtypes
    import numpy as np
    import concourse.bacc as bacc
    from concourse.bass_utils import run_bass_kernel_spmd

    i = {name: np.asarray(value) for name, value in inputs.items()}
    nc = bacc.Bacc("TRN2", target_bir_lowering=False, num_devices=1)
    arrays, args = {}, {}

    def put(name, value):
        value = np.ascontiguousarray(value)
        arrays[f"in_{name}"] = value
        args[name] = nc.dram_tensor(f"in_{name}", value.shape, mybir.dt.from_np(value.dtype), kind="ExternalInput").ap()

    bf16 = ml_dtypes.bfloat16
    put("ident", np.eye(P, dtype=np.float32))
    put("ident16", np.eye(P, dtype=bf16))
    put("mask16", np.tile(np.triu(np.full((S, S), -1e30, np.float32), 1), (1, 4)).astype(bf16))
    put("head_rows", np.repeat(np.eye(HH, dtype=np.float32), HD, axis=0))

    put("x", i["x"].transpose(1, 0, 2))
    qkv = i["L0_attn_Wqkv"]
    attn_layout(put, "L0_attn", qkv[:, 0:D], qkv[:, D:2 * D], qkv[:, 2 * D:3 * D], i["L0_attn_Wo"])

    put("ctx", i["ctx_512"])
    cos, sin = rope_tables(LT * P, DL)
    half = np.arange(DL) < DL // 2
    put("ctx_cos", cos.reshape(LT, P, DL).transpose(1, 0, 2))
    put("ctx_sin", np.where(half, -sin, sin).reshape(LT, P, DL).transpose(1, 0, 2))
    cos, sin = rope_tables(S, CQ)
    put("q_cos", cos.T.reshape(2, CH, S).transpose(1, 0, 2))
    put("q_sin", np.stack([sin.T[CH:], -sin.T[:CH]], 1))
    for layer in ("L0", "L1", "L2"):
        n = f"{layer}_xattn"
        wo = i[n + "_Wo"].T.reshape(H, HK, D)
        put(n + "_raw", np.concatenate([i[n + "_Wq"].reshape(H, HK, D), i[n + "_w_kc_q"], i[n + "_w_kc_kv"], wo], 2))
        wkr = i[n + "_W_kr"].transpose(0, 2, 1)
        put(n + "_rkr", np.concatenate([i[n + "_W_qr"].transpose(0, 2, 1), wkr, wkr], 2))

    def shared(w, columns):
        return np.repeat(w.reshape(-1, columns, HD), H // columns, axis=-2).reshape(w.shape[:-1] + (D,))
    n = "L1_attn"
    attn_layout(put, n, i[n + "_Wq"], shared(i[n + "_Wk"], 2), shared(i[n + "_Wv"], 2), i[n + "_Wo"],
                i[n + "_bq"], shared(i[n + "_bk"], 2), shared(i[n + "_bv"], 2), i[n + "_bo"])
    n = "L2_attn"
    attn_layout(put, n, i[n + "_wq"].T, i[n + "_wk"].T, i[n + "_wv"].T, i[n + "_wo"].T,
                i[n + "_bq"], i[n + "_bk"], i[n + "_bv"], i[n + "_bo"])
    n = "L3_xattn"
    kv = i[n + "_Wkv_expand"].T
    attn_layout(put, n, i[n + "_Wq"].T, kv[:, 0:D], kv[:, D:], i[n + "_Wout"].T)

    def tiles_of(w):
        return w.reshape(DC, P, -1, P).transpose(2, 1, 0, 3).reshape(-1, P, DC * P)

    def ffn_layout(n, gate, up, down):
        put(n + "_gu", np.concatenate([tiles_of(gate), tiles_of(up)], 2))
        if down is not None:
            put(n + "_dn", down.reshape(-1, P, D))

    def experts_layout(n, experts, hidden, router_w):
        put(n + "_wr", router_w.reshape(DC, P, experts).transpose(1, 0, 2))
        one = np.repeat(np.eye(experts, dtype=np.float16) * np.float16(OUT_SCALE), hidden, axis=1)
        put(n + "_expert_of", np.concatenate([one, one, np.zeros((P - 2 * experts, experts * hidden), np.float16)]))

    for experts in (8, 16):
        put(f"lower{experts}", np.tile(np.tril(np.ones((experts, experts), np.float32), -1), (S, 1, 1)))
    n = "L0_ffn"
    ffn_layout(n, i[n + "_gate_w"].transpose(1, 0, 2).reshape(D, -1), i[n + "_up_w"].transpose(1, 0, 2).reshape(D, -1),
               i[n + "_down_w"].reshape(-1, D))
    experts_layout(n, 8, 512, i[n + "_router_w"])
    n = "L1_ffn"
    ffn_layout(n, i[n + "_w_gate"].reshape(-1, D).T, i[n + "_w_up"].reshape(-1, D).T,
               i[n + "_w_down"].transpose(0, 2, 1).reshape(-1, D))
    experts_layout(n, 16, 176, i[n + "_gate_w"].T)
    n = "L3_ffn"
    ffn_layout(n, i[n + "_W1"].reshape(-1, D).T, i[n + "_W2"].reshape(-1, D).T,
               i[n + "_W3"].transpose(0, 2, 1).reshape(-1, D))
    experts_layout(n, 8, 176, i[n + "_Wg"].T)
    n = "L2_ffn"
    ffn_layout(n, i[n + "_W_gate"].T, i[n + "_W_up"].T, None)
    hidden = FFN_TILES * P
    h = np.ones((1, 1), np.float32)
    while len(h) < D:
        h = np.block([[h, h], [h, -h]])
    put("h256", h)
    put(n + "_wd", i[n + "_W_down"].T.reshape(FFN_TILES, P, D).transpose(1, 0, 2))
    put(n + "_su_dp", i[n + "_SU_dp"].reshape(FFN_TILES, P).T)
    put(n + "_su_ug", i[n + "_SU_ug"].reshape(DC, P).T)
    put(n + "_sc_u", i[n + "_Wscale_ug"][:hidden].reshape(FFN_TILES, P).T)
    put(n + "_sc_g", i[n + "_Wscale_ug"][hidden:].reshape(FFN_TILES, P).T)
    put(n + "_sc_d", i[n + "_Wscale_dp"].reshape(DC, P).T)

    n = "L3_attn"
    w = np.concatenate([i[n + "_Wq"], i[n + "_Wk"], i[n + "_Wv"]], 0).T
    put(n + "_w", w.reshape(DC, P, -1).transpose(1, 0, 2))
    put(n + "_bias", np.concatenate([i[n + "_bq"], i[n + "_bk"], i[n + "_bv"]]))
    put(n + "_wo", i[n + "_Wo"].T.reshape(DC, P, D).transpose(1, 0, 2))
    put(n + "_bo", i[n + "_bo"])
    blocks = np.zeros((HKV, HD, HKV, FE), np.float32)
    for g in range(HKV):
        blocks[g, :, g, :] = i[n + "_rand_matrix"].T
    put(n + "_rb", blocks.reshape(P, HKV * FE))
    inv = np.float32(1.0) / np.power(np.float32(10000.0), np.arange(0, HD, 2, dtype=np.float32) / np.float32(HD))
    f = np.arange(S, dtype=np.float32)[:, None] * np.concatenate([inv, inv])[None, :]
    put(n + "_cos", np.cos(f))
    put(n + "_sin", np.where(np.arange(HD) < HD // 2, -np.sin(f), np.sin(f)))

    out = nc.dram_tensor("out", (S, B, D), F32, kind="ExternalOutput").ap()
    program(nc, args, out, FIRST, STAGES)
    r = run_bass_kernel_spmd(nc, [arrays], core_ids=[0])
    return np.ascontiguousarray(r.results[0]["out"].transpose(1, 0, 2))
```
